# Optimizing a Trainium2 kernel written in Bass

```python
import numpy as np
import jax
import jax.numpy as jnp

def _softmax(x, axis=-1):
    return jax.nn.softmax(x, axis=axis)

def _gelu(x):
    return jax.nn.gelu(x, approximate=True)

def _silu(x):
    return jax.nn.silu(x)

def _sigmoid(x):
    return jax.nn.sigmoid(x)

def _layernorm(x, axis=-1, eps=1e-05):
    m = jnp.mean(x, axis=axis, keepdims=True)
    v = jnp.var(x, axis=axis, keepdims=True)
    return (x - m) / jnp.sqrt(v + eps)

def _scatter_add(tgt, idx, src, axis=0):
    return tgt.at[idx].add(src)

def _segment_sum(src, seg, n):
    return jax.ops.segment_sum(src, seg, n)
kernel_name = 'mk_audio_tower_d1_tok_audfeat512_r4_8caf32'

def setup_inputs(seed: int=0):
    np.random.seed(seed)
    _w = jnp.asarray

    def _rec_inputs():
        import jax
        import jax.numpy as jnp
        _rk = jax.random.key(seed)
        x = 7.22013e-05 + 1.00017 * jax.random.normal(jax.random.fold_in(_rk, 1), (16, 375, 64), jnp.float32)
        return x
    x = _rec_inputs()

    def _L0_tok_setup():
        import jax, jax.numpy as jnp
        import numpy as np
        EPS = 1e-07
        C_CURV = 1.0
        LAM_HALF = 1.0 / (1.0 + EPS)
        key = jax.random.key(seed)
        k1, k2 = jax.random.split(key)
        B, L, Cin, K, F = (32, 256, 64, 9, 128)
        x = jax.random.normal(k1, (B, L, Cin), dtype=jnp.float32)
        lim = float(np.sqrt(6.0 / (K * Cin + F)))
        kernel = jax.random.uniform(k2, (K, Cin, F), dtype=jnp.float32, minval=-lim, maxval=lim)
        bias = jnp.zeros((F,), dtype=jnp.float32)
        return {'x': x, 'kernel': kernel, 'bias': bias}
    _L0_tok_all = _L0_tok_setup()
    _L0_tok_in = {k: v for k, v in _L0_tok_all.items() if k in ('kernel', 'bias')}
    del _L0_tok_all

    def _L0_attn_setup():
        import jax, jax.numpy as jnp
        import numpy as np
        B, T, D = (8, 512, 128)
        DK = 128
        FENETRES = (24, 168, 180)
        EPS = 1e-05
        key = jax.random.key(seed)
        ks = jax.random.split(key, 8)
        s = 0.02
        return {'x': jax.random.normal(ks[0], (B, T, D), dtype=jnp.float32), 'Wq': jax.random.normal(ks[1], (D, DK), dtype=jnp.float32) * s, 'bq': jnp.zeros((DK,), dtype=jnp.float32), 'Wk': jax.random.normal(ks[2], (D, DK), dtype=jnp.float32) * s, 'bk': jnp.zeros((DK,), dtype=jnp.float32), 'Wo': jax.random.normal(ks[3], (D, D), dtype=jnp.float32) * s, 'bo': jnp.zeros((D,), dtype=jnp.float32), 'gamma': jnp.ones((D,), dtype=jnp.float32), 'beta': jnp.zeros((D,), dtype=jnp.float32)}
    _L0_attn_all = _L0_attn_setup()
    _L0_attn_in = {k: v for k, v in _L0_attn_all.items() if k in ('Wq', 'bq', 'Wk', 'bk', 'Wo', 'bo', 'gamma', 'beta')}
    del _L0_attn_all

    def _L0_ffn_setup():
        import jax, jax.numpy as jnp
        import numpy as np
        B, S, D, O = (1, 512, 128, 128)
        H, QD, K, PK = (8, 64, 16, 64)
        N = PK * PK
        HALF = QD // 2

        def _l2norm(x):
            n = jnp.sqrt(jnp.sum(x * x, axis=-1, keepdims=True))
            return x / jnp.maximum(n, 1e-12)
        key = jax.random.key(seed)
        ks = jax.random.split(key, 9)
        return {'hidden_states': jax.random.normal(ks[0], (B, S, D), jnp.float32), 'Wq': jax.random.normal(ks[1], (H * QD, D), jnp.float32) * 0.02, 'bq': jnp.zeros((H * QD,), jnp.float32), 'ln_g': jnp.ones((QD,), jnp.float32), 'ln_b': jnp.zeros((QD,), jnp.float32), 'keys0': jax.random.normal(ks[2], (PK, HALF), jnp.float32) * 0.02, 'keys1': jax.random.normal(ks[3], (PK, HALF), jnp.float32) * 0.02, 'expert_down': jax.random.normal(ks[4], (N, D), jnp.float32) * 0.02, 'expert_up': jax.random.normal(ks[5], (N, O), jnp.float32) * 0.02}
    _L0_ffn_all = _L0_ffn_setup()
    _L0_ffn_in = {k: v for k, v in _L0_ffn_all.items() if k in ('Wq', 'bq', 'ln_g', 'ln_b', 'keys0', 'keys1', 'expert_down', 'expert_up')}
    del _L0_ffn_all
    return {'x': x, 'L0_tok_kernel': _L0_tok_in['kernel'], 'L0_tok_bias': _L0_tok_in['bias'], 'L0_attn_Wq': _L0_attn_in['Wq'], 'L0_attn_bq': _L0_attn_in['bq'], 'L0_attn_Wk': _L0_attn_in['Wk'], 'L0_attn_bk': _L0_attn_in['bk'], 'L0_attn_Wo': _L0_attn_in['Wo'], 'L0_attn_bo': _L0_attn_in['bo'], 'L0_attn_gamma': _L0_attn_in['gamma'], 'L0_attn_beta': _L0_attn_in['beta'], 'L0_ffn_Wq': _L0_ffn_in['Wq'], 'L0_ffn_bq': _L0_ffn_in['bq'], 'L0_ffn_ln_g': _L0_ffn_in['ln_g'], 'L0_ffn_ln_b': _L0_ffn_in['ln_b'], 'L0_ffn_keys0': _L0_ffn_in['keys0'], 'L0_ffn_keys1': _L0_ffn_in['keys1'], 'L0_ffn_expert_down': _L0_ffn_in['expert_down'], 'L0_ffn_expert_up': _L0_ffn_in['expert_up']}

def reference(x, L0_tok_kernel, L0_tok_bias, L0_attn_Wq, L0_attn_bq, L0_attn_Wk, L0_attn_bk, L0_attn_Wo, L0_attn_bo, L0_attn_gamma, L0_attn_beta, L0_ffn_Wq, L0_ffn_bq, L0_ffn_ln_g, L0_ffn_ln_b, L0_ffn_keys0, L0_ffn_keys1, L0_ffn_expert_down, L0_ffn_expert_up):
    import jax
    import jax.numpy as jnp

    def _L0_tok_ref(x, kernel, bias):
        import jax, jax.numpy as jnp
        import numpy as np
        EPS = 1e-07
        C_CURV = 1.0
        LAM_HALF = 1.0 / (1.0 + EPS)
        B, L, Cin = x.shape
        K, _, F = kernel.shape
        Lout = L - K + 1
        sq = jnp.sum(x * x, axis=-1)
        cs = jnp.concatenate([jnp.zeros((B, 1), x.dtype), jnp.cumsum(sq, axis=1)], axis=1)
        wsq = cs[:, K:] - cs[:, :Lout]
        wnorm = jnp.sqrt(jnp.maximum(wsq, 0.0))
        scale = jnp.where(wnorm < 1.0, 1.0, 1.0 / (wnorm + EPS))[..., None]
        conv = jax.lax.conv_general_dilated(x, kernel, window_strides=(1,), padding='VALID', dimension_numbers=('NWC', 'WIO', 'NWC'))
        v = conv * scale
        v_norm = jnp.maximum(jnp.abs(v), EPS)
        y = jnp.tanh(v_norm * LAM_HALF) * (v / v_norm)
        return jax.nn.relu(y + bias)

    def _L0_attn_ref(x, Wq, bq, Wk, bk, Wo, bo, gamma, beta):
        import jax, jax.numpy as jnp
        import numpy as np
        B, T, D = (8, 512, 128)
        DK = 128
        FENETRES = (24, 168, 180)
        EPS = 1e-05
        q = x @ Wq + bq
        k = x @ Wk + bk
        dk = q.shape[-1]
        scores = jnp.einsum('btd,bsd->bts', q, k) / jnp.sqrt(jnp.float32(dk))
        t = jnp.arange(x.shape[1])
        dist = jnp.abs(t[:, None] - t[None, :])
        acc = jnp.zeros_like(x)
        for w in FENETRES:
            band = dist <= w // 2
            s = jnp.where(band[None, :, :], scores, jnp.float32(-1000000000.0))
            attn = jax.nn.softmax(s, axis=-1)
            acc = acc + jnp.einsum('bts,bsd->btd', attn, x)
        acc = acc / jnp.float32(len(FENETRES))
        out = acc @ Wo + bo
        res = x + out
        mu = jnp.mean(res, axis=-1, keepdims=True)
        var = jnp.mean(jnp.square(res - mu), axis=-1, keepdims=True)
        return (res - mu) * jax.lax.rsqrt(var + EPS) * gamma + beta

    def _L0_ffn_ref(hidden_states, Wq, bq, ln_g, ln_b, keys0, keys1, expert_down, expert_up):
        import jax, jax.numpy as jnp
        import numpy as np
        B, S, D, O = (1, 512, 128, 128)
        H, QD, K, PK = (8, 64, 16, 64)
        N = PK * PK
        HALF = QD // 2

        def _l2norm(x):
            n = jnp.sqrt(jnp.sum(x * x, axis=-1, keepdims=True))
            return x / jnp.maximum(n, 1e-12)
        b, s, d = hidden_states.shape
        q = (hidden_states @ Wq.T + bq).reshape(b, s, H, QD)
        mu = jnp.mean(q, axis=-1, keepdims=True)
        var = jnp.mean((q - mu) ** 2, axis=-1, keepdims=True)
        q = (q - mu) / jnp.sqrt(var + 1e-05) * ln_g + ln_b
        q0, q1 = (q[..., :HALF], q[..., HALF:])
        s0 = jnp.einsum('bshq,eq->bshe', _l2norm(q0), _l2norm(keys0))
        s1 = jnp.einsum('bshq,eq->bshe', _l2norm(q1), _l2norm(keys1))
        sc0, ix0 = jax.lax.top_k(s0, K)
        sc1, ix1 = jax.lax.top_k(s1, K)
        cs = (sc0[..., :, None] + sc1[..., None, :]).reshape(b, s, H, K * K)
        ci = (ix0[..., :, None] + ix1[..., None, :]).reshape(b, s, H, K * K)
        fs, pos = jax.lax.top_k(cs, K)
        fi = jnp.take_along_axis(ci, pos, axis=-1)
        w = jax.nn.softmax(fs, axis=-1)
        down = expert_down[fi]
        up = expert_up[fi]
        inner = jnp.einsum('bsd,bshkd->bshk', hidden_states, down)
        act = jax.nn.gelu(inner, approximate=False)
        out = jnp.einsum('bshk,bshko->bso', act * w, up)
        return out
    h = _L0_tok_ref(x, L0_tok_kernel, L0_tok_bias)
    h = h + _L0_attn_ref(_layernorm(h, axis=-1), L0_attn_Wq, L0_attn_bq, L0_attn_Wk, L0_attn_bk, L0_attn_Wo, L0_attn_bo, L0_attn_gamma, L0_attn_beta)
    h = h + _L0_ffn_ref(_layernorm(h, axis=-1), L0_ffn_Wq, L0_ffn_bq, L0_ffn_ln_g, L0_ffn_ln_b, L0_ffn_keys0, L0_ffn_keys1, L0_ffn_expert_down, L0_ffn_expert_up)
    return h

_drawn_inputs = setup_inputs


def setup_inputs(seed=0):
    import zlib

    import numpy as np

    out = dict(_drawn_inputs(seed))
    spreads = {'L0_tok_bias': (0.0, 0.1),
     'L0_attn_bq': (0.0, 0.8),
     'L0_attn_bk': (0.0, 0.8),
     'L0_attn_bo': (0.0, 0.1),
     'L0_attn_gamma': (1.0, 0.2),
     'L0_attn_beta': (0.0, 0.1),
     'L0_ffn_bq': (0.0, 0.8),
     'L0_ffn_ln_g': (1.0, 0.6),
     'L0_ffn_ln_b': (0.0, 0.8)}
    factors = {'L0_attn_Wq': 8.0,
     'L0_attn_Wk': 8.0,
     'L0_ffn_Wq': 8.0,
     'L0_ffn_keys0': 8.0,
     'L0_ffn_keys1': 8.0,
     'L0_ffn_expert_down': 8.0,
     'L0_ffn_expert_up': 8.0}
    for name, (base, spread) in spreads.items():
        noise = np.random.default_rng([zlib.crc32(name.encode()), seed]).standard_normal(out[name].shape)
        drawn = base * np.exp(spread * noise) if base else spread * noise
        out[name] = jnp.asarray(drawn.astype(out[name].dtype))
    for name, factor in factors.items():
        out[name] = (out[name] * factor).astype(out[name].dtype)
    return out
```

```python
import numpy as np
import concourse.bass as bass
from concourse import mybir
from concourse.alu_op_type import AluOpType as ALU
from contextlib import ExitStack

B, L, C = 16, 375, 64
TAPS, D = 9, 128
T = L - TAPS + 1
NT = 124
OFF = [0, 122, T - NT]
FIRST = [0, 2, OFF[1] + NT - OFF[2]]
KEYS = [OFF[1], OFF[2] - OFF[1], NT]
RADII = [24 // 2, 168 // 2, 180 // 2]
XT = L // 3
H, QD, HALF, PK, TOP = 8, 64, 32, 64, 16
CELLS = [(a, c) for a in range(TOP) for c in range(TOP) if (a + 1) * (c + 1) <= TOP]
NC = len(CELLS)
PAIRS = H // 2
SLOTS = 32
EH, EL, TG = 32, 4, 4
NG = NT // TG
WSCALE = 4096.0
NEG = -1.0e30
SCORE_SCALE = 1.0 / float(np.sqrt(np.float32(D)))


def merge_matrix():
    def together(p, q):
        (a, c), (e, g) = p, q
        return (a + 1) * (c + 1) + (e + 1) * (g + 1) - (min(a, e) + 1) * (min(c, g) + 1) <= TOP
    slots = [[(0, c)] for c in range(TOP)] + [[] for _ in range(SLOTS - TOP)]
    rest = sorted((p for p in CELLS if p[0]), key=lambda p: -(p[0] + 1) * (p[1] + 1) + 0.01 * p[0])
    moves = {(a, 0): a for a in range(8, 16)}
    moves.update({(1, 4): 12, (1, 5): 13, (1, 6): 14, (1, 7): 15, (2, 3): 10, (2, 4): 11,
                  (3, 2): 8, (3, 3): 9, (5, 1): 6, (6, 1): 7})
    free = iter(range(TOP, SLOTS))
    for p in rest:
        slots[moves[p] if p in moves else next(free)].append(p)
    m = np.zeros((2 * NC, 2 * SLOTS), np.float16)
    for s, cells in enumerate(slots):
        assert not any(together(p, q) for i, p in enumerate(cells) for q in cells[:i])
        for p in cells:
            for h in range(2):
                m[h * NC + CELLS.index(p), h * SLOTS + s] = 1
    assert m.sum() == 2 * NC
    return m


def band(t, w):
    return max(0, OFF[t] - RADII[w]), min(T, OFF[t] + NT + RADII[w])


def chunks(t, w):
    lo, hi = band(t, w)
    return [c for c in range(3) if lo < OFF[c] + KEYS[c] and hi > OFF[c]]


def build(nc, x, tok_kernel, tok_bias, wq, bq, wk, bk, wo, bo, gamma, beta, fwq, fbq, lng, lnb,
          keys0, keys1, down, up, merge, ident, out):
    f32, f16, i16, u16 = mybir.dt.float32, mybir.dt.float16, mybir.dt.int16, mybir.dt.uint16
    ACT = mybir.ActivationFunctionType
    X = mybir.AxisListType.X
    ctx = ExitStack()
    with ctx:
        def sb(name, shape, dt=f32):
            return ctx.enter_context(nc.sbuf_tensor(name, shape, dt))

        def sem(name):
            return ctx.enter_context(nc.semaphore(name))

        def col(v):
            return v.rearrange("(p a) -> p a", a=1)

        def row(v):
            return v.rearrange("(a p) -> a p", a=1)

        id32 = sb("id32", [128, 128])
        id16 = sb("id16", [128, 128], f16)
        merge_sb = sb("merge_sb", [2 * NC, 2 * SLOTS], f16)
        ones = sb("ones", [128, 128])
        power = sb("power", [128, 48])
        conv_w = sb("conv_w", [128, 5, D])
        wq_sb, wk_sb, wo_sb = sb("wq_sb", [D, D]), sb("wk_sb", [D, D]), sb("wo_sb", [D, D])
        bq_sb, bk_sb = sb("bq_sb", [D, 1]), sb("bk_sb", [D, 1])
        rows = sb("rows", [1, 4 * D + 2 * QD + H * QD])
        vecs = sb("vecs", [128, 4 * D + 2 * QD])
        tokb, bob, gam, bet = (vecs[0:NT, i * D:(i + 1) * D] for i in range(4))
        lng_bc = vecs[0:NT, 4 * D:4 * D + QD]
        lnb_bc = vecs[0:NT, 4 * D + QD:4 * D + 2 * QD]
        fbq_row = rows[0:1, 4 * D + 2 * QD:4 * D + 2 * QD + H * QD]
        fwq_in = sb("fwq_in", [128, 4, D])
        fwqT = sb("fwqT", [D, H * QD])
        fmean = sb("fmean", [D, H])
        bmean = sb("bmean", [1, H])
        key_in = sb("key_in", [PK, 2, HALF])
        key_sq = sb("key_sq", [PK, 2, HALF])
        key_n = sb("key_n", [PK, 2])
        key_z = sb("key_z", [PK, 4, 128])
        key_bd = sb("key_bd", [128, 4 * PK])
        down_in = sb("down_in", [128, D])
        downT = sb("downT", [D, 128])
        down_x = sb("down_x", [D, TG, EL, 128])
        up_x = sb("up_x", [128, EL, D])
        masks = {}
        for t in range(3):
            for w in range(3):
                lo, hi = band(t, w)
                masks[t, w] = sb(f"mask{t}{w}", [NT, hi - lo])

        x_in = [sb(f"x_in{p}", [XT, 3, 2, C]) for p in range(2)]
        xT = sb("xT", [128, L])
        xT_sq = sb("xT_sq", [128, L])
        wsq = sb("wsq", [NT, 3])
        wnorm = sb("wnorm", [NT, 3])
        small = sb("small", [NT, 3])
        wden = sb("wden", [NT, 3])
        tscale = sb("tscale", [NT, 3])
        th = sb("th", [NT, 3, D])
        h0 = sb("h0", [NT, 3, D])
        bns = [sb(f"bns{i}", [NT, 3, 6]) for i in range(3)]
        bna = [sb(f"bna{i}", [NT, 3, 2]) for i in range(3)]
        lnv = [sb(f"lnv{i}", [NT, 3]) for i in range(3)]
        lnr = [sb(f"lnr{i}", [NT, 3]) for i in range(3)]
        lnm = [sb(f"lnm{i}", [NT, 3]) for i in range(3)]
        xl = sb("xl", [NT, 3, D])
        xb = sb("xb", [NT, 3, D])
        xlT = sb("xlT", [D, T])
        qT, kT = sb("qT", [D, T]), sb("kT", [D, T])
        masked = [sb(f"masked{w}", [NT, NT + 2 * RADII[w]]) for w in range(3)]
        smax = sb("smax", [NT, 3])
        sbias = sb("sbias", [NT, 3])
        probs = [[sb(f"probs{t}{w}", [NT, T]) for w in range(3)] for t in range(3)]
        den = sb("den", [NT, 3])
        rden = sb("rden", [NT, 3])
        diag = sb("diag", [NT, 3, NT])
        attnT = sb("attnT", [NT, 3 * NT])
        axT = sb("axT", [D, NT])
        res = sb("res", [NT, 3, D])
        xh = sb("xh", [NT, 3, D])
        h = [sb(f"hsum{p}", [NT, 3, D]) for p in range(2)]
        hn = sb("hn", [NT, 3, D])
        hnT = [sb(f"hnT{p}", [D, 3, NT]) for p in range(2)]
        act_g = [sb(f"act_g{p}", [128, 3, NG, EL, TG]) for p in range(2)]

        sq_junk = sb("sq_junk", [NT, H, QD])
        qss = sb("qss", [NT, H])
        qvar = sb("qvar", [NT, H])
        qrstd = sb("qrstd", [NT, H])
        qn = sb("qn", [NT, H, QD])
        qsq = sb("qsq", [NT, 2 * H, HALF])
        nss = sb("nss", [NT, 2 * H])
        nmx = sb("nmx", [NT, 2 * H])
        nrec = sb("nrec", [NT, 2 * H])
        qnT = sb("qnT", [128, PAIRS, NT])
        scores = [sb(f"scores{p}", [NT, H, 2, PK]) for p in range(2)]
        val = sb("val", [NT, H, 2, TOP])
        idx = sb("idx", [NT, H, 2, TOP], u16)
        idxf = sb("idxf", [NT, H, 2, TOP])
        cs = sb("cs", [NT, H, NC])
        cr = sb("cr", [NT, H, NC])
        ce = sb("ce", [NT, H, NC])
        cx = sb("cx", [NT, H, NC])
        best = sb("best", [NT, H, TOP])
        wsel = sb("wsel", [NT, H, NC])
        wsum = sb("wsum", [NT, H])
        wsum2 = sb("wsum2", [NT, H])
        wrec = sb("wrec", [NT, H])
        wn = sb("wn", [NT, H, NC])
        wcell = sb("wcell", [NT, 3, H, NC], f16)
        wcT = sb("wcT", [2 * NC, PAIRS, 3, NT], f16)
        wm = sb("wm", [128, 2, 2, NT], f16)
        eh = sb("eh", [128, 2, NT], i16)
        el = sb("el", [128, 2, NT], i16)
        oh = sb("oh", [128, 2, NG, EH, TG], f16)
        ol = sb("ol", [128, 2, EL, NT], f16)
        wl = sb("wl", [128, 2, 2, EL, NT], f16)
        prod = sb("prod", [128, EL, NT])
        o_sb = sb("o_sb", [NT, 3, D])

        bankA, bankB, bankC, bankQ = (ctx.enter_context(nc.psum_tensor(f"bank{i}", [128, 512], f32)) for i in "ABCQ")
        bankS = ctx.enter_context(nc.psum_tensor("bankS", [128, 1024], f32))
        bankM = ctx.enter_context(nc.psum_tensor("bankM", [128, 1024], f32))
        wcT_ps = bankS[0:2 * NC, :].bitcast(f16).rearrange("p (k n) -> p k n", k=2)
        merged = bankM[:, :].rearrange("p (k n) -> p k n", k=2)
        coef = bankM[:, 0:NG * EL * TG].rearrange("p (g l t) -> p g l t", g=NG, l=EL)
        ffn = bankM[0:NT, 512:512 + D]

        w_in = sem("w_in")
        setup_pool, setup_dve, setup_act, setup_pe = (sem(f"setup_{e}") for e in ("pool", "dve", "act", "pe"))
        passed_dve, passed_pool = sem("passed_dve"), sem("passed_pool")
        setup_key = sem("setup_key")
        x_loaded = [sem(f"x_loaded{p}") for p in range(2)]
        x_turned = sem("x_turned")
        xT_ready = sem("xT_ready")
        conv_done = sem("conv_done")
        wsq_ready = sem("wsq_ready")
        wnorm_ready = sem("wnorm_ready")
        tscale_ready = sem("tscale_ready")
        tanh_done = sem("tanh_done")
        h0_ready = sem("h0_ready")
        ln_stats = [sem(f"ln_stats{i}") for i in range(3)]
        ln_rstd = [sem(f"ln_rstd{i}") for i in range(3)]
        ln_shift = [sem(f"ln_shift{i}") for i in range(3)]
        xl_ready = sem("xl_ready")
        xl_turned = sem("xl_turned")
        xlT_ready = sem("xlT_ready")
        qk_done = sem("qk_done")
        qk_ready = sem("qk_ready")
        xb_ready = sem("xb_ready")
        attn_scored = sem("attn_scored")
        smax_ready = sem("smax_ready")
        probs_ready = sem("probs_ready")
        rden_ready = sem("rden_ready")
        diag_ready = sem("diag_ready")
        attn_turned = sem("attn_turned")
        attnT_ready = sem("attnT_ready")
        ax_done = sem("ax_done")
        axT_ready = sem("axT_ready")
        wo_done = sem("wo_done")
        res_ready = sem("res_ready")
        xh_ready = sem("xh_ready")
        h_ready = sem("h_ready")
        hn_ready = sem("hn_ready")
        hn_turned = sem("hn_turned")
        hnT_ready = sem("hnT_ready")
        inner_done = sem("inner_done")
        gelu_done = sem("gelu_done")
        q_done = sem("q_done")
        qss_ready = sem("qss_ready")
        qrstd_ready = sem("qrstd_ready")
        qn_scaled = sem("qn_scaled")
        qn_affine = sem("qn_affine")
        nss_ready = sem("nss_ready")
        qn_ready = sem("qn_ready")
        qn_turned = sem("qn_turned")
        qnT_ready = sem("qnT_ready")
        scored = sem("scored")
        scores_ready = sem("scores_ready")
        ranked = sem("ranked")
        idxf_ready = sem("idxf_ready")
        cells_ready = sem("cells_ready")
        exp_ready = sem("exp_ready")
        chosen = sem("chosen")
        weights = sem("weights")
        whigh_ready = sem("whigh_ready")
        cells_turned = sem("cells_turned")
        wcT_ready = sem("wcT_ready")
        merge_done = sem("merge_done")
        wm_ready = sem("wm_ready")
        digits_ready = sem("digits_ready")
        onehigh_ready = sem("onehigh_ready")
        wl_ready = sem("wl_ready")
        scattered = sem("scattered")
        prod_ready = sem("prod_ready")
        ffn_done = sem("ffn_done")
        out_ready = sem("out_ready")
        stored = [sem(f"stored{t}") for t in range(3)]

        block = ctx.enter_context(nc.Block())

        def linker(eng, s, per, call):
            count = [0]

            def link(ins, wait=True):
                count[0] += 1
                assert count[0] <= per
                ins.then_inc(s, 1)
                if wait:
                    eng.wait_ge(s, per * call + count[0])
            return link

        def wait(eng, s, value):
            if not isinstance(value, int) or value > 0:
                eng.wait_ge(s, value)

        def settled(eng, s):
            eng.sem_inc(s, 1)

        def following(j, par):
            return (j, 1) if par == 0 else (j + 1, 0)

        def batch(v, b):
            one = v[b:b + 1, :, :] if isinstance(b, int) else v[bass.ds(b, 1), :, :]
            return one.rearrange("a p c -> (a p) c")

        def run(eng, start, body, end):
            start()
            body(0, 0, first=True)
            with eng.Fori(0, B // 2 - 1) as i:
                body(i, 1)
                body(i + 1, 0)
            body(B // 2 - 1, 1, final=True)
            end()

        kern = tok_kernel[0:TAPS - 1, :, :].rearrange("(m s) c f -> s c m f", s=2)
        loads = [(id32[:, :], ident), (merge_sb[:, :], merge),
                 (rows[0:1, 0:D], row(tok_bias)), (rows[0:1, D:2 * D], row(bo)),
                 (rows[0:1, 2 * D:3 * D], row(gamma)), (rows[0:1, 3 * D:4 * D], row(beta)),
                 (rows[0:1, 4 * D:4 * D + QD], row(lng)), (rows[0:1, 4 * D + QD:4 * D + 2 * QD], row(lnb)),
                 (fbq_row, row(fbq)), (fwq_in[:, :, :], fwq.rearrange("(k p) d -> p k d", p=128)),
                 (key_in[:, 0, :], keys0), (key_in[:, 1, :], keys1), (down_in[:, :], down[0:128, :]),
                 (conv_w[0:C, 0:4, :], kern[0, :, :, :]), (conv_w[C:2 * C, 0:4, :], kern[1, :, :, :]),
                 (conv_w[0:C, 4, :], tok_kernel[TAPS - 1, :, :]),
                 (wq_sb[:, :], wq), (wk_sb[:, :], wk), (wo_sb[:, :], wo),
                 (bq_sb[:, :], col(bq)), (bk_sb[:, :], col(bk))]
        for t in range(TG):
            loads.append((up_x[t:128:TG, :, :], up[0:128, :].rearrange("(h l) o -> h l o", l=EL)))
        ALL_LOADED = 16 * len(loads)

        @block.sync
        def _(sp):
            def load_x(j, par):
                b = 2 * j + par
                wait(sp, x_turned, b - 1)
                xb_, s = batch(x, b), x_in[par]
                sp.dma_start(s[:, :, 0, :], xb_[0:L, :].rearrange("(t p) c -> p t c", t=3)).then_inc(x_loaded[par], 16)
                sp.dma_start(s[:, 0:2, 1, :], xb_[1:1 + 2 * XT, :].rearrange("(t p) c -> p t c", t=2)).then_inc(x_loaded[par], 16)
                sp.dma_start(s[0:XT - 1, 2, 1, :], xb_[1 + 2 * XT:L, :]).then_inc(x_loaded[par], 16)

            def store(b, t):
                sp.wait_ge(out_ready, 3 * b + t + 1)
                f = FIRST[t]
                sp.dma_start(batch(out, b)[OFF[t] + f:OFF[t] + NT, :], o_sb[f:NT, t, :]).then_inc(stored[t], 16)

            def start():
                for dst, src in loads:
                    sp.dma_start(dst, src).then_inc(w_in, 16)
                sp.wait_ge(setup_pool, 1)
                load_x(0, 0)
                load_x(0, 1)

            def body(j, par, first=False, final=False):
                b = 2 * j + par
                if not first:
                    if not final:
                        load_x(*following(j, par))
                    store(b - 1, 2)
                store(b, 0)
                store(b, 1)

            def end():
                store(B - 1, 2)
                for t in range(3):
                    sp.wait_ge(stored[t], 16 * B)

            run(sp, start, body, end)

        @block.gpsimd
        def _(pool):
            g = nc.gpsimd

            def start():
                for p in range(2):
                    last = g.memset(x_in[p][:, 2, 1, :], 0.0)
                last.then_inc(setup_pool, 1)
                g.memset(ones[:, :], 1.0)
                g.memset(power[:, 0:45], -0.5)
                g.memset(power[:, 45:48], 0.5)
                g.memset(key_z[:, :, :], 0.0).then_inc(setup_pool, 1)
                pool.wait_ge(setup_dve, 2)
                link = linker(pool, setup_key, 2, 0)
                link(g.tensor_scalar(key_n[:, :], key_n[:, :], 1.0e-24, None, ALU.max))
                link(g.tensor_tensor(key_n[:, :], key_n[:, :], power[0:PK, 0:2], ALU.pow))
                g.memset(down_x[:, :, :, :], 0.0).then_inc(setup_pool, 1)
                for t in range(3):
                    for w in range(3):
                        g.memset(masks[t, w][:, :], 0.0)
                        g.memset(probs[t][w][:, :], 0.0)
                g.memset(small[:, :], 0.0).then_inc(setup_pool, 1)
                pool.wait_ge(setup_pool, 4)
                for t in range(3):
                    for w in range(3):
                        lo, hi = band(t, w)
                        g.affine_select(out=masks[t, w][:, :], in_=masks[t, w][:, :], compare_op=ALU.is_ge, fill=NEG,
                                        base=lo - OFF[t] + RADII[w], pattern=[[1, hi - lo]], channel_multiplier=-1)
                g.memset(small[:, :], 0.0).then_inc(setup_pool, 1)
                pool.wait_ge(setup_pool, 5)
                for t in range(3):
                    for w in range(3):
                        lo, hi = band(t, w)
                        last = g.affine_select(out=masks[t, w][:, :], in_=masks[t, w][:, :], compare_op=ALU.is_ge, fill=NEG,
                                               base=OFF[t] - lo + RADII[w], pattern=[[-1, hi - lo]], channel_multiplier=1)
                last.then_inc(setup_pool, 1)
                pool.wait_ge(setup_act, 2)
                p1_norm(0)
                p1_h0(0)
                p1_rstd(0, 0)
                p1_xb(0)
                for t in range(3):
                    p1_diag(0, t)
                p1_rstd(1, 0)
                p1_h(0, 0)
                p1_rstd(2, 0)
                q_rstd(0)
                q_affine(0)
                q_unit(0)

            def p1_norm(b):
                pool.wait_ge(wsq_ready, b + 1)
                wait(pool, tscale_ready, 5 * b)
                g.tensor_tensor(wnorm[:, :], wsq[:, :], power[0:NT, 45:48], ALU.pow).then_inc(wnorm_ready, 1)

            def p1_h0(b):
                link = linker(pool, h0_ready, 2, b)
                pool.wait_ge(tanh_done, b + 1)
                wait(pool, h_ready, 3 * b)
                link(g.tensor_tensor(h0[:, :, :], th[:, :, :], tokb.unsqueeze(1).to_broadcast([NT, 3, D]), ALU.add))
                settled(pool, passed_pool)
                link(g.tensor_scalar(h0[:, :, :], h0[:, :, :], 0.0, None, ALU.max))

            def p1_rstd(i, b):
                pool.wait_ge(ln_stats[i], 3 * (b + 1))
                wait(pool, ln_shift[i], b)
                wait(pool, (xl_ready, xh_ready, hn_ready)[i], b)
                g.tensor_tensor(lnr[i][:, :], lnv[i][:, :], power[0:NT, 0:3], ALU.pow).then_inc(ln_rstd[i], 1)

            def p1_xb(b):
                pool.wait_ge(xl_ready, b + 1)
                wait(pool, res_ready, b)
                g.tensor_tensor(xb[:, :, :], xl[:, :, :], bob.unsqueeze(1).to_broadcast([NT, 3, D]), ALU.add).then_inc(xb_ready, 1)

            def p1_diag(b, t):
                n = 3 * b + t
                pool.wait_ge(rden_ready, n + 1)
                wait(pool, attn_turned, n)
                settled(pool, passed_pool)
                for w in range(3):
                    last = g.tensor_scalar(diag[:, w, :], id32[0:NT, 0:NT], rden[:, w:w + 1], 1.0 / 3.0, ALU.mult, ALU.mult)
                last.then_inc(diag_ready, 1)

            def p1_h(j, par):
                b = 2 * j + par
                link = linker(pool, h_ready, 3, b)
                pool.wait_ge(xh_ready, b + 1)
                wait(pool, out_ready, 3 * (b - 1) if not isinstance(b, int) or b > 1 else 0)
                link(g.tensor_tensor(h[par][:, :, :], xh[:, :, :], gam.unsqueeze(1).to_broadcast([NT, 3, D]), ALU.mult))
                link(g.tensor_tensor(h[par][:, :, :], h[par][:, :, :], bet.unsqueeze(1).to_broadcast([NT, 3, D]), ALU.add))
                link(g.tensor_tensor(h[par][:, :, :], h[par][:, :, :], h0[:, :, :], ALU.add), wait=False)

            def q_rstd(n):
                link = linker(pool, qrstd_ready, 2, n)
                pool.wait_ge(qss_ready, n + 1)
                wait(pool, qn_scaled, n)
                settled(pool, passed_pool)
                link(g.tensor_scalar(qvar[:, :], qss[:, :], 1.0 / QD, 1.0e-5, ALU.mult, ALU.add))
                link(g.tensor_tensor(qrstd[:, :], qvar[:, :], power[0:NT, 0:H], ALU.pow), wait=False)

            def q_affine(n):
                link = linker(pool, qn_affine, 3, n)
                pool.wait_ge(qn_scaled, n + 1)
                wait(pool, nss_ready, n)
                link(g.tensor_tensor(qn[:, :, :], qn[:, :, :], lng_bc.unsqueeze(1).to_broadcast([NT, H, QD]), ALU.mult))
                link(g.tensor_tensor(qn[:, :, :], qn[:, :, :], lnb_bc.unsqueeze(1).to_broadcast([NT, H, QD]), ALU.add))
                q2 = qn[:, :, :].rearrange("p h (s q) -> p (h s) q", s=2)
                link(g.tensor_tensor(qsq[:, :, :], q2, q2, ALU.mult), wait=False)

            def q_unit(n):
                link = linker(pool, qn_ready, 3, n)
                pool.wait_ge(nss_ready, n + 1)
                settled(pool, passed_pool)
                link(g.tensor_scalar(nmx[:, :], nss[:, :], 1.0e-24, None, ALU.max))
                link(g.tensor_tensor(nrec[:, :], nmx[:, :], power[0:NT, 0:2 * H], ALU.pow))
                q2 = qn[:, :, :].rearrange("p h (s q) -> p (h s) q", s=2)
                link(g.tensor_tensor(q2, q2, nrec[:, :].unsqueeze(2).to_broadcast([NT, 2 * H, HALF]), ALU.mult), wait=False)

            def rank_sums(n):
                link = linker(pool, cells_ready, 2, n)
                pool.wait_ge(ranked, 16 * (n + 1))
                wait(pool, chosen, 8 * n)
                wait(pool, exp_ready, n)
                for src, dst in ((val, cs), (idxf, ce)):
                    if src is idxf:
                        pool.wait_ge(idxf_ready, n + 1)
                    at = 0
                    for a in range(5):
                        k = TOP // (a + 1)
                        last = g.tensor_tensor(dst[:, :, at:at + k], src[:, :, 0, a:a + 1].to_broadcast([NT, H, k]),
                                               src[:, :, 1, 0:k], ALU.add)
                        at += k
                    last = g.tensor_tensor(dst[:, :, at:at + 6].rearrange("p h (a c) -> p h a c", c=2),
                                           src[:, :, 0, 5:8].unsqueeze(3).to_broadcast([NT, H, 3, 2]),
                                           src[:, :, 1, 0:2].unsqueeze(2).to_broadcast([NT, H, 3, 2]), ALU.add)
                    at += 6
                    last = g.tensor_tensor(dst[:, :, at:at + 8], src[:, :, 0, 8:16],
                                           src[:, :, 1, 0:1].to_broadcast([NT, H, 8]), ALU.add)
                    assert at + 8 == NC
                    link(last, wait=False)

            def normalise(n):
                link = linker(pool, weights, 2, n)
                pool.wait_ge(chosen, 8 * (n + 1))
                wait(pool, cells_turned, n)
                link(g.tensor_tensor(wn[:, :, :], wsel[:, :, :], wrec[:, :].unsqueeze(2).to_broadcast([NT, H, NC]), ALU.mult))
                pool.wait_ge(whigh_ready, n + 1)
                link(g.tensor_tensor(wcell[:, 1, :, :], wn[:, :, :], wcell[:, 0, :, :], ALU.subtract), wait=False)

            def one_high(m, quarter):
                pool.wait_ge(digits_ready, 2 * m + 1)
                wait(pool, scattered, m)
                settled(pool, passed_pool)
                for v in range(8 * quarter, 8 * quarter + 8):
                    last = g.tensor_scalar(oh[:, :, :, v, :], eh[:, :, :].rearrange("p k (g t) -> p k g t", t=TG), float(v), None, ALU.is_equal)
                last.then_inc(onehigh_ready, 1)

            def body(j, par, first=False, final=False):
                b = 2 * j + par
                nj, npar = following(j, par)
                attend = not final
                for t in range(3):
                    n = 3 * b + t
                    back = not (first and t == 0)

                    def high(quarter):
                        if back:
                            one_high(n - 1, quarter)

                    if t == 0:
                        q_rstd(n + 1)
                        if attend:
                            p1_norm(b + 1)
                        high(0)
                        if attend:
                            p1_h0(b + 1)
                        q_affine(n + 1)
                        if attend:
                            p1_rstd(0, b + 1)
                        high(1)
                        q_unit(n + 1)
                        if attend:
                            p1_xb(b + 1)
                        high(2)
                        if attend:
                            p1_diag(b + 1, 0)
                        high(3)
                    elif t == 1:
                        q_rstd(n + 1)
                        high(0)
                        if attend:
                            p1_diag(b + 1, 1)
                        q_affine(n + 1)
                        high(1)
                        if attend:
                            p1_diag(b + 1, 2)
                        q_unit(n + 1)
                        high(2)
                        if attend:
                            p1_rstd(1, b + 1)
                        high(3)
                        if attend:
                            p1_h(nj, npar)
                    else:
                        if attend:
                            p1_rstd(2, b + 1)
                        high(0)
                        if attend:
                            q_rstd(n + 1)
                        high(1)
                        if attend:
                            q_affine(n + 1)
                        high(2)
                        high(3)
                        if attend:
                            q_unit(n + 1)
                    rank_sums(n)
                    normalise(n)

            def end():
                for quarter in range(4):
                    one_high(3 * B - 1, quarter)

            run(pool, start, body, end)

        @block.scalar
        def _(act):
            a = nc.scalar

            def start():
                act.wait_ge(w_in, ALL_LOADED)
                a.activation(id16[:, :], id32[:, :], ACT.Copy).then_inc(setup_act, 1)
                act.wait_ge(setup_pe, 1)
                a.activation(vecs[:, 0:4 * D], bankA[:, :], ACT.Copy)
                a.activation(vecs[:, 4 * D:], bankB[:, 0:2 * QD], ACT.Copy).then_inc(setup_act, 1)
                act.wait_ge(setup_pe, 2)
                a.activation(fwqT[:, :], bankS[:, 0:H * QD], ACT.Copy).then_inc(setup_act, 1)
                act.wait_ge(setup_pe, 3)
                a.activation(downT[:, :], bankC[:, 0:128], ACT.Copy).then_inc(setup_act, 1)
                act.wait_ge(setup_pe, 4)
                a.activation(key_bd[:, :], bankQ[:, 0:4 * PK], ACT.Copy).then_inc(setup_act, 1)
                p1_xT(0)
                p1_tanh(0)
                p1_ln(0, 0, 0)
                p1_xlT(0)
                p1_qk(0)
                act.wait_ge(setup_pool, 4)
                for t in range(3):
                    p1_probs(0, t)
                    p1_attnT(0, t)
                    p1_axT(0, t)
                p1_ln(1, 0, 0)
                p1_ln(2, 0, 0)
                p1_hnT(0, 0)
                q_squares(0)
                q_scaled(0)
                q_T(0)
                q_scores(0, 0)
                for t in range(3):
                    p1_gelu(0, 0, t)

            def p1_xT(b):
                act.wait_ge(x_turned, b + 1)
                wait(act, conv_done, b)
                a.activation(xT[:, :], bankA[:, 0:L], ACT.Copy).then_inc(xT_ready, 1)
                a.activation(xT_sq[:, :], bankA[:, 0:L], ACT.Square).then_inc(xT_ready, 1)

            def p1_tanh(b):
                act.wait_ge(conv_done, b + 1)
                act.wait_ge(tscale_ready, 5 * (b + 1))
                wait(act, h0_ready, 2 * b)
                for t in range(3):
                    last = a.activation(th[:, t, :], bankB[0:NT, t * D:(t + 1) * D], ACT.Tanh, scale=tscale[:, t:t + 1])
                last.then_inc(tanh_done, 1)

            def p1_ln(i, j, par):
                b = 2 * j + par
                src, dst, done = ((h0, xl, xl_ready), (res, xh, xh_ready), (h[par], hn, hn_ready))[i]
                act.wait_ge(ln_shift[i], b + 1)
                if i == 0:
                    wait(act, ax_done, 3 * b)
                    wait(act, xb_ready, b)
                elif i == 1:
                    wait(act, h_ready, 3 * b)
                else:
                    wait(act, hn_turned, b)
                for t in range(3):
                    last = a.activation(dst[:, t, :], src[:, t, :], ACT.Identity, bias=lnm[i][:, t:t + 1], scale=lnr[i][:, t:t + 1])
                last.then_inc(done, 1)

            def p1_xlT(b):
                act.wait_ge(xl_turned, b + 1)
                wait(act, qk_done, 2 * b)
                a.activation(xlT[:, :], bankA[:, 0:T], ACT.Copy).then_inc(xlT_ready, 1)

            def p1_qk(b):
                wait(act, attn_scored, 3 * b)
                for i, (dst, src, bias) in enumerate(((qT, bankB, bq_sb), (kT, bankC, bk_sb))):
                    act.wait_ge(qk_done, 2 * b + 1 + i)
                    a.activation(dst[:, :], src[:, 0:T], ACT.Identity, bias=bias[:, 0:1]).then_inc(qk_ready, 1)

            def p1_probs(b, t):
                n = 3 * b + t
                act.wait_ge(smax_ready, 2 * (n + 1))
                wait(act, attn_turned, 3 * b)
                wait(act, rden_ready, n)
                for w in range(3):
                    lo, hi = band(t, w)
                    last = a.activation(probs[t][w][:, lo:hi], masked[w][:, 0:hi - lo], ACT.Exp, bias=sbias[:, w:w + 1],
                                        scale=SCORE_SCALE, accum_out=den[:, w:w + 1])
                last.then_inc(probs_ready, 1)

            def p1_attnT(b, t):
                n = 3 * b + t
                act.wait_ge(attn_turned, n + 1)
                wait(act, ax_done, n)
                cc = chunks(t, 2)
                lo, hi = cc[0] * NT, (cc[-1] + 1) * NT
                a.activation(attnT[:, lo:hi], bankB[0:NT, lo:hi], ACT.Copy).then_inc(attnT_ready, 1)

            def p1_axT(b, t):
                n = 3 * b + t
                act.wait_ge(ax_done, n + 1)
                wait(act, wo_done, n)
                a.activation(axT[:, :], bankC[:, 0:NT], ACT.Copy).then_inc(axT_ready, 1)

            def p1_hnT(j, par):
                b = 2 * j + par
                act.wait_ge(hn_turned, b + 1)
                if not (isinstance(b, int) and b < 2):
                    wait(act, q_done, 3 * (b - 1))
                    wait(act, inner_done, 3 * (b - 1))
                a.activation(hnT[par][:, :, :].rearrange("p t n -> p (t n)"), bankA[:, 0:3 * NT], ACT.Copy).then_inc(hnT_ready, 1)

            def p1_gelu(j, par, t):
                b = 2 * j + par
                act.wait_ge(inner_done, 3 * b + t + 1)
                if not (isinstance(b, int) and b < 2):
                    wait(act, prod_ready, 3 * (b - 1))
                bank = (bankB, bankC, bankA)[t]
                a.activation(act_g[par][:, t, :, :, :].rearrange("p g l t -> p (g l t)"), bank[:, 0:NG * EL * TG], ACT.Gelu)\
                 .then_inc(gelu_done, 1)

            def q_squares(n):
                act.wait_ge(q_done, n + 1)
                wait(act, qrstd_ready, 2 * n)
                for i in range(H):
                    last = a.activation(sq_junk[:, i, :], bankQ[0:NT, i * QD:(i + 1) * QD], ACT.Square, accum_out=qss[:, i:i + 1])
                last.then_inc(qss_ready, 1)

            def q_scaled(n):
                act.wait_ge(qrstd_ready, 2 * (n + 1))
                wait(act, qn_turned, n)
                for i in range(H):
                    last = a.activation(qn[:, i, :], bankQ[0:NT, i * QD:(i + 1) * QD], ACT.Identity, scale=qrstd[:, i:i + 1])
                last.then_inc(qn_scaled, 1)

            def q_T(n):
                act.wait_ge(qn_turned, n + 1)
                wait(act, scored, n)
                a.activation(qnT[:, :, :].rearrange("p k n -> p (k n)"), bankQ[:, 0:PAIRS * NT], ACT.Copy).then_inc(qnT_ready, 1)

            def q_scores(n, slot):
                act.wait_ge(scored, n + 1)
                wait(act, ranked, 16 * (n - 1))
                a.activation(scores[slot][:, :, :, :].rearrange("p h s e -> p (h s e)"), bankS[0:NT, :], ACT.Copy)\
                 .then_inc(scores_ready, 1)

            def index_floats(n):
                act.wait_ge(ranked, 16 * (n + 1))
                wait(act, cells_ready, 2 * n)
                a.activation(idxf[:, :, :, :], idx[:, :, :, :], ACT.Copy).then_inc(idxf_ready, 1)

            def cell_exp(n):
                act.wait_ge(cells_ready, 2 * n + 1)
                wait(act, chosen, 8 * n)
                a.activation(cx[:, :, :], cs[:, :, :], ACT.Exp).then_inc(exp_ready, 1)

            def weight_high(n):
                act.wait_ge(weights, 2 * n + 1)
                a.activation(wcell[:, 0, :, :], wn[:, :, :], ACT.Copy).then_inc(whigh_ready, 1)

            def cells_T(n):
                act.wait_ge(cells_turned, n + 1)
                wait(act, merge_done, n)
                for k in range(2):
                    last = a.activation(wcT[:, 2 * k:2 * k + 2, :, :].rearrange("p a k n -> p (a k n)"),
                                        wcT_ps[:, k, 0:6 * NT], ACT.Copy)
                last.then_inc(wcT_ready, 1)

            def merged_weights(n):
                act.wait_ge(merge_done, n + 1)
                wait(act, wl_ready, 2 * n)
                a.activation(wm[:, :, :, :].rearrange("p k s n -> p k (s n)"), merged[:, :, 0:2 * NT], ACT.Copy).then_inc(wm_ready, 1)

            def body(j, par, first=False, final=False):
                b = 2 * j + par
                nj, npar = following(j, par)
                attend = not final
                for t in range(3):
                    n = 3 * b + t
                    slot = (par + t + 1) % 2
                    if t == 0:
                        if attend:
                            p1_xT(b + 1)
                        q_squares(n + 1)
                        if attend:
                            p1_tanh(b + 1)
                        q_scaled(n + 1)
                        if attend:
                            p1_ln(0, nj, npar)
                            p1_xlT(b + 1)
                        q_T(n + 1)
                        if attend:
                            p1_qk(b + 1)
                        q_scores(n + 1, slot)
                        if attend:
                            p1_probs(b + 1, 0)
                            p1_attnT(b + 1, 0)
                        index_floats(n)
                        if attend:
                            p1_axT(b + 1, 0)
                    elif t == 1:
                        if attend:
                            p1_probs(b + 1, 1)
                        q_squares(n + 1)
                        if attend:
                            p1_attnT(b + 1, 1)
                            p1_axT(b + 1, 1)
                        q_scaled(n + 1)
                        if attend:
                            p1_probs(b + 1, 2)
                            p1_attnT(b + 1, 2)
                            p1_axT(b + 1, 2)
                        q_T(n + 1)
                        q_scores(n + 1, slot)
                        if attend:
                            p1_ln(1, nj, npar)
                        index_floats(n)
                    else:
                        if attend:
                            p1_ln(2, nj, npar)
                            p1_hnT(nj, npar)
                            q_squares(n + 1)
                            q_scaled(n + 1)
                        index_floats(n)
                        if attend:
                            q_T(n + 1)
                            q_scores(n + 1, slot)
                    cell_exp(n)
                    weight_high(n)
                    cells_T(n)
                    merged_weights(n)
                    if t == 2 and attend:
                        for u in range(3):
                            p1_gelu(nj, npar, u)

            run(act, start, body, lambda: None)

        @block.tensor
        def _(pe):
            e = nc.tensor

            def start():
                pe.wait_ge(w_in, ALL_LOADED)
                pe.wait_ge(setup_pool, 2)
                e.matmul(bankA[:, :], ones[0:1, :], rows[0:1, 0:4 * D], start=True, stop=True)
                e.matmul(bankB[:, 0:2 * QD], ones[0:1, :], rows[0:1, 4 * D:4 * D + 2 * QD], start=True, stop=True)\
                 .then_inc(setup_pe, 1)
                for k in range(4):
                    last = e.transpose(bankS[:, k * 128:(k + 1) * 128], fwq_in[:, k, :], id32[:, :])
                last.then_inc(setup_pe, 1)
                e.transpose(bankC[:, 0:128], down_in[:, :], id32[:, :]).then_inc(setup_pe, 1)
                pe.wait_ge(setup_dve, 3)
                for k in range(4):
                    last = e.transpose(bankQ[:, k * PK:(k + 1) * PK], key_z[:, k, :], id32[0:PK, 0:PK])
                last.then_inc(setup_pe, 1)
                pe.wait_ge(setup_act, 5)
                pe.wait_ge(setup_dve, 10)
                p1_turn_x(0, 0)
                p1_conv(0)
                p1_turn_xl(0)
                p1_project(0)
                for t in range(3):
                    p1_scores(0, t)
                    p1_turn_attn(0, t)
                    p1_ax(0, t)
                    p1_wo(0, t)
                p1_turn_hn(0)
                q_product(0, 0, 0)
                for t in range(3):
                    p1_inner(0, 0, t)
                q_turn(0)
                q_score(0)

            def p1_turn_x(j, par):
                b = 2 * j + par
                pe.wait_ge(x_loaded[par], 48 * (j + 1))
                wait(pe, gelu_done, 3 * b)
                for t in range(3):
                    last = e.transpose(bankA[:, t * XT:(t + 1) * XT], x_in[par][:, t, :, :].rearrange("p s c -> p (s c)"), id32[0:XT, 0:XT])
                last.then_inc(x_turned, 1)

            def p1_conv(b):
                pe.wait_ge(xT_ready, 2 * (b + 1))
                for t in range(3):
                    for m in range(5):
                        k = 2 * C if m < 4 else C
                        win = slice(OFF[t] + 2 * m, OFF[t] + 2 * m + NT)
                        e.matmul(bankB[0:NT, t * D:(t + 1) * D], xT[0:k, win], conv_w[0:k, m, :], start=m == 0, stop=m == 4)
                    for m in range(5):
                        k = 2 * C if m < 4 else C
                        win = slice(OFF[t] + 2 * m, OFF[t] + 2 * m + NT)
                        last = e.matmul(bankB[0:NT, 3 * D + t:3 * D + t + 1], xT_sq[0:k, win], ones[0:k, 0:1], start=m == 0, stop=m == 4)
                last.then_inc(conv_done, 1)

            def p1_turn_xl(b):
                pe.wait_ge(xl_ready, b + 1)
                for t in range(3):
                    last = e.transpose(bankA[:, OFF[t]:OFF[t] + NT], xl[:, t, :], id32[0:NT, 0:NT])
                last.then_inc(xl_turned, 1)

            def p1_project(b):
                pe.wait_ge(xlT_ready, b + 1)
                pe.wait_ge(tanh_done, b + 1)
                e.matmul(bankB[:, 0:T], wq_sb[:, :], xlT[:, :], start=True, stop=True).then_inc(qk_done, 1)
                e.matmul(bankC[:, 0:T], wk_sb[:, :], xlT[:, :], start=True, stop=True).then_inc(qk_done, 1)

            def p1_scores(b, t):
                n = 3 * b + t
                pe.wait_ge(qk_ready, 2 * (b + 1))
                if t:
                    pe.wait_ge(smax_ready, 2 * n)
                lo, hi = band(t, 2)
                e.matmul(bankA[0:NT, 0:hi - lo], qT[:, OFF[t]:OFF[t] + NT], kT[:, lo:hi], start=True, stop=True)\
                 .then_inc(attn_scored, 1)

            def p1_turn_attn(b, t):
                n = 3 * b + t
                pe.wait_ge(diag_ready, n + 1)
                wait(pe, attnT_ready, n)
                for c in chunks(t, 2):
                    ws = [w for w in range(3) if c in chunks(t, w)]
                    for w in ws:
                        last = e.matmul(bankB[0:NT, c * NT:(c + 1) * NT], probs[t][w][:, OFF[c]:OFF[c] + NT], diag[:, w, :],
                                        start=w == ws[0], stop=w == ws[-1])
                last.then_inc(attn_turned, 1)

            def p1_ax(b, t):
                n = 3 * b + t
                pe.wait_ge(attnT_ready, n + 1)
                wait(pe, axT_ready, n)
                if t == 0:
                    wait(pe, qk_ready, 2 * (b + 1))
                cc = chunks(t, 2)
                for c in cc:
                    last = e.matmul(bankC[:, 0:NT], xl[0:KEYS[c], c, :], attnT[0:KEYS[c], c * NT:(c + 1) * NT],
                                    start=c == cc[0], stop=c == cc[-1])
                last.then_inc(ax_done, 1)

            def p1_wo(b, t):
                n = 3 * b + t
                pe.wait_ge(axT_ready, n + 1)
                e.matmul(bankC[0:NT, (1 + t) * D:(2 + t) * D], axT[:, :], wo_sb[:, :], start=True, stop=True).then_inc(wo_done, 1)

            def p1_turn_hn(b):
                pe.wait_ge(hn_ready, b + 1)
                for t in range(3):
                    last = e.transpose(bankA[:, t * NT:(t + 1) * NT], hn[:, t, :], id32[0:NT, 0:NT])
                last.then_inc(hn_turned, 1)

            def p1_inner(j, par, t):
                b = 2 * j + par
                pe.wait_ge(hnT_ready, b + 1)
                if t == 0:
                    pe.wait_ge(attnT_ready, 3 * (b + 1))
                elif t == 1:
                    pe.wait_ge(res_ready, b + 1)
                bank = (bankB, bankC, bankA)[t]
                dst = bank[:, 0:NG * EL * TG].rearrange("p (g l t) -> p g l t", g=NG, l=EL)
                toks = hnT[par][:, t, :].rearrange("p (g t) -> p g t", t=TG)
                for q in range(TG):
                    for l in range(EL):
                        last = e.matmul(dst[:, :, l, q], down_x[:, q, l, :], toks[:, :, q], start=True, stop=True)
                last.then_inc(inner_done, 1)

            def q_product(j, par, t):
                b = 2 * j + par
                n = 3 * b + t
                pe.wait_ge(hnT_ready, b + 1)
                wait(pe, qnT_ready, n)
                e.matmul(bankQ[0:NT, :], hnT[par][:, t, :], fwqT[:, :], start=True, stop=False)
                e.matmul(bankQ[0:NT, :], ones[0:1, 0:NT], fbq_row, start=False, stop=True).then_inc(q_done, 1)

            def q_turn(n):
                pe.wait_ge(qn_ready, 3 * (n + 1))
                for k in range(PAIRS):
                    last = e.transpose(bankQ[:, k * NT:(k + 1) * NT], qn[:, 2 * k:2 * k + 2, :].rearrange("p h q -> p (h q)"), id32[0:NT, 0:NT])
                last.then_inc(qn_turned, 1)

            def q_score(n):
                pe.wait_ge(qnT_ready, n + 1)
                wait(pe, scores_ready, n)
                wait(pe, wcT_ready, n - 1)
                for k in range(PAIRS):
                    last = e.matmul(bankS[0:NT, k * 4 * PK:(k + 1) * 4 * PK], qnT[:, k, :], key_bd[:, :], start=True, stop=True)
                last.then_inc(scored, 1)

            def turn_cells(n, final):
                pe.wait_ge(weights, 2 * (n + 1))
                pe.wait_ge(chosen, 8 * (n + 1))
                pe.wait_ge(scores_ready, n + (1 if final else 2))
                wait(pe, wcT_ready, n)
                for i in range(3 * PAIRS):
                    k, part = i // 3, i % 3
                    last = e.transpose(wcT_ps[:, i // 6, (i % 6) * NT:(i % 6 + 1) * NT],
                                       wcell[:, part, 2 * k:2 * k + 2, :].rearrange("p h c -> p (h c)"), id16[0:NT, 0:NT])
                last.then_inc(cells_turned, 1)

            def merge_cells(n):
                pe.wait_ge(wcT_ready, n + 1)
                wait(pe, out_ready, n)
                wait(pe, prod_ready, n)
                for k in range(PAIRS):
                    q = 2 * SLOTS * (k % 2)
                    last = e.matmul(merged[q:q + 2 * SLOTS, k // 2, 0:3 * NT], merge_sb[:, :],
                                    wcT[:, k, :, :].rearrange("p k n -> p (k n)"), start=True, stop=True)
                last.then_inc(merge_done, 1)

            def scatter(m):
                pe.wait_ge(wl_ready, 2 * (m + 1))
                pe.wait_ge(wm_ready, m + 1)
                pe.wait_ge(digits_ready, 2 * (m + 1))
                pe.wait_ge(onehigh_ready, 4 * (m + 1))
                for g in range(NG):
                    for k in range(2):
                        for part in range(2):
                            last = e.matmul(coef[:, g, :, :], oh[:, k, g, :, :].rearrange("p v t -> p (v t)"),
                                            wl[:, part, k, :, TG * g:TG * (g + 1)], start=k + part == 0, stop=k + part == 2)
                last.then_inc(scattered, 1)

            def experts_out(m):
                pe.wait_ge(prod_ready, m + 1)
                for l in range(EL):
                    last = e.matmul(ffn, prod[:, l, :], up_x[:, l, :], start=l == 0, stop=l == EL - 1)
                last.then_inc(ffn_done, 1)

            def body(j, par, first=False, final=False):
                b = 2 * j + par
                nj, npar = following(j, par)
                attend = not final
                for t in range(3):
                    n = 3 * b + t
                    back = not (first and t == 0)
                    if t == 0:
                        if attend:
                            p1_turn_x(nj, npar)
                        q_product(j, par, 1)
                        if attend:
                            p1_conv(b + 1)
                        q_turn(n + 1)
                        if attend:
                            p1_turn_xl(b + 1)
                            p1_project(b + 1)
                            p1_scores(b + 1, 0)
                        q_score(n + 1)
                        if back:
                            scatter(n - 1)
                        if attend:
                            p1_turn_attn(b + 1, 0)
                            p1_scores(b + 1, 1)
                        if back:
                            experts_out(n - 1)
                        if attend:
                            p1_ax(b + 1, 0)
                            p1_wo(b + 1, 0)
                    elif t == 1:
                        q_product(j, par, 2)
                        if attend:
                            p1_scores(b + 1, 2)
                            p1_turn_attn(b + 1, 1)
                            p1_ax(b + 1, 1)
                            p1_wo(b + 1, 1)
                        q_turn(n + 1)
                        if attend:
                            p1_turn_attn(b + 1, 2)
                            p1_ax(b + 1, 2)
                            p1_wo(b + 1, 2)
                        q_score(n + 1)
                        scatter(n - 1)
                        experts_out(n - 1)
                    else:
                        if attend:
                            p1_turn_hn(b + 1)
                            q_product(nj, npar, 0)
                            for u in range(3):
                                p1_inner(nj, npar, u)
                            q_turn(n + 1)
                        scatter(n - 1)
                        if attend:
                            q_score(n + 1)
                        experts_out(n - 1)
                    turn_cells(n, final and t == 2)
                    merge_cells(n)

            def end():
                scatter(3 * B - 1)
                experts_out(3 * B - 1)

            run(pe, start, body, end)

        @block.vector
        def _(dve):
            v = nc.vector

            def start():
                link = linker(dve, setup_dve, 10, 0)
                dve.wait_ge(w_in, ALL_LOADED)
                link(v.tensor_tensor(key_sq[:, :, :], key_in[:, :, :], key_in[:, :, :], ALU.mult))
                link(v.tensor_reduce(out=key_n[:, :], in_=key_sq[:, :, :], axis=X, op=ALU.add))
                dve.wait_ge(setup_key, 2)
                for hd in range(2):
                    for s in range(2):
                        k = 2 * hd + s
                        last = v.tensor_scalar(key_z[:, k, HALF * k:HALF * (k + 1)], key_in[:, s, :], key_n[:, s:s + 1], None, ALU.mult)
                link(last)
                dve.wait_ge(setup_act, 3)
                for wt, mean in ((fwqT[:, :], fmean[:, :]), (fbq_row, bmean[:, :])):
                    w3 = wt.rearrange("p (h q) -> p h q", h=H)
                    link(v.tensor_reduce(out=mean, in_=w3, axis=X, op=ALU.add))
                    link(v.tensor_scalar(mean, mean, 1.0 / QD, None, ALU.mult))
                    link(v.tensor_tensor(w3, w3, mean.unsqueeze(2).to_broadcast([w3.shape[0], H, QD]), ALU.subtract))
                dve.wait_ge(setup_act, 4)
                dve.wait_ge(setup_pool, 3)
                for q in range(TG):
                    last = v.tensor_copy(down_x[:, q, :, q:128:TG], downT[:, :].rearrange("p (h l) -> p l h", l=EL))
                link(last)
                dve.wait_ge(setup_pool, 6)
                p1_wsq(0)
                p1_tscale(0)
                p1_stats(0, 0, 0)
                p1_shift(0, 0)
                for t in range(3):
                    p1_smax(0, t)
                    p1_rden(0, t)
                p1_res(0)
                p1_stats(1, 0, 0)
                p1_shift(1, 0)
                p1_stats(2, 0, 0)
                p1_shift(2, 0)
                q_norms(0)

            def p1_wsq(b):
                dve.wait_ge(conv_done, b + 1)
                wait(dve, wnorm_ready, b)
                v.tensor_scalar(wsq[:, :], bankB[0:NT, 3 * D:3 * D + 3], 0.0, None, ALU.max).then_inc(wsq_ready, 1)

            def p1_tscale(b):
                link = linker(dve, tscale_ready, 5, b)
                dve.wait_ge(wnorm_ready, b + 1)
                wait(dve, tanh_done, b)
                link(v.tensor_scalar(small[:, :], wnorm[:, :], 1.0, None, ALU.is_lt))
                link(v.tensor_scalar(wden[:, :], wnorm[:, :], 1.0e-7, None, ALU.add))
                link(v.reciprocal(wden[:, :], wden[:, :]))
                link(v.scalar_tensor_tensor(out=tscale[:, :], in0=wden[:, :], scalar=1.0, in1=small[:, :], op0=ALU.min, op1=ALU.max))
                link(v.tensor_scalar(tscale[:, :], tscale[:, :], 1.0 / (1.0 + 1.0e-7), None, ALU.mult), wait=False)

            def p1_stats(i, j, par):
                b = 2 * j + par
                link = linker(dve, ln_stats[i], 3, b)
                src = (h0, res, h[par])[i]
                if i == 0:
                    dve.wait_ge(h0_ready, 2 * (b + 1))
                elif i == 1:
                    dve.wait_ge(res_ready, b + 1)
                else:
                    dve.wait_ge(h_ready, 3 * (b + 1))
                wait(dve, ln_rstd[i], b)
                for t in range(3):
                    last = v.bn_stats(out=bns[i][:, t, :], in_=src[:, t, :])
                link(last)
                settled(dve, passed_dve)
                for t in range(3):
                    last = v.bn_aggr(out=bna[i][:, t, :], in_=bns[i][:, t, :])
                link(last)
                link(v.tensor_scalar(lnv[i][:, :], bna[i][:, :, 1], 1.0e-5, None, ALU.add), wait=False)

            def p1_shift(i, b):
                dve.wait_ge(ln_rstd[i], b + 1)
                wait(dve, (xl_ready, xh_ready, hn_ready)[i], b)
                v.scalar_tensor_tensor(out=lnm[i][:, :], in0=bna[i][:, :, 0], scalar=-1.0, in1=lnr[i][:, :],
                                       op0=ALU.mult, op1=ALU.mult).then_inc(ln_shift[i], 1)

            def p1_smax(b, t):
                n = 3 * b + t
                link = linker(dve, smax_ready, 2, n)
                dve.wait_ge(attn_scored, n + 1)
                wait(dve, probs_ready, n)
                lo2 = band(t, 2)[0]
                settled(dve, passed_dve)
                for w in range(3):
                    lo, hi = band(t, w)
                    last = v.tensor_tensor_reduce(out=masked[w][:, 0:hi - lo], in0=bankA[0:NT, lo - lo2:hi - lo2], in1=masks[t, w][:, :],
                                                  scale=1.0, scalar=-3.0e38, op0=ALU.add, op1=ALU.max, accum_out=smax[:, w:w + 1])
                link(last)
                link(v.tensor_scalar(sbias[:, :], smax[:, :], -SCORE_SCALE, None, ALU.mult), wait=False)

            def p1_rden(b, t):
                n = 3 * b + t
                dve.wait_ge(probs_ready, n + 1)
                wait(dve, diag_ready, n)
                v.reciprocal(rden[:, :], den[:, :]).then_inc(rden_ready, 1)

            def p1_res(b):
                dve.wait_ge(wo_done, 3 * (b + 1))
                dve.wait_ge(xb_ready, b + 1)
                wait(dve, xh_ready, b)
                v.tensor_tensor(res[:, :, :].rearrange("p t d -> p (t d)"), bankC[0:NT, D:4 * D],
                                xb[:, :, :].rearrange("p t d -> p (t d)"), ALU.add).then_inc(res_ready, 1)

            def q_norms(n):
                dve.wait_ge(qn_affine, 3 * (n + 1))
                wait(dve, qn_ready, 3 * n)
                v.tensor_reduce(out=nss[:, :], in_=qsq[:, :, :], axis=X, op=ALU.add).then_inc(nss_ready, 1)

            def rank(n, slot, quarter):
                heads = [(hd, s) for hd in (2 * quarter, 2 * quarter + 1) for s in range(2)]
                base = 16 * n + 4 * quarter
                src = scores[slot]
                if quarter == 0:
                    dve.wait_ge(scores_ready, n + 1)
                    wait(dve, cells_ready, 2 * n)
                    wait(dve, idxf_ready, n)
                settled(dve, passed_dve)
                for hd, s in heads:
                    last = v.max(out=val[:, hd, s, 0:8], in_=src[:, hd, s, :])
                last.then_inc(ranked, 1)
                dve.wait_ge(ranked, base + 1)
                settled(dve, passed_dve)
                for hd, s in heads:
                    v.max_index(out=idx[:, hd, s, 0:8], in_max=val[:, hd, s, 0:8], in_values=src[:, hd, s, :])
                for hd, s in heads:
                    last = v.match_replace(out=src[:, hd, s, :], in_to_replace=val[:, hd, s, 0:8], in_values=src[:, hd, s, :], imm_value=NEG)
                last.then_inc(ranked, 1)
                dve.wait_ge(ranked, base + 2)
                settled(dve, passed_dve)
                for hd, s in heads:
                    last = v.max(out=val[:, hd, s, 8:16], in_=src[:, hd, s, :])
                last.then_inc(ranked, 1)
                dve.wait_ge(ranked, base + 3)
                settled(dve, passed_dve)
                for hd, s in heads:
                    last = v.max_index(out=idx[:, hd, s, 8:16], in_max=val[:, hd, s, 8:16], in_values=src[:, hd, s, :])
                last.then_inc(ranked, 1)

            def digits(m):
                link = linker(dve, digits_ready, 2, m)
                dve.wait_ge(merge_done, m + 1)
                dve.wait_ge(wm_ready, m + 1)
                wait(dve, onehigh_ready, 4 * m)
                wait(dve, wl_ready, 2 * m)
                experts = merged[:, :, 2 * NT:3 * NT]
                link(v.tensor_scalar(eh[:, :, :], experts, -(EL - 1) / 2.0, 1.0 / EL, ALU.add, ALU.mult))
                link(v.scalar_tensor_tensor(out=el[:, :, :], in0=eh[:, :, :], scalar=-float(EL), in1=experts, op0=ALU.mult, op1=ALU.add))

            def low_weights(m):
                link = linker(dve, wl_ready, 2, m)
                wait(dve, scattered, m)
                for l in range(EL):
                    last = v.tensor_scalar(ol[:, :, l, :], el[:, :, :], float(l), None, ALU.is_equal)
                link(last)
                for k in range(2):
                    last = v.tensor_tensor(wl[:, :, k, :, :], wm[:, k, :, :].unsqueeze(2).to_broadcast([128, 2, EL, NT]),
                                           ol[:, k, :, :].unsqueeze(1).to_broadcast([128, 2, EL, NT]), ALU.mult)
                link(last, wait=False)

            def product(m, par, t):
                dve.wait_ge(scattered, m + 1)
                dve.wait_ge(gelu_done, m + 1)
                wait(dve, ffn_done, m)
                v.tensor_tensor(prod[:, :, :].rearrange("p l (g t) -> p g l t", t=TG), coef, act_g[par][:, t, :, :, :], ALU.mult)\
                 .then_inc(prod_ready, 1)

            def finish(m, b, par, t):
                dve.wait_ge(ffn_done, m + 1)
                wait(dve, stored[t], 16 * b)
                v.scalar_tensor_tensor(out=o_sb[:, t, :], in0=ffn, scalar=1.0 / WSCALE, in1=h[par][:, t, :], op0=ALU.mult, op1=ALU.add)\
                 .then_inc(out_ready, 1)

            def choose(n):
                link = linker(dve, chosen, 8, n)
                dve.wait_ge(cells_ready, 2 * n + 1)
                settled(dve, passed_dve)
                for hd in range(H):
                    last = v.max(out=best[:, hd, 0:8], in_=cs[:, hd, :])
                link(last)
                settled(dve, passed_dve)
                for hd in range(H):
                    last = v.match_replace(out=cr[:, hd, :], in_to_replace=best[:, hd, 0:8], in_values=cs[:, hd, :], imm_value=NEG)
                link(last)
                settled(dve, passed_dve)
                for hd in range(H):
                    last = v.max(out=best[:, hd, 8:16], in_=cr[:, hd, :])
                link(last)
                settled(dve, passed_dve)
                for hd in range(H):
                    last = v.match_replace(out=cr[:, hd, :], in_to_replace=best[:, hd, 8:16], in_values=cr[:, hd, :], imm_value=NEG)
                link(last)
                dve.wait_ge(exp_ready, n + 1)
                wait(dve, weights, 2 * n)
                link(v.scalar_tensor_tensor(out=wsel[:, :, :], in0=cr[:, :, :], scalar=NEG / 2, in1=cx[:, :, :], op0=ALU.is_lt, op1=ALU.mult))
                link(v.tensor_reduce(out=wsum[:, :], in_=wsel[:, :, :], axis=X, op=ALU.add))
                dve.wait_ge(cells_ready, 2 * n + 2)
                wait(dve, cells_turned, n)
                v.scalar_tensor_tensor(out=wcell[:, 2, :, :], in0=cr[:, :, :], scalar=NEG / 2, in1=ce[:, :, :], op0=ALU.is_lt, op1=ALU.mult)
                link(v.tensor_scalar(wsum2[:, :], wsum[:, :], 1.0 / WSCALE, None, ALU.mult))
                link(v.reciprocal(wrec[:, :], wsum2[:, :]), wait=False)

            def body(j, par, first=False, final=False):
                b = 2 * j + par
                nj, npar = following(j, par)
                attend = not final
                for t in range(3):
                    n = 3 * b + t
                    slot = (par + t) % 2
                    back = not (first and t == 0)
                    mb, mpar, mt = (b - 1, 1 - par, 2) if t == 0 else (b, par, t - 1)
                    if attend and t == 0:
                        p1_wsq(b + 1)
                    if attend and t == 1:
                        p1_rden(b + 1, 1)
                    rank(n, slot, 0)
                    if back:
                        digits(n - 1)
                    if attend and t == 0:
                        p1_tscale(b + 1)
                    if attend and t == 1:
                        p1_smax(b + 1, 2)
                    if attend and t == 2:
                        p1_shift(2, b + 1)
                    rank(n, slot, 1)
                    if attend and t == 0:
                        p1_stats(0, nj, npar)
                    if attend and t == 1:
                        p1_rden(b + 1, 2)
                    if t < 2:
                        q_norms(n + 1)
                    if back:
                        low_weights(n - 1)
                    if attend and t == 0:
                        p1_shift(0, b + 1)
                    rank(n, slot, 2)
                    if attend and t == 0:
                        p1_smax(b + 1, 0)
                    if attend and t == 1:
                        p1_res(b + 1)
                        p1_stats(1, nj, npar)
                    rank(n, slot, 3)
                    if attend and t == 0:
                        p1_rden(b + 1, 0)
                    if attend and t == 1:
                        p1_shift(1, b + 1)
                    if attend and t == 2:
                        q_norms(n + 1)
                    if back:
                        product(n - 1, mpar, mt)
                    if attend and t == 0:
                        p1_smax(b + 1, 1)
                    choose(n)
                    if back:
                        finish(n - 1, mb, mpar, mt)
                    if attend and t == 1:
                        p1_stats(2, nj, npar)

            def end():
                m = 3 * B - 1
                digits(m)
                low_weights(m)
                product(m, 1, 2)
                finish(m, B - 1, 1, 2)

            run(dve, start, body, end)


_INS = ["x", "L0_tok_kernel", "L0_tok_bias", "L0_attn_Wq", "L0_attn_bq", "L0_attn_Wk", "L0_attn_bk", "L0_attn_Wo", "L0_attn_bo",
        "L0_attn_gamma", "L0_attn_beta", "L0_ffn_Wq", "L0_ffn_bq", "L0_ffn_ln_g", "L0_ffn_ln_b", "L0_ffn_keys0", "L0_ffn_keys1",
        "L0_ffn_expert_down", "L0_ffn_expert_up"]


def kernel(**inputs):
    import concourse.bacc as bacc
    from concourse.bass_utils import run_bass_kernel_spmd
    nc = bacc.Bacc("TRN2", target_bir_lowering=False, num_devices=1)
    arrays, args = {}, []
    given = [(name, np.ascontiguousarray(inputs[name])) for name in _INS]
    given += [("merge", merge_matrix()), ("identity", np.eye(128, dtype=np.float32))]
    for name, a in given:
        arrays[f"in_{name}"] = a
        args.append(nc.dram_tensor(f"in_{name}", a.shape, mybir.dt.from_np(a.dtype), kind="ExternalInput").ap())
    out = nc.dram_tensor("out_0", (B, T, D), mybir.dt.float32, kind="ExternalOutput").ap()
    build(nc, *args, out)
    r = run_bass_kernel_spmd(nc, [arrays], core_ids=[0])
    return r.results[0]["out_0"]
```

```python
import numpy as np
import concourse.bass as bass
from concourse import mybir
from concourse.alu_op_type import AluOpType as ALU
from contextlib import ExitStack

B, L, C = 16, 375, 64
TAPS, D = 9, 128
T = L - TAPS + 1
NT = 124
OFF = [0, 122, T - NT]
FIRST = [0, 2, OFF[1] + NT - OFF[2]]
KEYS = [OFF[1], OFF[2] - OFF[1], NT]
RADII = [24 // 2, 168 // 2, 180 // 2]
XT = L // 3
H, QD, HALF, PK, TOP = 8, 64, 32, 64, 16
CELLS = [(a, c) for a in range(TOP) for c in range(TOP) if (a + 1) * (c + 1) <= TOP]
NC = len(CELLS)
PAIRS = H // 2
SLOTS = 32
EH, EL, TG = 32, 4, 4
NG = NT // TG
WSCALE = 4096.0
NEG = -1.0e30
BEFORE, PEELED, AFTER = -2, 4, B + 2
SCORE_SCALE = 1.0 / float(np.sqrt(np.float32(D)))


def merge_matrix():
    def together(p, q):
        (a, c), (e, g) = p, q
        return (a + 1) * (c + 1) + (e + 1) * (g + 1) - (min(a, e) + 1) * (min(c, g) + 1) <= TOP
    slots = [[(0, c)] for c in range(TOP)] + [[] for _ in range(SLOTS - TOP)]
    rest = sorted((p for p in CELLS if p[0]), key=lambda p: -(p[0] + 1) * (p[1] + 1) + 0.01 * p[0])
    moves = {(a, 0): a for a in range(8, 16)}
    moves.update({(1, 4): 12, (1, 5): 13, (1, 6): 14, (1, 7): 15, (2, 3): 10, (2, 4): 11,
                  (3, 2): 8, (3, 3): 9, (5, 1): 6, (6, 1): 7})
    free = iter(range(TOP, SLOTS))
    for p in rest:
        slots[moves[p] if p in moves else next(free)].append(p)
    m = np.zeros((2 * NC, 2 * SLOTS), np.float16)
    for s, cells in enumerate(slots):
        assert not any(together(p, q) for i, p in enumerate(cells) for q in cells[:i])
        for p in cells:
            for h in range(2):
                m[h * NC + CELLS.index(p), h * SLOTS + s] = 1
    assert m.sum() == 2 * NC
    return m


def band(t, w):
    return max(0, OFF[t] - RADII[w]), min(T, OFF[t] + NT + RADII[w])


def chunks(t, w):
    lo, hi = band(t, w)
    return [c for c in range(3) if lo < OFF[c] + KEYS[c] and hi > OFF[c]]


def build(nc, x, tok_kernel, tok_bias, wq, bq, wk, bk, wo, bo, gamma, beta, fwq, fbq, lng, lnb,
          keys0, keys1, down, up, merge, ident, own, out):
    f32, f16, bf16, i16, u16 = mybir.dt.float32, mybir.dt.float16, mybir.dt.bfloat16, mybir.dt.int16, mybir.dt.uint16
    ACT = mybir.ActivationFunctionType
    X = mybir.AxisListType.X
    ctx = ExitStack()
    with ctx:
        def sb(name, shape, dt=f32):
            return ctx.enter_context(nc.sbuf_tensor(name, shape, dt))

        def sem(name):
            return ctx.enter_context(nc.semaphore(name))

        def col(v):
            return v.rearrange("(p a) -> p a", a=1)

        def row(v):
            return v.rearrange("(a p) -> a p", a=1)

        id32 = sb("id32", [128, 128])
        id16 = sb("id16", [128, 128], f16)
        merge_sb = sb("merge_sb", [2 * NC, 2 * SLOTS], f16)
        own_sb = sb("own_sb", [128, TG])
        ones = sb("ones", [128, 128])
        ones3 = sb("ones3", [3, NT], bf16)
        third = sb("third", [128, 1])
        digit_bias = sb("digit_bias", [128, 1])
        power = sb("power", [128, 48])
        conv_w = sb("conv_w", [128, 5, D])
        wq_sb, wk_sb, wo_sb = sb("wq_sb", [D, D]), sb("wk_sb", [D, D]), sb("wo_sb", [D, D])
        bq_sb, bk_sb = sb("bq_sb", [D, 1]), sb("bk_sb", [D, 1])
        rows = sb("rows", [1, 4 * D + 2 * QD + H * QD])
        vecs = sb("vecs", [128, 4 * D + 2 * QD])
        tokb, bob, gam, bet = (vecs[0:NT, i * D:(i + 1) * D] for i in range(4))
        lng_bc = vecs[0:NT, 4 * D:4 * D + QD]
        lnb_bc = vecs[0:NT, 4 * D + QD:4 * D + 2 * QD]
        fbq_row = rows[0:1, 4 * D + 2 * QD:4 * D + 2 * QD + H * QD]
        fwq_in = sb("fwq_in", [128, 4, D])
        fwqT = sb("fwqT", [D, H * QD])
        fbq3 = sb("fbq3", [3, H * QD], bf16)
        fbq_part = sb("fbq_part", [1, 2, H * QD], bf16)
        fbq_rest = sb("fbq_rest", [1, 2, H * QD])
        fmean = sb("fmean", [D, H])
        bmean = sb("bmean", [1, H])
        key_in = sb("key_in", [PK, 2, HALF])
        key_sq = sb("key_sq", [PK, 2, HALF])
        key_n = sb("key_n", [PK, 2])
        key_z = sb("key_z", [PK, 4, 128])
        key_bd = sb("key_bd", [128, 4 * PK])
        down_in = sb("down_in", [128, D])
        downT = sb("downT", [D, 128])
        down_x = sb("down_x", [D, EL, EH, TG])
        up_x = sb("up_x", [128, EL, D])
        masks = {}
        for t in range(3):
            for w in range(3):
                lo, hi = band(t, w)
                masks[t, w] = sb(f"mask{t}{w}", [NT, hi - lo])

        x_in = [sb(f"x_in{p}", [XT, 3, 2, C]) for p in range(2)]
        xT = sb("xT", [128, L])
        xT_sq = sb("xT_sq", [128, L])
        sq_pairs = sb("sq_pairs", [128, L - 2])
        sq_win = sb("sq_win", [128, T])
        convT = sb("convT", [D, T])
        wsq = sb("wsq", [NT, 3])
        wnorm = sb("wnorm", [NT, 3])
        small = sb("small", [NT, 3])
        wden = sb("wden", [NT, 3])
        tscale = sb("tscale", [NT, 3])
        th = sb("th", [NT, 3, D])
        h0 = sb("h0", [NT, 3, D])
        bns = [sb(f"bns{i}", [NT, 3, 6]) for i in range(3)]
        bna = [sb(f"bna{i}", [NT, 3, 2]) for i in range(3)]
        lnv = [sb(f"lnv{i}", [NT, 3]) for i in range(3)]
        lnr = [sb(f"lnr{i}", [NT, 3]) for i in range(3)]
        lnm = [sb(f"lnm{i}", [NT, 3]) for i in range(3)]
        xl = sb("xl", [NT, 3, D])
        xb = sb("xb", [NT, 3, D])
        xlT = sb("xlT", [D, T])
        qT, kT = sb("qT", [D, T]), sb("kT", [D, T])
        masked = [sb(f"masked{w}", [NT, NT + 2 * RADII[w]]) for w in range(3)]
        smax = sb("smax", [NT, 3])
        sbias = sb("sbias", [NT, 3])
        probs = [sb(f"probs{w}", [NT, NT + 2 * RADII[w]]) for w in range(3)]
        mixed = [sb(f"mixed{t}", [NT, T]) for t in range(3)]
        den = sb("den", [NT, 3])
        rden = sb("rden", [NT, 3])
        attnT = sb("attnT", [NT, 3 * NT])
        axT = sb("axT", [D, NT])
        res = sb("res", [NT, 3, D])
        xh = sb("xh", [NT, 3, D])
        h = [sb(f"hsum{p}", [NT, 3, D]) for p in range(2)]
        hn = sb("hn", [NT, 3, D])
        hnT = [sb(f"hnT{p}", [D, 3, NT]) for p in range(2)]
        act_g = [sb(f"act_g{p}", [128, 3, NG, EL, TG]) for p in range(2)]

        sq_junk = sb("sq_junk", [NT, H, QD])
        ns_junk = sb("ns_junk", [NT, 2 * H, HALF])
        qss = sb("qss", [NT, H])
        qvar = sb("qvar", [NT, H])
        qrstd = sb("qrstd", [NT, H])
        qn = sb("qn", [NT, H, QD])
        nss = sb("nss", [NT, 2 * H])
        nmx = sb("nmx", [NT, 2 * H])
        nrec = sb("nrec", [NT, 2 * H])
        qnT = sb("qnT", [128, PAIRS, NT])
        scores = [sb(f"scores{p}", [NT, H, 2, PK]) for p in range(2)]
        val = [sb(f"val{p}", [NT, H, 2, TOP]) for p in range(2)]
        idx = [sb(f"idx{p}", [NT, H, 2, TOP], u16) for p in range(2)]
        idxf = [sb(f"idxf{p}", [NT, H, 2, TOP]) for p in range(2)]
        cs = sb("cs", [NT, H, NC])
        cr = sb("cr", [NT, H, NC])
        ce = sb("ce", [NT, H, NC])
        cx = sb("cx", [NT, H, NC])
        best = sb("best", [NT, H, TOP])
        best_exp = sb("best_exp", [NT, H, TOP])
        taken = sb("taken", [NT, H, NC])
        wsel = sb("wsel", [NT, H, NC])
        wsum = sb("wsum", [NT, H])
        wsum2 = sb("wsum2", [NT, H])
        wrec = sb("wrec", [NT, H])
        wn = sb("wn", [NT, H, NC])
        wcell = sb("wcell", [NT, 3, H, NC], f16)
        wcT = sb("wcT", [2 * NC, PAIRS, 3, NT], f16)
        wm = sb("wm", [128, 2, 3, NT], f16)
        eh = sb("eh", [128, 2, NT], i16)
        el = sb("el", [128, 2, NT], i16)
        oh = sb("oh", [128, 2, NG, EH, TG], f16)
        ol = sb("ol", [128, 2, EL, NT], f16)
        wl = sb("wl", [128, 2, 2, EL, NT], f16)
        prod = sb("prod", [128, EL, NT])
        o_sb = sb("o_sb", [NT, 3, D])

        banks3 = ctx.enter_context(nc.psum_tensor("banks3", [128, 3 * 512], f32))
        bankA, bankB, bankC = (banks3[:, i * 512:(i + 1) * 512] for i in range(3))
        bankQ = ctx.enter_context(nc.psum_tensor("bankQ", [128, 512], f32))
        bankS = ctx.enter_context(nc.psum_tensor("bankS", [128, 1024], f32))
        bankM = ctx.enter_context(nc.psum_tensor("bankM", [128, 1024], f32))
        wcT_ps = bankS[0:2 * NC, :].bitcast(f16).rearrange("p (k n) -> p k n", k=2)
        merged = bankM[:, :].rearrange("p (k n) -> p k n", k=2)
        coef = bankM[:, 0:NG * EL * TG].rearrange("p (g l t) -> p g l t", g=NG, l=EL)
        ffn = bankM[0:NT, 512:512 + D]

        w_in = sem("w_in")
        setup_pool, setup_dve, setup_act, setup_pe = (sem(f"setup_{e}") for e in ("pool", "dve", "act", "pe"))
        passed_dve, passed_pool = sem("passed_dve"), sem("passed_pool")
        setup_fbq, fbq_spread = sem("setup_fbq"), sem("fbq_spread")
        setup_key = sem("setup_key")
        x_loaded = [sem(f"x_loaded{p}") for p in range(2)]
        x_turned = sem("x_turned")
        xT_ready = sem("xT_ready")
        conv_done = sem("conv_done")
        convT_ready = sem("convT_ready")
        conv_turned = sem("conv_turned")
        sq_win_ready = sem("sq_win_ready")
        wsq_done = sem("wsq_done")
        wsq_ready = sem("wsq_ready")
        wnorm_ready = sem("wnorm_ready")
        tscale_ready = sem("tscale_ready")
        tanh_done = sem("tanh_done")
        h0_ready = sem("h0_ready")
        ln_stats = [sem(f"ln_stats{i}") for i in range(3)]
        ln_rstd = [sem(f"ln_rstd{i}") for i in range(3)]
        ln_shift = [sem(f"ln_shift{i}") for i in range(3)]
        xl_ready = sem("xl_ready")
        xl_turned = sem("xl_turned")
        xlT_ready = sem("xlT_ready")
        qk_done = sem("qk_done")
        qk_ready = sem("qk_ready")
        xb_ready = sem("xb_ready")
        attn_scored = sem("attn_scored")
        smax_ready = sem("smax_ready")
        probs_ready = sem("probs_ready")
        mixed_ready = sem("mixed_ready")
        attn_turned = sem("attn_turned")
        attnT_ready = sem("attnT_ready")
        ax_done = sem("ax_done")
        axT_ready = sem("axT_ready")
        wo_done = sem("wo_done")
        res_ready = sem("res_ready")
        xh_ready = sem("xh_ready")
        h_ready = sem("h_ready")
        hn_ready = sem("hn_ready")
        hn_turned = sem("hn_turned")
        hnT_ready = sem("hnT_ready")
        inner_done = sem("inner_done")
        gelu_done = sem("gelu_done")
        q_done = sem("q_done")
        qss_ready = sem("qss_ready")
        qrstd_ready = sem("qrstd_ready")
        qn_scaled = sem("qn_scaled")
        qn_affine = sem("qn_affine")
        nss_ready = sem("nss_ready")
        qn_ready = sem("qn_ready")
        qn_turned = sem("qn_turned")
        qnT_ready = sem("qnT_ready")
        scored = sem("scored")
        scores_ready = sem("scores_ready")
        ranked = sem("ranked")
        idxf_ready = sem("idxf_ready")
        cells_ready = sem("cells_ready")
        exp_ready = sem("exp_ready")
        best_exp_ready = sem("best_exp_ready")
        chosen = sem("chosen")
        weights = sem("weights")
        whigh_ready = sem("whigh_ready")
        cells_turned = sem("cells_turned")
        wcT_ready = sem("wcT_ready")
        merge_done = sem("merge_done")
        wm_ready = sem("wm_ready")
        high_ready = sem("high_ready")
        digits_ready = sem("digits_ready")
        onehigh_ready = sem("onehigh_ready")
        wl_ready = sem("wl_ready")
        scattered = sem("scattered")
        prod_ready = sem("prod_ready")
        ffn_done = sem("ffn_done")
        out_ready = sem("out_ready")
        stored = [sem(f"stored{t}") for t in range(3)]

        block = ctx.enter_context(nc.Block())

        def linker(eng, s, per, call):
            count = [0]

            def link(ins, wait=True):
                count[0] += 1
                assert count[0] <= per
                ins.then_inc(s, 1)
                if wait:
                    eng.wait_ge(s, per * call + count[0])
            return link

        def wait(eng, s, value):
            if not isinstance(value, int) or value > 0:
                eng.wait_ge(s, value)

        def settled(eng, s):
            eng.sem_inc(s, 1)

        class Batch:
            def __init__(self, j, par):
                self.j, self.par, self.b = j, par, 2 * j + par
                self.exists = not isinstance(j, int) or 0 <= self.b < B

            def __add__(self, k):
                return Batch(self.j + (self.par + k) // 2, (self.par + k) % 2)

            def tile(self, t):
                return 3 * self.b + t

            def slot(self, t):
                return (self.par + t) % 2

        def do(step, c, *rest):
            if c.exists:
                step(c, *rest)

        def at_most(value, top):
            return min(value, top) if isinstance(value, int) else value

        def batch(v, b):
            one = v[b:b + 1, :, :] if isinstance(b, int) else v[bass.ds(b, 1), :, :]
            return one.rearrange("a p c -> (a p) c")

        def run(eng, start, body, end):
            start()
            for b in range(BEFORE, PEELED):
                body(Batch(b // 2, b % 2))
            with eng.Fori(PEELED // 2, B // 2 - 1) as j:
                body(Batch(j, 0))
                body(Batch(j, 1))
            for b in range(B - 2, AFTER):
                body(Batch(b // 2, b % 2))
            end()

        kern = tok_kernel[0:TAPS - 1, :, :].rearrange("(m s) c f -> s c m f", s=2)
        loads = [(id32[:, :], ident), (own_sb[:, :], own), (merge_sb[:, :], merge),
                 (rows[0:1, 0:D], row(tok_bias)), (rows[0:1, D:2 * D], row(bo)),
                 (rows[0:1, 2 * D:3 * D], row(gamma)), (rows[0:1, 3 * D:4 * D], row(beta)),
                 (rows[0:1, 4 * D:4 * D + QD], row(lng)), (rows[0:1, 4 * D + QD:4 * D + 2 * QD], row(lnb)),
                 (fbq_row, row(fbq)), (fwq_in[:, :, :], fwq.rearrange("(k p) d -> p k d", p=128)),
                 (key_in[:, 0, :], keys0), (key_in[:, 1, :], keys1), (down_in[:, :], down[0:128, :]),
                 (conv_w[0:C, 0:4, :], kern[0, :, :, :]), (conv_w[C:2 * C, 0:4, :], kern[1, :, :, :]),
                 (conv_w[0:C, 4, :], tok_kernel[TAPS - 1, :, :]),
                 (wq_sb[:, :], wq), (wk_sb[:, :], wk), (wo_sb[:, :], wo),
                 (bq_sb[:, :], col(bq)), (bk_sb[:, :], col(bk))]
        for t in range(TG):
            loads.append((up_x[t:128:TG, :, :], up[0:128, :].rearrange("(h l) o -> h l o", l=EL)))
        ALL_LOADED = 16 * len(loads)

        @block.sync
        def _(sp):
            def load_x(c):
                b = c.b
                wait(sp, x_turned, b - 1)
                x_b, slot = batch(x, b), x_in[c.par]
                sp.dma_start(slot[:, :, 0, :], x_b[0:L, :].rearrange("(t p) c -> p t c", t=3)).then_inc(x_loaded[c.par], 16)
                sp.dma_start(slot[:, 0:2, 1, :], x_b[1:1 + 2 * XT, :].rearrange("(t p) c -> p t c", t=2)).then_inc(x_loaded[c.par], 16)
                sp.dma_start(slot[0:XT - 1, 2, 1, :], x_b[1 + 2 * XT:L, :]).then_inc(x_loaded[c.par], 16)

            def store(c, t):
                b = c.b
                sp.wait_ge(out_ready, 3 * b + t + 1)
                f = FIRST[t]
                sp.dma_start(batch(out, b)[OFF[t] + f:OFF[t] + NT, :], o_sb[f:NT, t, :]).then_inc(stored[t], 16)

            def start():
                for dst, src in loads:
                    sp.dma_start(dst, src).then_inc(w_in, 16)
                sp.wait_ge(setup_pool, 1)
                sp.wait_ge(setup_fbq, 5)
                for k in range(2):
                    sp.dma_start(fbq3[1 + k:2 + k, :], fbq_part[0:1, k, :]).then_inc(fbq_spread, 16)

            def body(c):
                do(store, c + -1, 1)
                do(load_x, c + 2)
                do(store, c + -1, 2)
                do(store, c, 0)

            def end():
                for t in range(3):
                    sp.wait_ge(stored[t], 16 * B)

            run(sp, start, body, end)

        @block.gpsimd
        def _(pool):
            g = nc.gpsimd

            def start():
                for p in range(2):
                    last = g.memset(x_in[p][:, 2, 1, :], 0.0)
                last.then_inc(setup_pool, 1)
                g.memset(ones[:, :], 1.0)
                g.memset(power[:, 0:45], -0.5)
                g.memset(power[:, 45:48], 0.5)
                g.memset(key_z[:, :, :], 0.0).then_inc(setup_pool, 1)
                pool.wait_ge(setup_dve, 2)
                link = linker(pool, setup_key, 2, 0)
                link(g.tensor_scalar(key_n[:, :], key_n[:, :], 1.0e-24, None, ALU.max))
                link(g.tensor_tensor(key_n[:, :], key_n[:, :], power[0:PK, 0:2], ALU.pow))
                g.memset(ones3[:, :], 1.0)
                g.memset(third[:, :], 1.0 / 3.0)
                g.memset(digit_bias[:, :], -(EL - 1) / 2.0 / EL).then_inc(setup_pool, 1)
                for t in range(3):
                    g.memset(mixed[t][:, :], 0.0)
                    for w in range(3):
                        g.memset(masks[t, w][:, :], 0.0)
                g.memset(small[:, :], 0.0).then_inc(setup_pool, 1)
                pool.wait_ge(setup_pool, 4)
                for t in range(3):
                    for w in range(3):
                        lo, hi = band(t, w)
                        g.affine_select(out=masks[t, w][:, :], in_=masks[t, w][:, :], compare_op=ALU.is_ge, fill=NEG,
                                        base=lo - OFF[t] + RADII[w], pattern=[[1, hi - lo]], channel_multiplier=-1)
                g.memset(small[:, :], 0.0).then_inc(setup_pool, 1)
                pool.wait_ge(setup_pool, 5)
                for t in range(3):
                    for w in range(3):
                        lo, hi = band(t, w)
                        last = g.affine_select(out=masks[t, w][:, :], in_=masks[t, w][:, :], compare_op=ALU.is_ge, fill=NEG,
                                               base=OFF[t] - lo + RADII[w], pattern=[[-1, hi - lo]], channel_multiplier=1)
                last.then_inc(setup_pool, 1)
                pool.wait_ge(setup_act, 2)

            def p1_windows(c):
                b = c.b
                link = linker(pool, sq_win_ready, 3, b)
                pool.wait_ge(xT_ready, 2 * (b + 1))
                wait(pool, wsq_done, b)
                link(g.tensor_tensor(sq_pairs[:, :], xT_sq[:, 0:L - 2], xT_sq[:, 2:L], ALU.add))
                link(g.tensor_tensor(sq_win[:, :], sq_pairs[:, 0:T], sq_pairs[:, 4:T + 4], ALU.add))
                link(g.tensor_tensor(sq_win[0:C, :], sq_win[0:C, :], xT_sq[0:C, 8:T + 8], ALU.add), wait=False)

            def p1_norm(c):
                b = c.b
                pool.wait_ge(wsq_ready, b + 1)
                wait(pool, tscale_ready, 5 * b)
                g.tensor_tensor(wnorm[:, :], wsq[:, :], power[0:NT, 45:48], ALU.pow).then_inc(wnorm_ready, 1)

            def p1_h0(c):
                b = c.b
                link = linker(pool, h0_ready, 2, b)
                pool.wait_ge(tanh_done, b + 1)
                wait(pool, h_ready, 3 * b)
                link(g.tensor_tensor(h0[:, :, :], th[:, :, :], tokb.unsqueeze(1).to_broadcast([NT, 3, D]), ALU.add))
                settled(pool, passed_pool)
                link(g.tensor_scalar(h0[:, :, :], h0[:, :, :], 0.0, None, ALU.max))

            def p1_rstd(c, i):
                b = c.b
                pool.wait_ge(ln_stats[i], 3 * (b + 1))
                wait(pool, ln_shift[i], b)
                wait(pool, (xl_ready, xh_ready, hn_ready)[i], b)
                g.tensor_tensor(lnr[i][:, :], lnv[i][:, :], power[0:NT, 0:3], ALU.pow).then_inc(ln_rstd[i], 1)

            def p1_xb(c):
                b = c.b
                pool.wait_ge(xl_ready, b + 1)
                wait(pool, res_ready, b)
                g.tensor_tensor(xb[:, :, :], xl[:, :, :], bob.unsqueeze(1).to_broadcast([NT, 3, D]), ALU.add).then_inc(xb_ready, 1)

            def p1_h(c):
                b = c.b
                link = linker(pool, h_ready, 3, b)
                pool.wait_ge(xh_ready, b + 1)
                wait(pool, out_ready, 3 * (b - 1))
                link(g.tensor_tensor(h[c.par][:, :, :], xh[:, :, :], gam.unsqueeze(1).to_broadcast([NT, 3, D]), ALU.mult))
                link(g.tensor_tensor(h[c.par][:, :, :], h[c.par][:, :, :], bet.unsqueeze(1).to_broadcast([NT, 3, D]), ALU.add))
                link(g.tensor_tensor(h[c.par][:, :, :], h[c.par][:, :, :], h0[:, :, :], ALU.add), wait=False)

            def q_rstd(c, t):
                n = c.tile(t)
                link = linker(pool, qrstd_ready, 2, n)
                pool.wait_ge(qss_ready, n + 1)
                wait(pool, qn_scaled, n)
                settled(pool, passed_pool)
                link(g.tensor_scalar(qvar[:, :], qss[:, :], 1.0 / QD, 1.0e-5, ALU.mult, ALU.add))
                link(g.tensor_tensor(qrstd[:, :], qvar[:, :], power[0:NT, 0:H], ALU.pow), wait=False)

            def q_affine(c, t):
                n = c.tile(t)
                link = linker(pool, qn_affine, 2, n)
                pool.wait_ge(qn_scaled, n + 1)
                link(g.tensor_tensor(qn[:, :, :], qn[:, :, :], lng_bc.unsqueeze(1).to_broadcast([NT, H, QD]), ALU.mult))
                link(g.tensor_tensor(qn[:, :, :], qn[:, :, :], lnb_bc.unsqueeze(1).to_broadcast([NT, H, QD]), ALU.add), wait=False)

            def q_unit(c, t):
                n = c.tile(t)
                link = linker(pool, qn_ready, 3, n)
                pool.wait_ge(nss_ready, n + 1)
                settled(pool, passed_pool)
                link(g.tensor_scalar(nmx[:, :], nss[:, :], 1.0e-24, None, ALU.max))
                link(g.tensor_tensor(nrec[:, :], nmx[:, :], power[0:NT, 0:2 * H], ALU.pow))
                q2 = qn[:, :, :].rearrange("p h (s q) -> p (h s) q", s=2)
                link(g.tensor_tensor(q2, q2, nrec[:, :].unsqueeze(2).to_broadcast([NT, 2 * H, HALF]), ALU.mult), wait=False)

            def rank_sums(c, t, part):
                n = c.tile(t)
                first, end = ((0, H // 2), (H // 2, H), (0, H))[part]
                k = end - first
                src, dst = (idxf[c.slot(t)], ce) if part == 2 else (val[c.slot(t)], cs)
                if part == 0:
                    pool.wait_ge(ranked, 16 * n + 6)
                    wait(pool, chosen, 12 * n - 8)
                    wait(pool, exp_ready, n)
                elif part == 1:
                    pool.wait_ge(ranked, 16 * n + 14)
                else:
                    pool.wait_ge(idxf_ready, n + 1)
                src, dst = src[:, first:end, :, :], dst[:, first:end, :]
                at = 0
                for a in range(5):
                    m = TOP // (a + 1)
                    g.tensor_tensor(dst[:, :, at:at + m], src[:, :, 0, a:a + 1].to_broadcast([NT, k, m]), src[:, :, 1, 0:m], ALU.add)
                    at += m
                g.tensor_tensor(dst[:, :, at:at + 6].rearrange("p h (a c) -> p h a c", c=2),
                                src[:, :, 0, 5:8].unsqueeze(3).to_broadcast([NT, k, 3, 2]),
                                src[:, :, 1, 0:2].unsqueeze(2).to_broadcast([NT, k, 3, 2]), ALU.add)
                at += 6
                g.tensor_tensor(dst[:, :, at:at + 8], src[:, :, 0, 8:16], src[:, :, 1, 0:1].to_broadcast([NT, k, 8]), ALU.add)\
                 .then_inc(cells_ready, 1)
                assert at + 8 == NC

            def select(c, t):
                n = c.tile(t)
                pool.wait_ge(cells_ready, 3 * (n + 1))
                pool.wait_ge(chosen, 12 * n + 9)
                wait(pool, cells_turned, n)
                g.tensor_tensor(wcell[:, 2, :, :], taken[:, :, :], ce[:, :, :], ALU.mult).then_inc(weights, 1)
                pool.wait_ge(exp_ready, n + 1)
                g.tensor_tensor(wsel[:, :, :], taken[:, :, :], cx[:, :, :], ALU.mult).then_inc(weights, 1)

            def normalise(c, t):
                n = c.tile(t)
                pool.wait_ge(weights, 4 * n + 2)
                pool.wait_ge(chosen, 12 * (n + 1))
                g.tensor_tensor(wn[:, :, :], wsel[:, :, :], wrec[:, :].unsqueeze(2).to_broadcast([NT, H, NC]), ALU.mult).then_inc(weights, 1)
                pool.wait_ge(whigh_ready, n + 1)
                pool.wait_ge(weights, 4 * n + 3)
                g.tensor_tensor(wcell[:, 1, :, :], wn[:, :, :], wcell[:, 0, :, :], ALU.subtract).then_inc(weights, 1)

            def body(c):
                do(p1_rstd, c, 1)
                do(p1_h, c)
                do(rank_sums, c + -1, 1, 0)
                do(p1_rstd, c, 2)
                do(rank_sums, c + -1, 1, 1)
                do(rank_sums, c + -1, 1, 2)
                do(q_rstd, c, 0)
                do(select, c + -1, 1)
                do(normalise, c + -1, 1)
                do(q_affine, c, 0)
                do(p1_windows, c + 1)
                do(q_unit, c, 0)
                do(p1_norm, c + 1)
                do(rank_sums, c + -1, 2, 0)
                do(rank_sums, c + -1, 2, 1)
                do(p1_h0, c + 1)
                do(rank_sums, c + -1, 2, 2)
                do(p1_rstd, c + 1, 0)
                do(q_rstd, c, 1)
                do(select, c + -1, 2)
                do(q_affine, c, 1)
                do(normalise, c + -1, 2)
                do(rank_sums, c, 0, 0)
                do(rank_sums, c, 0, 1)
                do(q_unit, c, 1)
                do(p1_xb, c + 1)
                do(rank_sums, c, 0, 2)
                do(select, c, 0)
                do(normalise, c, 0)
                do(q_rstd, c, 2)
                do(q_affine, c, 2)
                do(q_unit, c, 2)

            run(pool, start, body, lambda: None)

        @block.scalar
        def _(act):
            a = nc.scalar

            def start():
                act.wait_ge(w_in, ALL_LOADED)
                a.activation(id16[:, :], id32[:, :], ACT.Copy).then_inc(setup_act, 1)
                act.wait_ge(setup_pe, 1)
                a.activation(vecs[:, 0:4 * D], bankA[:, :], ACT.Copy)
                a.activation(vecs[:, 4 * D:], bankB[:, 0:2 * QD], ACT.Copy).then_inc(setup_act, 1)
                act.wait_ge(setup_pe, 2)
                a.activation(fwqT[:, :], bankS[:, 0:H * QD], ACT.Copy).then_inc(setup_act, 1)
                act.wait_ge(setup_pe, 3)
                a.activation(downT[:, :], bankC[:, 0:128], ACT.Copy).then_inc(setup_act, 1)
                act.wait_ge(setup_pe, 4)
                a.activation(key_bd[:, :], bankQ[:, 0:4 * PK], ACT.Copy).then_inc(setup_act, 1)
                act.wait_ge(setup_pool, 4)

            def p1_xT(c):
                b = c.b
                act.wait_ge(x_turned, b + 1)
                wait(act, conv_done, b)
                wait(act, sq_win_ready, 3 * b)
                a.activation(xT[:, :], bankA[:, 0:L], ACT.Copy).then_inc(xT_ready, 1)
                a.activation(xT_sq[:, :], bankA[:, 0:L], ACT.Square).then_inc(xT_ready, 1)

            def p1_convT(c):
                b = c.b
                act.wait_ge(conv_done, b + 1)
                wait(act, conv_turned, b)
                a.activation(convT[:, :], bankB[:, 0:T], ACT.Copy).then_inc(convT_ready, 1)

            def p1_tanh(c):
                b = c.b
                act.wait_ge(conv_turned, b + 1)
                act.wait_ge(tscale_ready, 5 * (b + 1))
                wait(act, h0_ready, 2 * b)
                for t in range(3):
                    last = a.activation(th[:, t, :], bankA[0:NT, t * D:(t + 1) * D], ACT.Tanh, scale=tscale[:, t:t + 1])
                last.then_inc(tanh_done, 1)

            def p1_ln(c, i):
                b = c.b
                src, dst, done = ((h0, xl, xl_ready), (res, xh, xh_ready), (h[c.par], hn, hn_ready))[i]
                act.wait_ge(ln_shift[i], b + 1)
                if i == 0:
                    wait(act, ax_done, 3 * b)
                    wait(act, xb_ready, b)
                elif i == 1:
                    wait(act, h_ready, 3 * b)
                else:
                    wait(act, hn_turned, b)
                for t in range(3):
                    last = a.activation(dst[:, t, :], src[:, t, :], ACT.Identity, bias=lnm[i][:, t:t + 1], scale=lnr[i][:, t:t + 1])
                last.then_inc(done, 1)

            def p1_xlT(c):
                b = c.b
                act.wait_ge(xl_turned, b + 1)
                wait(act, qk_done, 2 * b)
                a.activation(xlT[:, :], bankA[:, 0:T], ACT.Copy).then_inc(xlT_ready, 1)

            def p1_qk(c):
                b = c.b
                wait(act, attn_scored, 3 * b)
                for i, (dst, src, bias) in enumerate(((qT, bankB, bq_sb), (kT, bankC, bk_sb))):
                    act.wait_ge(qk_done, 2 * b + 1 + i)
                    a.activation(dst[:, :], src[:, 0:T], ACT.Identity, bias=bias[:, 0:1]).then_inc(qk_ready, 1)

            def p1_probs(c, t):
                b, n = c.b, c.tile(t)
                act.wait_ge(smax_ready, 2 * (n + 1))
                wait(act, mixed_ready, 4 * n)
                for w in range(3):
                    lo, hi = band(t, w)
                    last = a.activation(probs[w][:, 0:hi - lo], masked[w][:, 0:hi - lo], ACT.Exp, bias=sbias[:, w:w + 1],
                                        scale=SCORE_SCALE, accum_out=den[:, w:w + 1])
                last.then_inc(probs_ready, 1)

            def p1_attnT(c, t):
                b, n = c.b, c.tile(t)
                act.wait_ge(attn_turned, n + 1)
                wait(act, ax_done, n)
                cc = chunks(t, 2)
                lo, hi = cc[0] * NT, (cc[-1] + 1) * NT
                a.activation(attnT[:, lo:hi], bankB[0:NT, lo:hi], ACT.Copy).then_inc(attnT_ready, 1)

            def p1_axT(c, t):
                b, n = c.b, c.tile(t)
                act.wait_ge(ax_done, n + 1)
                wait(act, wo_done, n)
                a.activation(axT[:, :], bankC[:, 0:NT], ACT.Identity, scale=third[:, 0:1]).then_inc(axT_ready, 1)

            def p1_hnT(c):
                b = c.b
                act.wait_ge(hn_turned, b + 1)
                wait(act, q_done, 3 * (b - 1))
                wait(act, inner_done, 2 * (b - 1))
                a.activation(hnT[c.par][:, :, :].rearrange("p t n -> p (t n)"), bankA[:, 0:3 * NT], ACT.Copy).then_inc(hnT_ready, 1)

            def p1_gelu(c, part):
                b = c.b
                wait(act, prod_ready, 3 * (b - 1))
                dst = act_g[c.par][:, :, :, :, :].rearrange("p a g l t -> p (a g) l t")
                src = banks3[:, :].rearrange("p (l n) -> p l n", l=3)[:, :, 0:3 * NT].rearrange("p l (g t) -> p g l t", t=TG)
                act.wait_ge(inner_done, 2 * b + 1 + part)
                for q in range(TG):
                    into, of = (dst[:, :, 0:3, q], src[:, :, :, q]) if part == 0 else (dst[:, :, 3, q], src[:, :, 0, q])
                    last = a.activation(into, of, ACT.Gelu, scale=own_sb[:, q:q + 1])
                last.then_inc(gelu_done, 1)

            def q_squares(c, t):
                n = c.tile(t)
                act.wait_ge(q_done, n + 1)
                wait(act, qrstd_ready, 2 * n)
                for i in range(H):
                    last = a.activation(sq_junk[:, i, :], bankQ[0:NT, i * QD:(i + 1) * QD], ACT.Square, accum_out=qss[:, i:i + 1])
                last.then_inc(qss_ready, 1)

            def q_scaled(c, t):
                n = c.tile(t)
                act.wait_ge(qrstd_ready, 2 * (n + 1))
                wait(act, qn_turned, n)
                for i in range(H):
                    last = a.activation(qn[:, i, :], bankQ[0:NT, i * QD:(i + 1) * QD], ACT.Identity, scale=qrstd[:, i:i + 1])
                last.then_inc(qn_scaled, 1)

            def q_norms(c, t):
                n = c.tile(t)
                act.wait_ge(qn_affine, 2 * (n + 1))
                wait(act, qn_ready, 3 * n)
                for i in range(2 * H):
                    last = a.activation(ns_junk[:, i, :], qn[:, i // 2, (i % 2) * HALF:(i % 2 + 1) * HALF], ACT.Square, accum_out=nss[:, i:i + 1])
                last.then_inc(nss_ready, 1)

            def q_T(c, t):
                n = c.tile(t)
                act.wait_ge(qn_turned, n + 1)
                wait(act, scored, n)
                a.activation(qnT[:, :, :].rearrange("p k n -> p (k n)"), bankQ[:, 0:PAIRS * NT], ACT.Copy).then_inc(qnT_ready, 1)

            def q_scores(c, t):
                n = c.tile(t)
                act.wait_ge(scored, n + 1)
                wait(act, ranked, 16 * (n - 1))
                a.activation(scores[c.slot(t)][:, :, :, :].rearrange("p h s e -> p (h s e)"), bankS[0:NT, :], ACT.Copy)\
                 .then_inc(scores_ready, 1)

            def index_floats(c, t):
                n = c.tile(t)
                act.wait_ge(ranked, 16 * (n + 1))
                wait(act, cells_ready, 3 * (n - 1))
                a.activation(idxf[c.slot(t)][:, :, :, :], idx[c.slot(t)][:, :, :, :], ACT.Copy).then_inc(idxf_ready, 1)

            def cell_exp(c, t):
                n = c.tile(t)
                act.wait_ge(cells_ready, 3 * n + 2)
                wait(act, weights, 4 * n)
                a.activation(cx[:, :, :], cs[:, :, :], ACT.Exp).then_inc(exp_ready, 1)

            def best_exps(c, t):
                n = c.tile(t)
                act.wait_ge(chosen, 12 * n + 6)
                a.activation(best_exp[:, :, :], best[:, :, :], ACT.Exp).then_inc(best_exp_ready, 1)

            def weight_high(c, t):
                n = c.tile(t)
                act.wait_ge(weights, 4 * n + 3)
                a.activation(wcell[:, 0, :, :], wn[:, :, :], ACT.Copy).then_inc(whigh_ready, 1)

            def cells_T(c, t):
                n = c.tile(t)
                act.wait_ge(cells_turned, n + 1)
                wait(act, merge_done, n)
                for k in range(2):
                    last = a.activation(wcT[:, 2 * k:2 * k + 2, :, :].rearrange("p a k n -> p (a k n)"),
                                        wcT_ps[:, k, 0:6 * NT], ACT.Copy)
                last.then_inc(wcT_ready, 1)

            def merged_weights(c, t):
                n = c.tile(t)
                act.wait_ge(merge_done, n + 1)
                wait(act, wl_ready, 2 * n)
                wait(act, onehigh_ready, n)
                a.activation(eh[:, :, :], merged[:, :, 2 * NT:3 * NT], ACT.Identity, bias=digit_bias[:, 0:1], scale=1.0 / EL).then_inc(high_ready, 1)
                a.activation(wm[:, :, :, :].rearrange("p k s n -> p k (s n)"), merged[:, :, 0:3 * NT], ACT.Copy).then_inc(wm_ready, 1)

            def body(c):
                do(cell_exp, c + -2, 1)
                do(q_scores, c + -2, 2)
                do(p1_hnT, c + -1)
                do(q_squares, c + -1, 0)
                do(best_exps, c + -2, 1)
                do(p1_gelu, c + -1, 0)
                do(weight_high, c + -2, 1)
                do(q_scaled, c + -1, 0)
                do(p1_gelu, c + -1, 1)
                do(cells_T, c + -2, 1)
                do(p1_xT, c)
                do(q_norms, c + -1, 0)
                do(merged_weights, c + -2, 1)
                do(index_floats, c + -2, 2)
                do(p1_convT, c)
                do(q_T, c + -1, 0)
                do(p1_tanh, c)
                do(cell_exp, c + -2, 2)
                do(q_scores, c + -1, 0)
                do(best_exps, c + -2, 2)
                do(q_squares, c + -1, 1)
                do(p1_ln, c, 0)
                do(q_scaled, c + -1, 1)
                do(p1_xlT, c)
                do(p1_qk, c)
                do(weight_high, c + -2, 2)
                do(q_norms, c + -1, 1)
                do(cells_T, c + -2, 2)
                do(p1_probs, c, 0)
                do(cell_exp, c + -1, 0)
                do(merged_weights, c + -2, 2)
                do(best_exps, c + -1, 0)
                do(index_floats, c + -1, 0)
                do(q_T, c + -1, 1)
                do(p1_attnT, c, 0)
                do(p1_axT, c, 0)
                do(p1_probs, c, 1)
                do(q_scores, c + -1, 1)
                do(weight_high, c + -1, 0)
                do(q_squares, c + -1, 2)
                do(p1_attnT, c, 1)
                do(q_scaled, c + -1, 2)
                do(p1_axT, c, 1)
                do(p1_probs, c, 2)
                do(q_norms, c + -1, 2)
                do(p1_attnT, c, 2)
                do(p1_axT, c, 2)
                do(p1_ln, c, 1)
                do(cells_T, c + -1, 0)
                do(merged_weights, c + -1, 0)
                do(q_T, c + -1, 2)
                do(index_floats, c + -1, 1)
                do(p1_ln, c, 2)

            run(act, start, body, lambda: None)

        @block.tensor
        def _(pe):
            e = nc.tensor

            def start():
                pe.wait_ge(w_in, ALL_LOADED)
                pe.wait_ge(setup_pool, 2)
                e.matmul(bankA[:, :], ones[0:1, :], rows[0:1, 0:4 * D], start=True, stop=True)
                e.matmul(bankB[:, 0:2 * QD], ones[0:1, :], rows[0:1, 4 * D:4 * D + 2 * QD], start=True, stop=True)\
                 .then_inc(setup_pe, 1)
                for k in range(4):
                    last = e.transpose(bankS[:, k * 128:(k + 1) * 128], fwq_in[:, k, :], id32[:, :])
                last.then_inc(setup_pe, 1)
                e.transpose(bankC[:, 0:128], down_in[:, :], id32[:, :]).then_inc(setup_pe, 1)
                pe.wait_ge(setup_dve, 3)
                for k in range(4):
                    last = e.transpose(bankQ[:, k * PK:(k + 1) * PK], key_z[:, k, :], id32[0:PK, 0:PK])
                last.then_inc(setup_pe, 1)
                pe.wait_ge(setup_act, 5)
                pe.wait_ge(setup_dve, 10)
                pe.wait_ge(setup_pool, 3)
                pe.wait_ge(fbq_spread, 32)

            def p1_turn_x(c):
                b = c.b
                pe.wait_ge(x_loaded[c.par], 48 * (c.j + 1))
                wait(pe, gelu_done, 2 * b)
                for t in range(3):
                    last = e.transpose(bankA[:, t * XT:(t + 1) * XT], x_in[c.par][:, t, :, :].rearrange("p s c -> p (s c)"), id32[0:XT, 0:XT])
                last.then_inc(x_turned, 1)

            def p1_conv(c):
                b = c.b
                pe.wait_ge(xT_ready, 2 * (b + 1))
                for m in range(5):
                    k = 2 * C if m < 4 else C
                    last = e.matmul(bankB[:, 0:T], conv_w[0:k, m, :], xT[0:k, 2 * m:2 * m + T], start=m == 0, stop=m == 4)
                last.then_inc(conv_done, 1)

            def p1_sum_sq(c):
                b = c.b
                pe.wait_ge(sq_win_ready, 3 * (b + 1))
                for t in range(3):
                    last = e.matmul(bankC[0:NT, t:t + 1], sq_win[:, OFF[t]:OFF[t] + NT], ones[:, 0:1], start=True, stop=True)
                last.then_inc(wsq_done, 1)

            def p1_turn_conv(c):
                b = c.b
                pe.wait_ge(convT_ready, b + 1)
                for t in range(3):
                    last = e.transpose(bankA[0:NT, t * D:(t + 1) * D], convT[:, OFF[t]:OFF[t] + NT], id32[:, :])
                last.then_inc(conv_turned, 1)

            def p1_turn_xl(c):
                b = c.b
                pe.wait_ge(xl_ready, b + 1)
                for t in range(3):
                    last = e.transpose(bankA[:, OFF[t]:OFF[t] + NT], xl[:, t, :], id32[0:NT, 0:NT])
                last.then_inc(xl_turned, 1)

            def p1_project(c):
                b = c.b
                pe.wait_ge(xlT_ready, b + 1)
                e.matmul(bankB[:, 0:T], wq_sb[:, :], xlT[:, :], start=True, stop=True).then_inc(qk_done, 1)
                e.matmul(bankC[:, 0:T], wk_sb[:, :], xlT[:, :], start=True, stop=True).then_inc(qk_done, 1)

            def p1_scores(c, t):
                b, n = c.b, c.tile(t)
                pe.wait_ge(qk_ready, 2 * (b + 1))
                if t:
                    pe.wait_ge(smax_ready, 2 * n)
                lo, hi = band(t, 2)
                e.matmul(bankA[0:NT, 0:hi - lo], qT[:, OFF[t]:OFF[t] + NT], kT[:, lo:hi], start=True, stop=True)\
                 .then_inc(attn_scored, 1)

            def p1_turn_attn(c, t):
                b, n = c.b, c.tile(t)
                pe.wait_ge(mixed_ready, 4 * (n + 1))
                wait(pe, attnT_ready, n)
                for c in chunks(t, 2):
                    last = e.transpose(bankB[0:NT, c * NT:(c + 1) * NT], mixed[t][:, OFF[c]:OFF[c] + NT], id32[0:NT, 0:NT])
                last.then_inc(attn_turned, 1)

            def p1_ax(c, t):
                b, n = c.b, c.tile(t)
                pe.wait_ge(attnT_ready, n + 1)
                wait(pe, axT_ready, n)
                if t == 0:
                    wait(pe, qk_ready, 2 * (b + 1))
                cc = chunks(t, 2)
                for c in cc:
                    last = e.matmul(bankC[:, 0:NT], xl[0:KEYS[c], c, :], attnT[0:KEYS[c], c * NT:(c + 1) * NT],
                                    start=c == cc[0], stop=c == cc[-1])
                last.then_inc(ax_done, 1)

            def p1_wo(c, t):
                b, n = c.b, c.tile(t)
                pe.wait_ge(axT_ready, n + 1)
                e.matmul(bankC[0:NT, (1 + t) * D:(2 + t) * D], axT[:, :], wo_sb[:, :], start=True, stop=True).then_inc(wo_done, 1)

            def p1_turn_hn(c):
                b = c.b
                pe.wait_ge(hn_ready, b + 1)
                for t in range(3):
                    last = e.transpose(bankA[:, t * NT:(t + 1) * NT], hn[:, t, :], id32[0:NT, 0:NT])
                last.then_inc(hn_turned, 1)

            def p1_inner(c, lows):
                b = c.b
                pe.wait_ge(hnT_ready, b + 1)
                pe.wait_ge(attnT_ready, 3 * (b + 1))
                pe.wait_ge(res_ready, b + 1)
                toks = hnT[c.par][:, :, :].rearrange("p t n -> p (t n)")
                for l in lows:
                    if l == 3:
                        pe.wait_ge(gelu_done, 2 * b + 1)
                    last = e.matmul(banks3[:, (l % 3) * 512:(l % 3) * 512 + 3 * NT], down_x[:, l, :, :].rearrange("p h t -> p (h t)"), toks,
                                    start=True, stop=True)
                    if l >= 2:
                        last.then_inc(inner_done, 1)

            def q_product(c, t):
                b, n = c.b, c.tile(t)
                pe.wait_ge(hnT_ready, b + 1)
                wait(pe, qnT_ready, n)
                e.matmul(bankQ[0:NT, :], hnT[c.par][:, t, :], fwqT[:, :], start=True, stop=False)
                e.matmul(bankQ[0:NT, :], ones3[:, :], fbq3[:, :], start=False, stop=True).then_inc(q_done, 1)

            def q_turn(c, t):
                n = c.tile(t)
                pe.wait_ge(qn_ready, 3 * (n + 1))
                for k in range(PAIRS):
                    last = e.transpose(bankQ[:, k * NT:(k + 1) * NT], qn[:, 2 * k:2 * k + 2, :].rearrange("p h q -> p (h q)"), id32[0:NT, 0:NT])
                last.then_inc(qn_turned, 1)

            def q_score(c, t):
                n = c.tile(t)
                pe.wait_ge(qnT_ready, n + 1)
                wait(pe, scores_ready, n)
                wait(pe, wcT_ready, n - 1)
                for k in range(PAIRS):
                    last = e.matmul(bankS[0:NT, k * 4 * PK:(k + 1) * 4 * PK], qnT[:, k, :], key_bd[:, :], start=True, stop=True)
                last.then_inc(scored, 1)

            def turn_cells(c, t):
                n = c.tile(t)
                pe.wait_ge(weights, 4 * (n + 1))
                pe.wait_ge(scores_ready, at_most(n + 2, 3 * B))
                wait(pe, wcT_ready, n)
                for i in range(3 * PAIRS):
                    k, part = i // 3, i % 3
                    last = e.transpose(wcT_ps[:, i // 6, (i % 6) * NT:(i % 6 + 1) * NT],
                                       wcell[:, part, 2 * k:2 * k + 2, :].rearrange("p h c -> p (h c)"), id16[0:NT, 0:NT])
                last.then_inc(cells_turned, 1)

            def merge_cells(c, t):
                n = c.tile(t)
                pe.wait_ge(wcT_ready, n + 1)
                wait(pe, out_ready, n)
                wait(pe, prod_ready, n)
                for k in range(PAIRS):
                    q = 2 * SLOTS * (k % 2)
                    last = e.matmul(merged[q:q + 2 * SLOTS, k // 2, 0:3 * NT], merge_sb[:, :],
                                    wcT[:, k, :, :].rearrange("p k n -> p (k n)"), start=True, stop=True)
                last.then_inc(merge_done, 1)

            def scatter(c, t):
                m = c.tile(t)
                pe.wait_ge(wl_ready, 2 * (m + 1))
                pe.wait_ge(wm_ready, m + 1)
                pe.wait_ge(high_ready, m + 1)
                pe.wait_ge(onehigh_ready, m + 1)
                for g in range(NG):
                    for k in range(2):
                        for part in range(2):
                            last = e.matmul(coef[:, g, :, :], oh[:, k, g, :, :].rearrange("p v t -> p (v t)"),
                                            wl[:, part, k, :, TG * g:TG * (g + 1)], start=k + part == 0, stop=k + part == 2)
                last.then_inc(scattered, 1)

            def experts_out(c, t):
                m = c.tile(t)
                pe.wait_ge(prod_ready, m + 1)
                for l in range(EL):
                    last = e.matmul(ffn, prod[:, l, :], up_x[:, l, :], start=l == 0, stop=l == EL - 1)
                last.then_inc(ffn_done, 1)

            def body(c):
                do(q_score, c, 0)
                do(q_product, c, 1)
                do(scatter, c + -1, 1)
                do(p1_turn_xl, c + 1)
                do(p1_project, c + 1)
                do(p1_scores, c + 1, 0)
                do(experts_out, c + -1, 1)
                do(turn_cells, c + -1, 2)
                do(merge_cells, c + -1, 2)
                do(q_turn, c, 1)
                do(p1_turn_attn, c + 1, 0)
                do(p1_scores, c + 1, 1)
                do(p1_ax, c + 1, 0)
                do(q_score, c, 1)
                do(q_product, c, 2)
                do(p1_wo, c + 1, 0)
                do(p1_turn_attn, c + 1, 1)
                do(p1_scores, c + 1, 2)
                do(p1_ax, c + 1, 1)
                do(scatter, c + -1, 2)
                do(p1_wo, c + 1, 1)
                do(experts_out, c + -1, 2)
                do(turn_cells, c, 0)
                do(p1_turn_attn, c + 1, 2)
                do(p1_ax, c + 1, 2)
                do(p1_wo, c + 1, 2)
                do(merge_cells, c, 0)
                do(q_turn, c, 2)
                do(q_score, c, 2)
                do(p1_turn_hn, c + 1)
                do(q_product, c + 1, 0)
                do(p1_inner, c + 1, range(3))
                do(scatter, c, 0)
                do(experts_out, c, 0)
                do(p1_inner, c + 1, (3,))
                do(turn_cells, c, 1)
                do(p1_turn_x, c + 2)
                do(merge_cells, c, 1)
                do(p1_conv, c + 2)
                do(p1_sum_sq, c + 2)
                do(p1_turn_conv, c + 2)
                do(q_turn, c + 1, 0)

            run(pe, start, body, lambda: None)

        @block.vector
        def _(dve):
            v = nc.vector

            def start():
                link = linker(dve, setup_dve, 10, 0)
                dve.wait_ge(w_in, ALL_LOADED)
                link(v.tensor_tensor(key_sq[:, :, :], key_in[:, :, :], key_in[:, :, :], ALU.mult))
                link(v.tensor_reduce(out=key_n[:, :], in_=key_sq[:, :, :], axis=X, op=ALU.add))
                dve.wait_ge(setup_key, 2)
                for hd in range(2):
                    for s in range(2):
                        k = 2 * hd + s
                        last = v.tensor_scalar(key_z[:, k, HALF * k:HALF * (k + 1)], key_in[:, s, :], key_n[:, s:s + 1], None, ALU.mult)
                link(last)
                dve.wait_ge(setup_act, 3)
                for wt, mean in ((fwqT[:, :], fmean[:, :]), (fbq_row, bmean[:, :])):
                    w3 = wt.rearrange("p (h q) -> p h q", h=H)
                    link(v.tensor_reduce(out=mean, in_=w3, axis=X, op=ALU.add))
                    link(v.tensor_scalar(mean, mean, 1.0 / QD, None, ALU.mult))
                    link(v.tensor_tensor(w3, w3, mean.unsqueeze(2).to_broadcast([w3.shape[0], H, QD]), ALU.subtract))
                dve.wait_ge(setup_act, 4)
                for q in range(TG):
                    last = v.tensor_copy(down_x[:, :, :, q], downT[:, :].rearrange("p (h l) -> p l h", l=EL))
                link(last)
                part = linker(dve, setup_fbq, 5, 0)
                part(v.tensor_copy(fbq3[0:1, :], fbq_row))
                part(v.tensor_tensor(fbq_rest[:, 0, :], fbq_row, fbq3[0:1, :], ALU.subtract))
                part(v.tensor_copy(fbq_part[:, 0, :], fbq_rest[:, 0, :]))
                part(v.tensor_tensor(fbq_rest[:, 1, :], fbq_rest[:, 0, :], fbq_part[:, 0, :], ALU.subtract))
                part(v.tensor_copy(fbq_part[:, 1, :], fbq_rest[:, 1, :]))
                dve.wait_ge(setup_pool, 6)

            def p1_wsq(c):
                b = c.b
                dve.wait_ge(wsq_done, b + 1)
                wait(dve, wnorm_ready, b)
                v.tensor_scalar(wsq[:, :], bankC[0:NT, 0:3], 0.0, None, ALU.max).then_inc(wsq_ready, 1)

            def p1_tscale(c):
                b = c.b
                link = linker(dve, tscale_ready, 5, b)
                dve.wait_ge(wnorm_ready, b + 1)
                wait(dve, tanh_done, b)
                link(v.tensor_scalar(small[:, :], wnorm[:, :], 1.0, None, ALU.is_lt))
                link(v.tensor_scalar(wden[:, :], wnorm[:, :], 1.0e-7, None, ALU.add))
                link(v.reciprocal(wden[:, :], wden[:, :]))
                link(v.scalar_tensor_tensor(out=tscale[:, :], in0=wden[:, :], scalar=1.0, in1=small[:, :], op0=ALU.min, op1=ALU.max))
                link(v.tensor_scalar(tscale[:, :], tscale[:, :], 1.0 / (1.0 + 1.0e-7), None, ALU.mult), wait=False)

            def p1_stats(c, i):
                b = c.b
                link = linker(dve, ln_stats[i], 3, b)
                src = (h0, res, h[c.par])[i]
                if i == 0:
                    dve.wait_ge(h0_ready, 2 * (b + 1))
                elif i == 1:
                    dve.wait_ge(res_ready, b + 1)
                else:
                    dve.wait_ge(h_ready, 3 * (b + 1))
                wait(dve, ln_rstd[i], b)
                for t in range(3):
                    last = v.bn_stats(out=bns[i][:, t, :], in_=src[:, t, :])
                link(last)
                settled(dve, passed_dve)
                for t in range(3):
                    last = v.bn_aggr(out=bna[i][:, t, :], in_=bns[i][:, t, :])
                link(last)
                link(v.tensor_scalar(lnv[i][:, :], bna[i][:, :, 1], 1.0e-5, None, ALU.add), wait=False)

            def p1_shift(c, i):
                b = c.b
                dve.wait_ge(ln_rstd[i], b + 1)
                wait(dve, (xl_ready, xh_ready, hn_ready)[i], b)
                v.scalar_tensor_tensor(out=lnm[i][:, :], in0=bna[i][:, :, 0], scalar=-1.0, in1=lnr[i][:, :],
                                       op0=ALU.mult, op1=ALU.mult).then_inc(ln_shift[i], 1)

            def p1_smax(c, t):
                b, n = c.b, c.tile(t)
                link = linker(dve, smax_ready, 2, n)
                dve.wait_ge(attn_scored, n + 1)
                wait(dve, probs_ready, n)
                lo2 = band(t, 2)[0]
                settled(dve, passed_dve)
                for w in range(3):
                    lo, hi = band(t, w)
                    last = v.tensor_tensor_reduce(out=masked[w][:, 0:hi - lo], in0=bankA[0:NT, lo - lo2:hi - lo2], in1=masks[t, w][:, :],
                                                  scale=1.0, scalar=-3.0e38, op0=ALU.add, op1=ALU.max, accum_out=smax[:, w:w + 1])
                link(last)
                link(v.tensor_scalar(sbias[:, :], smax[:, :], -SCORE_SCALE, None, ALU.mult), wait=False)

            def p1_mix(c, t):
                b, n = c.b, c.tile(t)
                link = linker(dve, mixed_ready, 4, n)
                dve.wait_ge(probs_ready, n + 1)
                wait(dve, attn_turned, 3 * b)
                link(v.reciprocal(rden[:, :], den[:, :]))
                for w in (2, 1, 0):
                    lo, hi = band(t, w)
                    dst = mixed[t][:, lo:hi]
                    if w == 2:
                        link(v.tensor_scalar(dst, probs[w][:, 0:hi - lo], rden[:, w:w + 1], None, ALU.mult))
                    else:
                        link(v.scalar_tensor_tensor(out=dst, in0=probs[w][:, 0:hi - lo], scalar=rden[:, w:w + 1], in1=dst,
                                                    op0=ALU.mult, op1=ALU.add), wait=w > 0)

            def p1_res(c):
                b = c.b
                dve.wait_ge(wo_done, 3 * (b + 1))
                dve.wait_ge(xb_ready, b + 1)
                wait(dve, xh_ready, b)
                v.tensor_tensor(res[:, :, :].rearrange("p t d -> p (t d)"), bankC[0:NT, D:4 * D],
                                xb[:, :, :].rearrange("p t d -> p (t d)"), ALU.add).then_inc(res_ready, 1)

            def rank(c, t, half):
                n = c.tile(t)
                src, v_, i_ = scores[c.slot(t)], val[c.slot(t)], idx[c.slot(t)]
                pairs = [[(hd, s) for hd in (4 * half + q, 4 * half + q + 1) for s in range(2)] for q in (0, 2)]
                base = 16 * n + 8 * half
                if half == 0:
                    dve.wait_ge(scores_ready, n + 1)
                    wait(dve, cells_ready, 3 * (n - 1))
                    wait(dve, idxf_ready, n - 1)
                settled(dve, passed_dve)
                for heads in pairs:
                    for hd, s in heads:
                        last = v.max(out=v_[:, hd, s, 0:8], in_=src[:, hd, s, :])
                    last.then_inc(ranked, 1)
                for q, heads in enumerate(pairs):
                    dve.wait_ge(ranked, base + 1 + q)
                    settled(dve, passed_dve)
                    for hd, s in heads:
                        v.max_index(out=i_[:, hd, s, 0:8], in_max=v_[:, hd, s, 0:8], in_values=src[:, hd, s, :])
                    for hd, s in heads:
                        last = v.match_replace(out=src[:, hd, s, :], in_to_replace=v_[:, hd, s, 0:8], in_values=src[:, hd, s, :], imm_value=NEG)
                    last.then_inc(ranked, 1)
                for q, heads in enumerate(pairs):
                    dve.wait_ge(ranked, base + 3 + q)
                    settled(dve, passed_dve)
                    for hd, s in heads:
                        last = v.max(out=v_[:, hd, s, 8:16], in_=src[:, hd, s, :])
                    last.then_inc(ranked, 1)
                for q, heads in enumerate(pairs):
                    dve.wait_ge(ranked, base + 5 + q)
                    settled(dve, passed_dve)
                    for hd, s in heads:
                        last = v.max_index(out=i_[:, hd, s, 8:16], in_max=v_[:, hd, s, 8:16], in_values=src[:, hd, s, :])
                    last.then_inc(ranked, 1)

            def digits(c, t):
                m = c.tile(t)
                dve.wait_ge(high_ready, m + 1)
                dve.wait_ge(wm_ready, m + 1)
                v.scalar_tensor_tensor(out=el[:, :, :], in0=eh[:, :, :], scalar=-float(EL), in1=wm[:, :, 2, :], op0=ALU.mult, op1=ALU.add)\
                 .then_inc(digits_ready, 1)

            def one_high(c, t):
                m = c.tile(t)
                wait(dve, scattered, m)
                for hi in range(EH):
                    last = v.tensor_scalar(oh[:, :, :, hi, :], eh[:, :, :].rearrange("p k (g t) -> p k g t", t=TG), float(hi), None, ALU.is_equal)
                last.then_inc(onehigh_ready, 1)

            def low_weights(c, t):
                m = c.tile(t)
                link = linker(dve, wl_ready, 2, m)
                dve.wait_ge(digits_ready, m + 1)
                for l in range(EL):
                    last = v.tensor_scalar(ol[:, :, l, :], el[:, :, :], float(l), None, ALU.is_equal)
                link(last)
                for k in range(2):
                    last = v.tensor_tensor(wl[:, :, k, :, :], wm[:, k, 0:2, :].unsqueeze(2).to_broadcast([128, 2, EL, NT]),
                                           ol[:, k, :, :].unsqueeze(1).to_broadcast([128, 2, EL, NT]), ALU.mult)
                link(last, wait=False)

            def product(c, t):
                b, m = c.b, c.tile(t)
                dve.wait_ge(scattered, m + 1)
                dve.wait_ge(gelu_done, 2 * (b + 1))
                wait(dve, ffn_done, m)
                v.tensor_tensor(prod[:, :, :].rearrange("p l (g t) -> p g l t", t=TG), coef, act_g[c.par][:, t, :, :, :], ALU.mult)\
                 .then_inc(prod_ready, 1)

            def finish(c, t):
                b, m = c.b, c.tile(t)
                dve.wait_ge(ffn_done, m + 1)
                wait(dve, stored[t], 16 * b)
                v.scalar_tensor_tensor(out=o_sb[:, t, :], in0=ffn, scalar=1.0 / WSCALE, in1=h[c.par][:, t, :], op0=ALU.mult, op1=ALU.add)\
                 .then_inc(out_ready, 1)

            def choose(c, t):
                n = c.tile(t)
                halves = (range(H // 2), range(H // 2, H))
                for q, heads in enumerate(halves):
                    dve.wait_ge(cells_ready, 3 * n + 1 + q)
                    settled(dve, passed_dve)
                    for hd in heads:
                        last = v.max(out=best[:, hd, 0:8], in_=cs[:, hd, :])
                    last.then_inc(chosen, 1)
                for q, heads in enumerate(halves):
                    dve.wait_ge(chosen, 12 * n + 1 + q)
                    settled(dve, passed_dve)
                    for hd in heads:
                        last = v.match_replace(out=cr[:, hd, :], in_to_replace=best[:, hd, 0:8], in_values=cs[:, hd, :], imm_value=NEG)
                    last.then_inc(chosen, 1)
                for q, heads in enumerate(halves):
                    dve.wait_ge(chosen, 12 * n + 3 + q)
                    settled(dve, passed_dve)
                    for hd in heads:
                        last = v.max(out=best[:, hd, 8:16], in_=cr[:, hd, :])
                    last.then_inc(chosen, 1)
                for q, heads in enumerate(halves):
                    dve.wait_ge(chosen, 12 * n + 5 + q)
                    settled(dve, passed_dve)
                    for hd in heads:
                        last = v.match_replace(out=cr[:, hd, :], in_to_replace=best[:, hd, 8:16], in_values=cr[:, hd, :], imm_value=NEG)
                    last.then_inc(chosen, 1)

            def weigh(c, t):
                n = c.tile(t)
                wait(dve, weights, 4 * n)
                dve.wait_ge(chosen, 12 * n + 8)
                v.tensor_scalar(taken[:, :, :], cr[:, :, :], NEG / 2, None, ALU.is_lt).then_inc(chosen, 1)
                dve.wait_ge(best_exp_ready, n + 1)
                v.tensor_reduce(out=wsum[:, :], in_=best_exp[:, :, :], axis=X, op=ALU.add).then_inc(chosen, 1)
                dve.wait_ge(chosen, 12 * n + 10)
                v.tensor_scalar(wsum2[:, :], wsum[:, :], 1.0 / WSCALE, None, ALU.mult).then_inc(chosen, 1)
                dve.wait_ge(chosen, 12 * n + 11)
                v.reciprocal(wrec[:, :], wsum2[:, :]).then_inc(chosen, 1)

            def body(c):
                do(weigh, c, 1)
                do(product, c, 0)
                do(rank, c, 2, 0)
                do(finish, c, 0)
                do(rank, c, 2, 1)
                do(digits, c, 1)
                do(p1_wsq, c + 2)
                do(one_high, c, 1)
                do(p1_tscale, c + 2)
                do(low_weights, c, 1)
                do(choose, c, 2)
                do(p1_stats, c + 2, 0)
                do(weigh, c, 2)
                do(product, c, 1)
                do(p1_shift, c + 2, 0)
                do(rank, c + 1, 0, 0)
                do(rank, c + 1, 0, 1)
                do(p1_smax, c + 2, 0)
                do(finish, c, 1)
                do(choose, c + 1, 0)
                do(p1_mix, c + 2, 0)
                do(digits, c, 2)
                do(weigh, c + 1, 0)
                do(p1_smax, c + 2, 1)
                do(one_high, c, 2)
                do(p1_mix, c + 2, 1)
                do(low_weights, c, 2)
                do(p1_smax, c + 2, 2)
                do(product, c, 2)
                do(p1_mix, c + 2, 2)
                do(rank, c + 1, 1, 0)
                do(p1_res, c + 2)
                do(finish, c, 2)
                do(p1_stats, c + 2, 1)
                do(p1_shift, c + 2, 1)
                do(rank, c + 1, 1, 1)
                do(p1_stats, c + 2, 2)
                do(digits, c + 1, 0)
                do(p1_shift, c + 2, 2)
                do(one_high, c + 1, 0)
                do(choose, c + 1, 1)
                do(low_weights, c + 1, 0)

            run(dve, start, body, lambda: None)


_INS = ["x", "L0_tok_kernel", "L0_tok_bias", "L0_attn_Wq", "L0_attn_bq", "L0_attn_Wk", "L0_attn_bk", "L0_attn_Wo", "L0_attn_bo",
        "L0_attn_gamma", "L0_attn_beta", "L0_ffn_Wq", "L0_ffn_bq", "L0_ffn_ln_g", "L0_ffn_ln_b", "L0_ffn_keys0", "L0_ffn_keys1",
        "L0_ffn_expert_down", "L0_ffn_expert_up"]


def kernel(**inputs):
    import concourse.bacc as bacc
    from concourse.bass_utils import run_bass_kernel_spmd
    nc = bacc.Bacc("TRN2", target_bir_lowering=False, num_devices=1)
    arrays, args = {}, []
    given = [(name, np.ascontiguousarray(inputs[name])) for name in _INS]
    given += [("merge", merge_matrix()), ("identity", np.eye(128, dtype=np.float32)),
              ("own", np.tile(np.eye(TG, dtype=np.float32), (EH, 1)))]
    for name, a in given:
        arrays[f"in_{name}"] = a
        args.append(nc.dram_tensor(f"in_{name}", a.shape, mybir.dt.from_np(a.dtype), kind="ExternalInput").ap())
    out = nc.dram_tensor("out_0", (B, T, D), mybir.dt.float32, kind="ExternalOutput").ap()
    build(nc, *args, out)
    r = run_bass_kernel_spmd(nc, [arrays], core_ids=[0])
    return r.results[0]["out_0"]
```

```python
import numpy as np
import concourse.bass as bass
from concourse import mybir
from concourse.alu_op_type import AluOpType as ALU
from contextlib import ExitStack

B, L, C = 16, 375, 64
TAPS, D = 9, 128
T = L - TAPS + 1
NT = 124
OFF = [0, 122, T - NT]
FIRST = [0, 2, OFF[1] + NT - OFF[2]]
KEYS = [OFF[1], OFF[2] - OFF[1], NT]
RADII = [24 // 2, 168 // 2, 180 // 2]
XT = L // 3
H, QD, HALF, PK, TOP = 8, 64, 32, 64, 16
CELLS = [(a, c) for a in range(TOP) for c in range(TOP) if (a + 1) * (c + 1) <= TOP]
NC = len(CELLS)
PAIRS = H // 2
SLOTS = 32
EH, EL, TG = 32, 4, 4
NG = NT // TG
WSCALE = 4096.0
NEG = -1.0e30
BEFORE, PEELED, AFTER = -2, 4, B + 2
SCORE_SCALE = 1.0 / float(np.sqrt(np.float32(D)))


def merge_matrix():
    def together(p, q):
        (a, c), (e, g) = p, q
        return (a + 1) * (c + 1) + (e + 1) * (g + 1) - (min(a, e) + 1) * (min(c, g) + 1) <= TOP
    slots = [[(0, c)] for c in range(TOP)] + [[] for _ in range(SLOTS - TOP)]
    rest = sorted((p for p in CELLS if p[0]), key=lambda p: -(p[0] + 1) * (p[1] + 1) + 0.01 * p[0])
    moves = {(a, 0): a for a in range(8, 16)}
    moves.update({(1, 4): 12, (1, 5): 13, (1, 6): 14, (1, 7): 15, (2, 3): 10, (2, 4): 11,
                  (3, 2): 8, (3, 3): 9, (5, 1): 6, (6, 1): 7})
    free = iter(range(TOP, SLOTS))
    for p in rest:
        slots[moves[p] if p in moves else next(free)].append(p)
    m = np.zeros((2 * NC, 2 * SLOTS), np.float16)
    for s, cells in enumerate(slots):
        assert not any(together(p, q) for i, p in enumerate(cells) for q in cells[:i])
        for p in cells:
            for h in range(2):
                m[h * NC + CELLS.index(p), h * SLOTS + s] = 1
    assert m.sum() == 2 * NC
    return m


def band(t, w):
    return max(0, OFF[t] - RADII[w]), min(T, OFF[t] + NT + RADII[w])


def chunks(t, w):
    lo, hi = band(t, w)
    return [c for c in range(3) if lo < OFF[c] + KEYS[c] and hi > OFF[c]]


def build(nc, x, tok_kernel, tok_bias, wq, bq, wk, bk, wo, bo, gamma, beta, fwq, fbq, lng, lnb,
          keys0, keys1, down, up, merge, ident, own, out):
    f32, f16, bf16, i16, u16 = mybir.dt.float32, mybir.dt.float16, mybir.dt.bfloat16, mybir.dt.int16, mybir.dt.uint16
    ACT = mybir.ActivationFunctionType
    X = mybir.AxisListType.X
    ctx = ExitStack()
    with ctx:
        def sb(name, shape, dt=f32):
            return ctx.enter_context(nc.sbuf_tensor(name, shape, dt))

        def sem(name):
            return ctx.enter_context(nc.semaphore(name))

        def col(v):
            return v.rearrange("(p a) -> p a", a=1)

        def row(v):
            return v.rearrange("(a p) -> a p", a=1)

        id32 = sb("id32", [128, 128])
        id16 = sb("id16", [128, 128], f16)
        merge_sb = sb("merge_sb", [2 * NC, 2 * SLOTS], f16)
        own_sb = sb("own_sb", [128, TG])
        ones = sb("ones", [128, 128])
        ones3 = sb("ones3", [3, NT], bf16)
        third = sb("third", [128, 1])
        eps3, tiny3, minus_scale = sb("eps3", [NT, 3]), sb("tiny3", [NT, 3]), sb("minus_scale", [NT, 3])
        digit_bias = sb("digit_bias", [128, 1])
        power = sb("power", [128, 2, 16])
        conv_w = sb("conv_w", [128, 5, D])
        wq_sb, wk_sb, wo_sb = sb("wq_sb", [D, D]), sb("wk_sb", [D, D]), sb("wo_sb", [D, D])
        bq_sb, bk_sb = sb("bq_sb", [D, 1]), sb("bk_sb", [D, 1])
        rows = sb("rows", [1, 4 * D + 2 * QD + H * QD])
        vecs = sb("vecs", [128, 4 * D + 2 * QD])
        tokb, bob, gam, bet = (vecs[0:NT, i * D:(i + 1) * D] for i in range(4))
        fbq_row = rows[0:1, 4 * D + 2 * QD:4 * D + 2 * QD + H * QD]
        fwq_in = sb("fwq_in", [128, 4, D])
        fwqT = sb("fwqT", [D, H * QD])
        fbq3 = sb("fbq3", [3, H * QD], bf16)
        fbq_part = sb("fbq_part", [1, 2, H * QD], bf16)
        fbq_rest = sb("fbq_rest", [1, 2, H * QD])
        eps8, guard8 = sb("eps8", [NT, H]), sb("guard8", [NT, H])
        wgT = sb("wgT", [D, H * QD])
        wg_rows = sb("wg_rows", [128, PAIRS, D])
        wgk = sb("wgk", [D, PAIRS, 4 * PK])
        bias_row = sb("bias_row", [1, H * QD])
        bias9 = sb("bias9", [H + 1, H * QD])
        bias9T = sb("bias9T", [128, PAIRS, H + 1])
        bias9k = sb("bias9k", [H + 1, PAIRS, 4 * PK])
        fmean = sb("fmean", [D, H])
        bmean = sb("bmean", [1, H])
        key_in = sb("key_in", [PK, 2, HALF])
        key_sq = sb("key_sq", [PK, 2, HALF])
        key_n = sb("key_n", [PK, 2])
        key_z = sb("key_z", [PK, 4, 128])
        key_bd = sb("key_bd", [128, 4 * PK])
        down_in = sb("down_in", [128, D])
        downT = sb("downT", [D, 128])
        down_x = sb("down_x", [D, EL, EH, TG])
        up_x = sb("up_x", [128, EL, D])
        masks = {}
        for t in range(3):
            for w in range(3):
                lo, hi = band(t, w)
                masks[t, w] = sb(f"mask{t}{w}", [NT, hi - lo])

        x_in = [sb(f"x_in{p}", [XT, 3, 2, C]) for p in range(2)]
        xT = sb("xT", [128, L])
        xT_sq = sb("xT_sq", [128, L])
        sq_pairs = sb("sq_pairs", [128, L - 2])
        sq_win = sb("sq_win", [128, T])
        convT = sb("convT", [D, T])
        wsq = sb("wsq", [NT, 3])
        wnorm = sb("wnorm", [NT, 3])
        wden = sb("wden", [NT, 3])
        tscale = sb("tscale", [NT, 3])
        th = sb("th", [NT, 3, D])
        h0 = sb("h0", [NT, 3, D])
        bns = [sb(f"bns{i}", [NT, 3, 6]) for i in range(3)]
        bna = [sb(f"bna{i}", [NT, 3, 2]) for i in range(3)]
        lnv = [sb(f"lnv{i}", [NT, 3]) for i in range(3)]
        lnr = [sb(f"lnr{i}", [NT, 3]) for i in range(3)]
        lnm = [sb(f"lnm{i}", [NT, 3]) for i in range(3)]
        xl = sb("xl", [NT, 3, D])
        xb = sb("xb", [NT, 3, D])
        xlT = sb("xlT", [D, T])
        qT, kT = sb("qT", [D, T]), sb("kT", [D, T])
        masked = [sb(f"masked{w}", [NT, NT + 2 * RADII[w]]) for w in range(3)]
        smax = sb("smax", [NT, 3])
        sbias = sb("sbias", [NT, 3])
        probs = [[sb(f"probs{t}{w}", [NT, T]) for w in range(3)] for t in range(3)]
        den = sb("den", [NT, 3])
        rden = sb("rden", [NT, 3])
        diag = sb("diag", [NT, 3, NT])
        attnT = sb("attnT", [NT, 3 * NT])
        axT = sb("axT", [D, NT])
        res = sb("res", [NT, 3, D])
        xh = sb("xh", [NT, 3, D])
        h = [sb(f"hsum{p}", [NT, 3, D]) for p in range(2)]
        hn = sb("hn", [NT, 3, D])
        hnT = [sb(f"hnT{p}", [D, 3, NT]) for p in range(2)]
        act_g = [sb(f"act_g{p}", [128, 3, NG, EL, TG]) for p in range(2)]

        sq_junk = sb("sq_junk", [NT, H, QD])
        ns_junk = sb("ns_junk", [NT, 2 * H, HALF])
        qss = sb("qss", [NT, H])
        qvar = sb("qvar", [NT, H])
        std9 = sb("std9", [NT, H + 1])
        std9T = sb("std9T", [H + 1, NT])
        qguard = sb("qguard", [NT, H])
        nss = sb("nss", [NT, H, 2])
        nmx = sb("nmx", [NT, H, 2])
        qscale = [sb(f"qscale{p}", [NT, H, 2]) for p in range(2)]
        val_s = sb("val_s", [NT, H, 2, TOP])
        scores = [sb(f"scores{p}", [NT, H, 2, PK]) for p in range(2)]
        val = [sb(f"val{p}", [NT, H, 2, TOP]) for p in range(2)]
        idx = [sb(f"idx{p}", [NT, H, 2, TOP], u16) for p in range(2)]
        idxf = [sb(f"idxf{p}", [NT, H, 2, TOP]) for p in range(2)]
        cs = sb("cs", [NT, H, NC])
        cr = sb("cr", [NT, H, NC])
        ce = sb("ce", [NT, H, NC])
        cx = sb("cx", [NT, H, NC])
        best = sb("best", [NT, H, TOP])
        best_exp = sb("best_exp", [NT, H, TOP])
        taken = sb("taken", [NT, H, NC])
        wsel = sb("wsel", [NT, H, NC])
        wsum = sb("wsum", [NT, H])
        wrec = sb("wrec", [NT, H])
        wn = sb("wn", [NT, H, NC])
        wcell = sb("wcell", [NT, 3, H, NC], f16)
        wcT = sb("wcT", [2 * NC, PAIRS, 3, NT], f16)
        wm = sb("wm", [128, 2, 3, NT], f16)
        eh = sb("eh", [128, 2, NT], i16)
        eh4 = sb("eh4", [128, 2, NT], f16)
        el = sb("el", [128, 2, NT], f16)
        oh = sb("oh", [128, 2, NG, EH, TG], f16)
        ol = sb("ol", [128, 2, EL, NT], f16)
        wl = sb("wl", [128, 2, 2, EL, NT], f16)
        prod = sb("prod", [128, EL, NT])
        o_sb = sb("o_sb", [NT, 3, D])

        banks3 = ctx.enter_context(nc.psum_tensor("banks3", [128, 3 * 512], f32))
        bankA, bankB, bankC = (banks3[:, i * 512:(i + 1) * 512] for i in range(3))
        bankQ = ctx.enter_context(nc.psum_tensor("bankQ", [128, 512], f32))
        bankS = ctx.enter_context(nc.psum_tensor("bankS", [128, 1024], f32))
        bankM = ctx.enter_context(nc.psum_tensor("bankM", [128, 1024], f32))
        wcT_ps = bankS[0:2 * NC, :].bitcast(f16).rearrange("p (k n) -> p k n", k=2)
        merged = bankM[:, :].rearrange("p (k n) -> p k n", k=2)
        coef = bankM[:, 0:NG * EL * TG].rearrange("p (g l t) -> p g l t", g=NG, l=EL)
        ffn = bankM[0:NT, 512:512 + D]

        w_in = sem("w_in")
        setup_pool, setup_dve, setup_act, setup_pe = (sem(f"setup_{e}") for e in ("pool", "dve", "act", "pe"))
        passed_dve, passed_pool = sem("passed_dve"), sem("passed_pool")
        setup_fbq, fbq_spread = sem("setup_fbq"), sem("fbq_spread")
        setup_key = sem("setup_key")
        x_loaded = [sem(f"x_loaded{p}") for p in range(2)]
        x_turned = sem("x_turned")
        xT_ready = sem("xT_ready")
        conv_done = sem("conv_done")
        convT_ready = sem("convT_ready")
        conv_turned = sem("conv_turned")
        sq_win_ready = sem("sq_win_ready")
        wsq_done = sem("wsq_done")
        wsq_ready = sem("wsq_ready")
        wnorm_ready = sem("wnorm_ready")
        tscale_ready = sem("tscale_ready")
        tanh_done = sem("tanh_done")
        h0_ready = sem("h0_ready")
        ln_stats = [sem(f"ln_stats{i}") for i in range(3)]
        ln_rstd = [sem(f"ln_rstd{i}") for i in range(3)]
        ln_shift = [sem(f"ln_shift{i}") for i in range(3)]
        xl_ready = sem("xl_ready")
        xl_turned = sem("xl_turned")
        xlT_ready = sem("xlT_ready")
        qk_done = sem("qk_done")
        qk_ready = sem("qk_ready")
        xb_ready = sem("xb_ready")
        attn_scored = sem("attn_scored")
        smax_ready = sem("smax_ready")
        sbias_ready = sem("sbias_ready")
        probs_ready = sem("probs_ready")
        rden_ready = sem("rden_ready")
        diag_ready = sem("diag_ready")
        attn_turned = sem("attn_turned")
        attnT_ready = sem("attnT_ready")
        ax_done = sem("ax_done")
        axT_ready = sem("axT_ready")
        wo_done = sem("wo_done")
        res_ready = sem("res_ready")
        xh_ready = sem("xh_ready")
        h_ready = sem("h_ready")
        hn_ready = sem("hn_ready")
        hn_turned = sem("hn_turned")
        hnT_ready = sem("hnT_ready")
        inner_done = sem("inner_done")
        gelu_done = sem("gelu_done")
        q_done = sem("q_done")
        qss_ready = sem("qss_ready")
        std_ready = sem("std_ready")
        std_turned = sem("std_turned")
        stdT_ready = sem("stdT_ready")
        q2_done = sem("q2_done")
        nss_ready = sem("nss_ready")
        nmx_ready = sem("nmx_ready")
        qscale_ready = sem("qscale_ready")
        vals_scaled = sem("vals_scaled")
        scored = sem("scored")
        scores_ready = sem("scores_ready")
        ranked = sem("ranked")
        idxf_ready = sem("idxf_ready")
        cells_ready = sem("cells_ready")
        exp_ready = sem("exp_ready")
        best_exp_ready = sem("best_exp_ready")
        chosen = sem("chosen")
        weights = sem("weights")
        whigh_ready = sem("whigh_ready")
        cells_turned = sem("cells_turned")
        wcT_ready = sem("wcT_ready")
        merge_done = sem("merge_done")
        wm_ready = sem("wm_ready")
        high_ready = sem("high_ready")
        digits_ready = sem("digits_ready")
        onehigh_ready = sem("onehigh_ready")
        wl_ready = sem("wl_ready")
        scattered = sem("scattered")
        prod_ready = sem("prod_ready")
        ffn_done = sem("ffn_done")
        out_ready = sem("out_ready")
        stored = [sem(f"stored{t}") for t in range(3)]

        block = ctx.enter_context(nc.Block())

        def linker(eng, s, per, call):
            count = [0]

            def link(ins, wait=True):
                count[0] += 1
                assert count[0] <= per
                ins.then_inc(s, 1)
                if wait:
                    eng.wait_ge(s, per * call + count[0])
            return link

        def wait(eng, s, value):
            if not isinstance(value, int) or value > 0:
                eng.wait_ge(s, value)

        def settled(eng, s):
            eng.sem_inc(s, 1)

        class Batch:
            def __init__(self, j, par):
                self.j, self.par, self.b = j, par, 2 * j + par
                self.exists = not isinstance(j, int) or 0 <= self.b < B

            def __add__(self, k):
                return Batch(self.j + (self.par + k) // 2, (self.par + k) % 2)

            def tile(self, t):
                return 3 * self.b + t

            def slot(self, t):
                return (self.par + t) % 2

        def do(step, c, *rest):
            if c.exists:
                step(c, *rest)

        def at_most(value, top):
            return min(value, top) if isinstance(value, int) else value

        def batch(v, b):
            one = v[b:b + 1, :, :] if isinstance(b, int) else v[bass.ds(b, 1), :, :]
            return one.rearrange("a p c -> (a p) c")

        def run(eng, start, body, end):
            start()
            for b in range(BEFORE, PEELED):
                body(Batch(b // 2, b % 2))
            with eng.Fori(PEELED // 2, B // 2 - 1) as j:
                body(Batch(j, 0))
                body(Batch(j, 1))
            for b in range(B - 2, AFTER):
                body(Batch(b // 2, b % 2))
            end()

        kern = tok_kernel[0:TAPS - 1, :, :].rearrange("(m s) c f -> s c m f", s=2)
        loads = [(id32[:, :], ident), (own_sb[:, :], own), (merge_sb[:, :], merge),
                 (rows[0:1, 0:D], row(tok_bias)), (rows[0:1, D:2 * D], row(bo)),
                 (rows[0:1, 2 * D:3 * D], row(gamma)), (rows[0:1, 3 * D:4 * D], row(beta)),
                 (rows[0:1, 4 * D:4 * D + QD], row(lng)), (rows[0:1, 4 * D + QD:4 * D + 2 * QD], row(lnb)),
                 (fbq_row, row(fbq)), (fwq_in[:, :, :], fwq.rearrange("(k p) d -> p k d", p=128)),
                 (key_in[:, 0, :], keys0), (key_in[:, 1, :], keys1), (down_in[:, :], down[0:128, :]),
                 (conv_w[0:C, 0:4, :], kern[0, :, :, :]), (conv_w[C:2 * C, 0:4, :], kern[1, :, :, :]),
                 (conv_w[0:C, 4, :], tok_kernel[TAPS - 1, :, :]),
                 (wq_sb[:, :], wq), (wk_sb[:, :], wk), (wo_sb[:, :], wo),
                 (bq_sb[:, :], col(bq)), (bk_sb[:, :], col(bk))]
        for t in range(TG):
            loads.append((up_x[t:128:TG, :, :], up[0:128, :].rearrange("(h l) o -> h l o", l=EL)))
        ALL_LOADED = 16 * len(loads)

        @block.sync
        def _(sp):
            def load_x(c):
                b = c.b
                wait(sp, x_turned, b - 1)
                x_b, slot = batch(x, b), x_in[c.par]
                sp.dma_start(slot[:, :, 0, :], x_b[0:L, :].rearrange("(t p) c -> p t c", t=3)).then_inc(x_loaded[c.par], 16)
                sp.dma_start(slot[:, 0:2, 1, :], x_b[1:1 + 2 * XT, :].rearrange("(t p) c -> p t c", t=2)).then_inc(x_loaded[c.par], 16)
                sp.dma_start(slot[0:XT - 1, 2, 1, :], x_b[1 + 2 * XT:L, :]).then_inc(x_loaded[c.par], 16)

            def store(c, t):
                b = c.b
                sp.wait_ge(out_ready, 3 * b + t + 1)
                f = FIRST[t]
                sp.dma_start(batch(out, b)[OFF[t] + f:OFF[t] + NT, :], o_sb[f:NT, t, :]).then_inc(stored[t], 16)

            def start():
                for dst, src in loads:
                    sp.dma_start(dst, src).then_inc(w_in, 16)
                sp.wait_ge(setup_pool, 1)
                sp.wait_ge(setup_fbq, 5)
                for k in range(2):
                    sp.dma_start(fbq3[1 + k:2 + k, :], fbq_part[0:1, k, :]).then_inc(fbq_spread, 16)
                sp.wait_ge(setup_dve, 13)
                sp.dma_start(bias9[H:H + 1, :], bias_row[:, :]).then_inc(fbq_spread, 16)

            def body(c):
                do(load_x, c + 2)
                do(store, c + -2, 0)
                do(store, c + -2, 1)
                do(store, c + -2, 2)

            def end():
                for t in range(3):
                    sp.wait_ge(stored[t], 16 * B)

            run(sp, start, body, end)

        @block.gpsimd
        def _(pool):
            g = nc.gpsimd

            def start():
                for p in range(2):
                    last = g.memset(x_in[p][:, 2, 1, :], 0.0)
                last.then_inc(setup_pool, 1)
                g.memset(ones[:, :], 1.0)
                g.memset(power[:, 0, :], -0.5)
                g.memset(power[:, 1, :], 0.5)
                g.memset(key_z[:, :, :], 0.0).then_inc(setup_pool, 1)
                pool.wait_ge(setup_dve, 2)
                link = linker(pool, setup_key, 2, 0)
                link(g.tensor_scalar(key_n[:, :], key_n[:, :], 1.0e-24, None, ALU.max))
                link(g.tensor_tensor(key_n[:, :], key_n[:, :], power[0:PK, 0, 0:2], ALU.pow))
                g.memset(ones3[:, :], 1.0)
                g.memset(third[:, :], 1.0 / 3.0)
                g.memset(eps8[:, :], 1.0e-5)
                g.memset(eps3[:, :], 1.0e-5)
                g.memset(tiny3[:, :], 1.0e-7)
                g.memset(minus_scale[:, :], -SCORE_SCALE)
                g.memset(guard8[:, :], 1.0e-24)
                g.memset(std9[:, H:H + 1], 1.0)
                g.memset(digit_bias[:, :], -(EL - 1) / 2.0 / EL).then_inc(setup_pool, 1)
                for t in range(3):
                    for w in range(3):
                        g.memset(probs[t][w][:, :], 0.0)
                        g.memset(masks[t, w][:, :], 0.0)
                g.memset(wden[:, :], 0.0).then_inc(setup_pool, 1)
                pool.wait_ge(setup_pool, 4)
                for t in range(3):
                    for w in range(3):
                        lo, hi = band(t, w)
                        g.affine_select(out=masks[t, w][:, :], in_=masks[t, w][:, :], compare_op=ALU.is_ge, fill=NEG,
                                        base=lo - OFF[t] + RADII[w], pattern=[[1, hi - lo]], channel_multiplier=-1)
                g.memset(wden[:, :], 0.0).then_inc(setup_pool, 1)
                pool.wait_ge(setup_pool, 5)
                for t in range(3):
                    for w in range(3):
                        lo, hi = band(t, w)
                        last = g.affine_select(out=masks[t, w][:, :], in_=masks[t, w][:, :], compare_op=ALU.is_ge, fill=NEG,
                                               base=OFF[t] - lo + RADII[w], pattern=[[-1, hi - lo]], channel_multiplier=1)
                last.then_inc(setup_pool, 1)
                pool.wait_ge(setup_act, 2)

            def p1_windows(c):
                b = c.b
                link = linker(pool, sq_win_ready, 3, b)
                pool.wait_ge(xT_ready, 2 * (b + 1))
                wait(pool, wsq_done, b)
                link(g.tensor_tensor(sq_pairs[:, :], xT_sq[:, 0:L - 2], xT_sq[:, 2:L], ALU.add))
                link(g.tensor_tensor(sq_win[:, :], sq_pairs[:, 0:T], sq_pairs[:, 4:T + 4], ALU.add))
                link(g.tensor_tensor(sq_win[0:C, :], sq_win[0:C, :], xT_sq[0:C, 8:T + 8], ALU.add), wait=False)

            def p1_norm(c):
                b = c.b
                link = linker(pool, wnorm_ready, 2, b)
                pool.wait_ge(wsq_ready, b + 1)
                wait(pool, tscale_ready, 2 * b)
                link(g.tensor_tensor(wnorm[:, :], wsq[:, :], power[0:NT, 1, 0:3], ALU.pow))
                link(g.tensor_tensor(wnorm[:, :], wnorm[:, :], tiny3[:, :], ALU.add), wait=False)

            def p1_h0(c):
                b = c.b
                link = linker(pool, h0_ready, 2, b)
                pool.wait_ge(tanh_done, b + 1)
                wait(pool, h_ready, 3 * b)
                link(g.tensor_tensor(h0[:, :, :], th[:, :, :], tokb.unsqueeze(1).to_broadcast([NT, 3, D]), ALU.add))
                settled(pool, passed_pool)
                link(g.tensor_scalar(h0[:, :, :], h0[:, :, :], 0.0, None, ALU.max))

            def p1_rstd(c, i):
                b = c.b
                link = linker(pool, ln_rstd[i], 2, b)
                pool.wait_ge(ln_stats[i], 2 * (b + 1))
                wait(pool, ln_shift[i], b)
                wait(pool, (xl_ready, xh_ready, hn_ready)[i], b)
                link(g.tensor_tensor(lnv[i][:, :], bna[i][:, :, 1], eps3[:, :], ALU.add))
                link(g.tensor_tensor(lnr[i][:, :], lnv[i][:, :], power[0:NT, 0, 0:3], ALU.pow), wait=False)

            def p1_sbias(c, t):
                n = c.tile(t)
                pool.wait_ge(smax_ready, n + 1)
                wait(pool, probs_ready, n)
                g.tensor_tensor(sbias[:, :], smax[:, :], minus_scale[:, :], ALU.mult).then_inc(sbias_ready, 1)

            def p1_xb(c):
                b = c.b
                pool.wait_ge(xl_ready, b + 1)
                wait(pool, res_ready, b)
                g.tensor_tensor(xb[:, :, :], xl[:, :, :], bob.unsqueeze(1).to_broadcast([NT, 3, D]), ALU.add).then_inc(xb_ready, 1)

            def p1_h(c):
                b = c.b
                link = linker(pool, h_ready, 3, b)
                pool.wait_ge(xh_ready, b + 1)
                wait(pool, out_ready, 3 * (b - 1))
                link(g.tensor_tensor(h[c.par][:, :, :], xh[:, :, :], gam.unsqueeze(1).to_broadcast([NT, 3, D]), ALU.mult))
                link(g.tensor_tensor(h[c.par][:, :, :], h[c.par][:, :, :], bet.unsqueeze(1).to_broadcast([NT, 3, D]), ALU.add))
                link(g.tensor_tensor(h[c.par][:, :, :], h[c.par][:, :, :], h0[:, :, :], ALU.add), wait=False)

            def q_std(c, t):
                n = c.tile(t)
                link = linker(pool, std_ready, 3, n)
                pool.wait_ge(qss_ready, n + 1)
                wait(pool, std_turned, n)
                wait(pool, nmx_ready, n)
                link(g.tensor_tensor(qvar[:, :], qss[:, :], eps8[:, :], ALU.add))
                link(g.tensor_tensor(std9[:, 0:H], qvar[:, :], power[0:NT, 1, 0:H], ALU.pow), wait=False)
                link(g.tensor_tensor(qguard[:, :], qvar[:, :], guard8[:, :], ALU.mult), wait=False)

            def q_scale(c, t):
                n = c.tile(t)
                pool.wait_ge(nmx_ready, n + 1)
                wait(pool, vals_scaled, 2 * (n - 1))
                g.tensor_tensor(qscale[c.slot(t)][:, :, :].rearrange("p h s -> p (h s)"), nmx[:, :, :].rearrange("p h s -> p (h s)"),
                                power[0:NT, 0, :], ALU.pow).then_inc(qscale_ready, 1)

            def rank_sums(c, t, part):
                n = c.tile(t)
                first, end = ((0, H // 2), (H // 2, H), (0, H))[part]
                k = end - first
                src, dst = (idxf[c.slot(t)], ce) if part == 2 else (val_s, cs)
                if part == 0:
                    pool.wait_ge(ranked, 16 * n + 6)
                    wait(pool, chosen, 11 * n - 7)
                    wait(pool, exp_ready, n)
                elif part == 1:
                    pool.wait_ge(ranked, 16 * n + 14)
                else:
                    pool.wait_ge(idxf_ready, n + 1)
                src, dst = src[:, first:end, :, :], dst[:, first:end, :]
                if part < 2:
                    pool.wait_ge(qscale_ready, n + 1)
                    g.tensor_tensor(src, val[c.slot(t)][:, first:end, :, :],
                                    qscale[c.slot(t)][:, first:end, :].unsqueeze(3).to_broadcast([NT, k, 2, TOP]), ALU.mult).then_inc(vals_scaled, 1)
                    pool.wait_ge(vals_scaled, 2 * n + 1 + part)
                at = 0
                for a in range(5):
                    m = TOP // (a + 1)
                    g.tensor_tensor(dst[:, :, at:at + m], src[:, :, 0, a:a + 1].to_broadcast([NT, k, m]), src[:, :, 1, 0:m], ALU.add)
                    at += m
                g.tensor_tensor(dst[:, :, at:at + 6].rearrange("p h (a c) -> p h a c", c=2),
                                src[:, :, 0, 5:8].unsqueeze(3).to_broadcast([NT, k, 3, 2]),
                                src[:, :, 1, 0:2].unsqueeze(2).to_broadcast([NT, k, 3, 2]), ALU.add)
                at += 6
                g.tensor_tensor(dst[:, :, at:at + 8], src[:, :, 0, 8:16], src[:, :, 1, 0:1].to_broadcast([NT, k, 8]), ALU.add)\
                 .then_inc(cells_ready, 1)
                assert at + 8 == NC

            def select(c, t):
                n = c.tile(t)
                pool.wait_ge(cells_ready, 3 * (n + 1))
                pool.wait_ge(chosen, 11 * n + 9)
                wait(pool, cells_turned, n)
                g.tensor_tensor(wcell[:, 2, :, :], taken[:, :, :], ce[:, :, :], ALU.mult).then_inc(weights, 1)
                pool.wait_ge(exp_ready, n + 1)
                g.tensor_tensor(wsel[:, :, :], taken[:, :, :], cx[:, :, :], ALU.mult).then_inc(weights, 1)

            def normalise(c, t):
                n = c.tile(t)
                pool.wait_ge(weights, 4 * n + 2)
                pool.wait_ge(chosen, 11 * (n + 1))
                g.tensor_tensor(wn[:, :, :], wsel[:, :, :], wrec[:, :].unsqueeze(2).to_broadcast([NT, H, NC]), ALU.mult).then_inc(weights, 1)
                pool.wait_ge(whigh_ready, n + 1)
                pool.wait_ge(weights, 4 * n + 3)
                g.tensor_tensor(wcell[:, 1, :, :], wn[:, :, :], wcell[:, 0, :, :], ALU.subtract).then_inc(weights, 1)

            def digits(c, t):
                m = c.tile(t)
                pool.wait_ge(high_ready, 2 * (m + 1))
                pool.wait_ge(wm_ready, m + 1)
                wait(pool, wl_ready, 2 * m - 1)
                g.tensor_tensor(el[:, :, :], wm[:, :, 2, :], eh4[:, :, :], ALU.subtract).then_inc(digits_ready, 1)

            def body(c):
                do(rank_sums, c + -1, 2, 0)
                do(rank_sums, c + -1, 2, 1)
                do(q_scale, c, 0)
                do(rank_sums, c + -1, 2, 2)
                do(p1_sbias, c + 1, 0)
                do(digits, c + -1, 1)
                do(p1_sbias, c + 1, 1)
                do(select, c + -1, 2)
                do(q_std, c, 1)
                do(normalise, c + -1, 2)
                do(p1_sbias, c + 1, 2)
                do(p1_xb, c + 1)
                do(rank_sums, c, 0, 0)
                do(rank_sums, c, 0, 1)
                do(digits, c + -1, 2)
                do(rank_sums, c, 0, 2)
                do(p1_windows, c + 2)
                do(select, c, 0)
                do(normalise, c, 0)
                do(q_scale, c, 1)
                do(p1_rstd, c + 1, 1)
                do(q_std, c, 2)
                do(p1_h, c + 1)
                do(rank_sums, c, 1, 0)
                do(p1_rstd, c + 1, 2)
                do(digits, c, 0)
                do(rank_sums, c, 1, 1)
                do(p1_norm, c + 2)
                do(q_scale, c, 2)
                do(p1_h0, c + 2)
                do(q_std, c + 1, 0)
                do(p1_rstd, c + 2, 0)
                do(rank_sums, c, 1, 2)
                do(select, c, 1)
                do(normalise, c, 1)

            run(pool, start, body, lambda: None)

        @block.scalar
        def _(act):
            a = nc.scalar

            def start():
                act.wait_ge(w_in, ALL_LOADED)
                a.activation(id16[:, :], id32[:, :], ACT.Copy).then_inc(setup_act, 1)
                act.wait_ge(setup_pe, 1)
                a.activation(vecs[:, 0:4 * D], bankA[:, :], ACT.Copy)
                a.activation(vecs[:, 4 * D:], bankB[:, 0:2 * QD], ACT.Copy).then_inc(setup_act, 1)
                act.wait_ge(setup_pe, 2)
                a.activation(fwqT[:, :], bankS[:, 0:H * QD], ACT.Copy).then_inc(setup_act, 1)
                act.wait_ge(setup_pe, 3)
                a.activation(downT[:, :], bankC[:, 0:128], ACT.Copy).then_inc(setup_act, 1)
                act.wait_ge(setup_pe, 4)
                a.activation(key_bd[:, :], bankQ[:, 0:4 * PK], ACT.Copy).then_inc(setup_act, 1)
                act.wait_ge(setup_pe, 5)
                a.activation(wg_rows[:, :, :].rearrange("p k d -> p (k d)"), bankS[:, 0:PAIRS * D], ACT.Copy).then_inc(setup_act, 1)
                act.wait_ge(setup_pe, 6)
                a.activation(bias9T[:, :, :].rearrange("p k n -> p (k n)"), bankC[:, 0:PAIRS * (H + 1)], ACT.Copy).then_inc(setup_act, 1)
                act.wait_ge(setup_pe, 7)
                a.activation(wgk[:, :, :].rearrange("p k n -> p (k n)"), bankS[:, :], ACT.Copy).then_inc(setup_act, 1)
                act.wait_ge(setup_pe, 8)
                a.activation(bias9k[:, :, :].rearrange("p k n -> p (k n)"), banks3[0:H + 1, 0:4 * PAIRS * PK], ACT.Copy).then_inc(setup_act, 1)
                act.wait_ge(setup_pool, 4)

            def p1_xT(c):
                b = c.b
                act.wait_ge(x_turned, b + 1)
                wait(act, conv_done, b)
                wait(act, sq_win_ready, 3 * b)
                a.activation(xT[:, :], bankA[:, 0:L], ACT.Copy).then_inc(xT_ready, 1)
                a.activation(xT_sq[:, :], bankA[:, 0:L], ACT.Square).then_inc(xT_ready, 1)

            def p1_convT(c):
                b = c.b
                act.wait_ge(conv_done, b + 1)
                wait(act, conv_turned, b)
                a.activation(convT[:, :], bankB[:, 0:T], ACT.Copy).then_inc(convT_ready, 1)

            def p1_tanh(c):
                b = c.b
                act.wait_ge(conv_turned, b + 1)
                act.wait_ge(tscale_ready, 2 * (b + 1))
                wait(act, h0_ready, 2 * b)
                for t in range(3):
                    last = a.activation(th[:, t, :], bankA[0:NT, t * D:(t + 1) * D], ACT.Tanh, scale=tscale[:, t:t + 1])
                last.then_inc(tanh_done, 1)

            def p1_ln(c, i):
                b = c.b
                src, dst, done = ((h0, xl, xl_ready), (res, xh, xh_ready), (h[c.par], hn, hn_ready))[i]
                act.wait_ge(ln_shift[i], b + 1)
                if i == 0:
                    wait(act, ax_done, 3 * b)
                    wait(act, xb_ready, b)
                elif i == 1:
                    wait(act, h_ready, 3 * b)
                else:
                    wait(act, hn_turned, b)
                for t in range(3):
                    last = a.activation(dst[:, t, :], src[:, t, :], ACT.Identity, bias=lnm[i][:, t:t + 1], scale=lnr[i][:, t:t + 1])
                last.then_inc(done, 1)

            def p1_xlT(c):
                b = c.b
                act.wait_ge(xl_turned, b + 1)
                wait(act, qk_done, 2 * b)
                a.activation(xlT[:, :], bankA[:, 0:T], ACT.Copy).then_inc(xlT_ready, 1)

            def p1_qk(c):
                b = c.b
                wait(act, attn_scored, 3 * b)
                for i, (dst, src, bias) in enumerate(((qT, bankB, bq_sb), (kT, bankC, bk_sb))):
                    act.wait_ge(qk_done, 2 * b + 1 + i)
                    a.activation(dst[:, :], src[:, 0:T], ACT.Identity, bias=bias[:, 0:1]).then_inc(qk_ready, 1)

            def p1_probs(c, t):
                b, n = c.b, c.tile(t)
                act.wait_ge(sbias_ready, n + 1)
                wait(act, rden_ready, n)
                wait(act, attn_turned, n - 2)
                for w in range(3):
                    lo, hi = band(t, w)
                    last = a.activation(probs[t][w][:, lo:hi], masked[w][:, 0:hi - lo], ACT.Exp, bias=sbias[:, w:w + 1],
                                        scale=SCORE_SCALE, accum_out=den[:, w:w + 1])
                last.then_inc(probs_ready, 1)

            def p1_diag(c, t):
                n = c.tile(t)
                act.wait_ge(rden_ready, n + 1)
                wait(act, attn_turned, n)
                for w in range(3):
                    last = a.activation(diag[:, w, :], id32[0:NT, 0:NT], ACT.Copy, scale=rden[:, w:w + 1])
                last.then_inc(diag_ready, 1)

            def p1_attnT(c, t):
                b, n = c.b, c.tile(t)
                act.wait_ge(attn_turned, n + 1)
                wait(act, ax_done, n)
                cc = chunks(t, 2)
                lo, hi = cc[0] * NT, (cc[-1] + 1) * NT
                a.activation(attnT[:, lo:hi], bankB[0:NT, lo:hi], ACT.Copy).then_inc(attnT_ready, 1)

            def p1_axT(c, t):
                b, n = c.b, c.tile(t)
                act.wait_ge(ax_done, n + 1)
                wait(act, wo_done, n)
                a.activation(axT[:, :], bankC[:, 0:NT], ACT.Identity, scale=third[:, 0:1]).then_inc(axT_ready, 1)

            def p1_hnT(c):
                b = c.b
                act.wait_ge(hn_turned, b + 1)
                wait(act, scored, 3 * (b - 1))
                wait(act, inner_done, EL * (b - 1))
                a.activation(hnT[c.par][:, :, :].rearrange("p t n -> p (t n)"), bankC[:, 0:3 * NT], ACT.Copy).then_inc(hnT_ready, 1)

            def q_gelu(c, low):
                b = c.b
                wait(act, prod_ready, 3 * (b - 1))
                act.wait_ge(inner_done, EL * b + low + 1)
                into = act_g[c.par][:, :, :, :, :].rearrange("p a g l t -> p (a g) l t")[:, :, low, :]
                of = bankQ[:, 0:3 * NT].rearrange("p (g t) -> p g t", t=TG)
                for q in range(TG):
                    last = a.activation(into[:, :, q], of[:, :, q], ACT.Gelu, scale=own_sb[:, q:q + 1])
                last.then_inc(gelu_done, 1)

            def q_squares(c, t):
                n = c.tile(t)
                act.wait_ge(q_done, n + 1)
                wait(act, std_ready, 3 * n)
                for i in range(H):
                    last = a.activation(sq_junk[:, i, :], bankQ[0:NT, i * QD:(i + 1) * QD], ACT.Square, scale=QD ** -0.5, accum_out=qss[:, i:i + 1])
                last.then_inc(qss_ready, 1)

            def q_stdT(c, t):
                n = c.tile(t)
                act.wait_ge(std_turned, n + 1)
                wait(act, scored, n)
                a.activation(std9T[:, :], bankQ[0:H + 1, 0:NT], ACT.Copy).then_inc(stdT_ready, 1)

            def q_norms(c, t):
                n = c.tile(t)
                act.wait_ge(q2_done, n + 1)
                wait(act, nmx_ready, n)
                for i in range(2 * H):
                    last = a.activation(ns_junk[:, i, :], bankQ[0:NT, i * HALF:(i + 1) * HALF], ACT.Square, accum_out=nss[:, i // 2, i % 2:i % 2 + 1])
                last.then_inc(nss_ready, 1)

            def q_scores(c, t):
                n = c.tile(t)
                act.wait_ge(scored, n + 1)
                wait(act, ranked, 16 * (n - 1))
                a.activation(scores[c.slot(t)][:, :, :, :].rearrange("p h s e -> p (h s e)"), bankS[0:NT, :], ACT.Copy)\
                 .then_inc(scores_ready, 1)

            def index_floats(c, t):
                n = c.tile(t)
                act.wait_ge(ranked, 16 * (n + 1))
                wait(act, cells_ready, 3 * (n - 1))
                a.activation(idxf[c.slot(t)][:, :, :, :], idx[c.slot(t)][:, :, :, :], ACT.Copy, scale=1.0 / WSCALE).then_inc(idxf_ready, 1)

            def cell_exp(c, t):
                n = c.tile(t)
                act.wait_ge(cells_ready, 3 * n + 2)
                wait(act, weights, 4 * n)
                a.activation(cx[:, :, :], cs[:, :, :], ACT.Exp).then_inc(exp_ready, 1)

            def best_exps(c, t):
                n = c.tile(t)
                act.wait_ge(chosen, 11 * n + 6)
                a.activation(best_exp[:, :, :], best[:, :, :], ACT.Exp).then_inc(best_exp_ready, 1)

            def weight_high(c, t):
                n = c.tile(t)
                act.wait_ge(weights, 4 * n + 3)
                a.activation(wcell[:, 0, :, :], wn[:, :, :], ACT.Copy).then_inc(whigh_ready, 1)

            def cells_T(c, t):
                n = c.tile(t)
                act.wait_ge(cells_turned, n + 1)
                wait(act, merge_done, n)
                for k in range(2):
                    last = a.activation(wcT[:, 2 * k:2 * k + 2, :, :].rearrange("p a k n -> p (a k n)"),
                                        wcT_ps[:, k, 0:6 * NT], ACT.Copy)
                last.then_inc(wcT_ready, 1)

            def merged_weights(c, t):
                n = c.tile(t)
                act.wait_ge(merge_done, n + 1)
                wait(act, wl_ready, 2 * n)
                wait(act, onehigh_ready, 2 * n)
                wait(act, digits_ready, n)
                a.activation(eh[:, :, :], merged[:, :, 2 * NT:3 * NT], ACT.Identity, bias=digit_bias[:, 0:1], scale=1.0 / EL).then_inc(high_ready, 1)
                act.wait_ge(high_ready, 2 * n + 1)
                a.activation(eh4[:, :, :], eh[:, :, :], ACT.Copy, scale=float(EL)).then_inc(high_ready, 1)
                a.activation(wm[:, :, :, :].rearrange("p k s n -> p k (s n)"), merged[:, :, 0:3 * NT], ACT.Copy).then_inc(wm_ready, 1)

            def body(c):
                do(p1_diag, c + 1, 0)
                do(q_scores, c, 0)
                do(p1_probs, c + 1, 1)
                do(best_exps, c + -1, 2)
                do(q_squares, c, 1)
                do(p1_attnT, c + 1, 0)
                do(weight_high, c + -1, 2)
                do(p1_axT, c + 1, 0)
                do(p1_diag, c + 1, 1)
                do(q_stdT, c, 1)
                do(p1_probs, c + 1, 2)
                do(p1_xT, c + 2)
                do(cells_T, c + -1, 2)
                do(index_floats, c, 0)
                do(p1_attnT, c + 1, 1)
                do(merged_weights, c + -1, 2)
                do(q_norms, c, 1)
                do(p1_axT, c + 1, 1)
                do(p1_diag, c + 1, 2)
                do(cell_exp, c, 0)
                do(best_exps, c, 0)
                do(q_scores, c, 1)
                do(p1_attnT, c + 1, 2)
                do(weight_high, c, 0)
                do(p1_axT, c + 1, 2)
                do(q_squares, c, 2)
                do(p1_ln, c + 1, 1)
                do(cells_T, c, 0)
                do(q_stdT, c, 2)
                do(merged_weights, c, 0)
                do(q_norms, c, 2)
                do(p1_ln, c + 1, 2)
                do(cell_exp, c, 1)
                do(p1_convT, c + 2)
                do(p1_hnT, c + 1)
                do(index_floats, c, 1)
                do(p1_tanh, c + 2)
                do(q_scores, c, 2)
                do(q_squares, c + 1, 0)
                do(best_exps, c, 1)
                do(q_stdT, c + 1, 0)
                do(p1_ln, c + 2, 0)
                do(q_norms, c + 1, 0)
                do(p1_xlT, c + 2)
                do(weight_high, c, 1)
                do(q_gelu, c + 1, 0)
                do(index_floats, c, 2)
                do(p1_qk, c + 2)
                do(q_gelu, c + 1, 1)
                do(cells_T, c, 1)
                do(q_gelu, c + 1, 2)
                do(merged_weights, c, 1)
                do(q_gelu, c + 1, 3)
                do(p1_probs, c + 2, 0)
                do(cell_exp, c, 2)

            run(act, start, body, lambda: None)

        @block.tensor
        def _(pe):
            e = nc.tensor

            def start():
                pe.wait_ge(w_in, ALL_LOADED)
                pe.wait_ge(setup_pool, 2)
                e.matmul(bankA[:, :], ones[0:1, :], rows[0:1, 0:4 * D], start=True, stop=True)
                e.matmul(bankB[:, 0:2 * QD], ones[0:1, :], rows[0:1, 4 * D:4 * D + 2 * QD], start=True, stop=True)\
                 .then_inc(setup_pe, 1)
                for k in range(4):
                    last = e.transpose(bankS[:, k * 128:(k + 1) * 128], fwq_in[:, k, :], id32[:, :])
                last.then_inc(setup_pe, 1)
                e.transpose(bankC[:, 0:128], down_in[:, :], id32[:, :]).then_inc(setup_pe, 1)
                pe.wait_ge(setup_dve, 3)
                for k in range(4):
                    last = e.transpose(bankQ[:, k * PK:(k + 1) * PK], key_z[:, k, :], id32[0:PK, 0:PK])
                last.then_inc(setup_pe, 1)
                pe.wait_ge(setup_act, 5)
                pe.wait_ge(setup_dve, 13)
                for k in range(PAIRS):
                    last = e.transpose(bankS[:, k * D:(k + 1) * D], wgT[:, k * 128:(k + 1) * 128], id32[:, :])
                last.then_inc(setup_pe, 1)
                pe.wait_ge(fbq_spread, 48)
                for k in range(PAIRS):
                    last = e.transpose(bankC[:, k * (H + 1):(k + 1) * (H + 1)], bias9[:, k * 128:(k + 1) * 128], id32[0:H + 1, 0:H + 1])
                last.then_inc(setup_pe, 1)
                pe.wait_ge(setup_act, 6)
                for k in range(PAIRS):
                    last = e.matmul(bankS[:, k * 4 * PK:(k + 1) * 4 * PK], wg_rows[:, k, :], key_bd[:, :], start=True, stop=True)
                last.then_inc(setup_pe, 1)
                pe.wait_ge(setup_act, 7)
                for k in range(PAIRS):
                    last = e.matmul(banks3[0:H + 1, k * 4 * PK:(k + 1) * 4 * PK], bias9T[:, k, :], key_bd[:, :], start=True, stop=True)
                last.then_inc(setup_pe, 1)
                pe.wait_ge(setup_act, 9)
                pe.wait_ge(setup_pool, 3)

            def p1_turn_x(c):
                b = c.b
                pe.wait_ge(x_loaded[c.par], 48 * (c.j + 1))
                wait(pe, smax_ready, 3 * b)
                for t in range(3):
                    last = e.transpose(bankA[:, t * XT:(t + 1) * XT], x_in[c.par][:, t, :, :].rearrange("p s c -> p (s c)"), id32[0:XT, 0:XT])
                last.then_inc(x_turned, 1)

            def p1_conv(c):
                b = c.b
                pe.wait_ge(xT_ready, 2 * (b + 1))
                wait(pe, attnT_ready, 3 * b)
                for m in range(5):
                    k = 2 * C if m < 4 else C
                    last = e.matmul(bankB[:, 0:T], conv_w[0:k, m, :], xT[0:k, 2 * m:2 * m + T], start=m == 0, stop=m == 4)
                last.then_inc(conv_done, 1)

            def p1_sum_sq(c):
                b = c.b
                pe.wait_ge(sq_win_ready, 3 * (b + 1))
                for t in range(3):
                    last = e.matmul(bankA[0:NT, 3 * D + t:3 * D + t + 1], sq_win[:, OFF[t]:OFF[t] + NT], ones[:, 0:1], start=True, stop=True)
                last.then_inc(wsq_done, 1)

            def p1_turn_conv(c):
                b = c.b
                pe.wait_ge(wsq_ready, b + 1)
                pe.wait_ge(convT_ready, b + 1)
                for t in range(3):
                    last = e.transpose(bankA[0:NT, t * D:(t + 1) * D], convT[:, OFF[t]:OFF[t] + NT], id32[:, :])
                last.then_inc(conv_turned, 1)

            def p1_turn_xl(c):
                b = c.b
                pe.wait_ge(xl_ready, b + 1)
                for t in range(3):
                    last = e.transpose(bankA[:, OFF[t]:OFF[t] + NT], xl[:, t, :], id32[0:NT, 0:NT])
                last.then_inc(xl_turned, 1)

            def p1_project(c):
                b = c.b
                pe.wait_ge(xlT_ready, b + 1)
                e.matmul(bankB[:, 0:T], wq_sb[:, :], xlT[:, :], start=True, stop=True).then_inc(qk_done, 1)
                wait(pe, hnT_ready, b)
                e.matmul(bankC[:, 0:T], wk_sb[:, :], xlT[:, :], start=True, stop=True).then_inc(qk_done, 1)

            def p1_scores(c, t):
                b, n = c.b, c.tile(t)
                pe.wait_ge(qk_ready, 2 * (b + 1))
                if t:
                    pe.wait_ge(smax_ready, n)
                lo, hi = band(t, 2)
                e.matmul(bankA[0:NT, 0:hi - lo], qT[:, OFF[t]:OFF[t] + NT], kT[:, lo:hi], start=True, stop=True)\
                 .then_inc(attn_scored, 1)

            def p1_turn_attn(c, t):
                b, n = c.b, c.tile(t)
                pe.wait_ge(diag_ready, n + 1)
                wait(pe, attnT_ready, n)
                for k in chunks(t, 2):
                    windows = [w for w in range(3) if k in chunks(t, w)]
                    for w in windows:
                        last = e.matmul(bankB[0:NT, k * NT:(k + 1) * NT], probs[t][w][:, OFF[k]:OFF[k] + NT], diag[:, w, :],
                                        start=w == windows[0], stop=w == windows[-1])
                last.then_inc(attn_turned, 1)

            def p1_ax(c, t):
                b, n = c.b, c.tile(t)
                pe.wait_ge(attnT_ready, n + 1)
                wait(pe, axT_ready, n)
                if t == 0:
                    wait(pe, qk_ready, 2 * (b + 1))
                cc = chunks(t, 2)
                for c in cc:
                    last = e.matmul(bankC[:, 0:NT], xl[0:KEYS[c], c, :], attnT[0:KEYS[c], c * NT:(c + 1) * NT],
                                    start=c == cc[0], stop=c == cc[-1])
                last.then_inc(ax_done, 1)

            def p1_wo(c, t):
                b, n = c.b, c.tile(t)
                pe.wait_ge(axT_ready, n + 1)
                e.matmul(bankC[0:NT, (1 + t) * D:(2 + t) * D], axT[:, :], wo_sb[:, :], start=True, stop=True).then_inc(wo_done, 1)

            def p1_turn_hn(c):
                b = c.b
                pe.wait_ge(hn_ready, b + 1)
                for t in range(3):
                    last = e.transpose(bankC[:, t * NT:(t + 1) * NT], hn[:, t, :], id32[0:NT, 0:NT])
                last.then_inc(hn_turned, 1)

            def q_inner(c, low):
                b = c.b
                if low == 0:
                    pe.wait_ge(nss_ready, 3 * b + 1)
                wait(pe, gelu_done, EL * b + low)
                e.matmul(bankQ[:, 0:3 * NT], down_x[:, low, :, :].rearrange("p h t -> p (h t)"),
                         hnT[c.par][:, :, :].rearrange("p t n -> p (t n)"), start=True, stop=True).then_inc(inner_done, 1)

            def q_product(c, t):
                b, n = c.b, c.tile(t)
                pe.wait_ge(hnT_ready, b + 1)
                wait(pe, nss_ready, n)
                if t == 1:
                    pe.wait_ge(gelu_done, EL * (b + 1))
                e.matmul(bankQ[0:NT, :], hnT[c.par][:, t, :], fwqT[:, :], start=True, stop=False)
                e.matmul(bankQ[0:NT, :], ones3[:, :], fbq3[:, :], start=False, stop=True).then_inc(q_done, 1)

            def q_turn_std(c, t):
                n = c.tile(t)
                pe.wait_ge(std_ready, 3 * n + 2)
                e.transpose(bankQ[0:H + 1, 0:NT], std9[:, :], id32[0:NT, 0:NT]).then_inc(std_turned, 1)

            def q_second(c, t):
                n = c.tile(t)
                pe.wait_ge(stdT_ready, n + 1)
                e.matmul(bankQ[0:NT, :], hnT[c.par][:, t, :], wgT[:, :], start=True, stop=False)
                e.matmul(bankQ[0:NT, :], std9T[:, :], bias9[:, :], start=False, stop=True).then_inc(q2_done, 1)

            def q_score(c, t):
                n = c.tile(t)
                pe.wait_ge(stdT_ready, n + 1)
                wait(pe, scores_ready, n)
                wait(pe, wcT_ready, n - 1)
                for k in range(2):
                    part = bankS[0:NT, k * 512:(k + 1) * 512]
                    e.matmul(part, hnT[c.par][:, t, :], wgk[:, 2 * k:2 * k + 2, :].rearrange("p k n -> p (k n)"), start=True, stop=False)
                    last = e.matmul(part, std9T[:, :], bias9k[:, 2 * k:2 * k + 2, :].rearrange("p k n -> p (k n)"), start=False, stop=True)
                last.then_inc(scored, 1)

            def turn_cells(c, t):
                n = c.tile(t)
                pe.wait_ge(weights, 4 * (n + 1))
                pe.wait_ge(scores_ready, at_most(n + 2, 3 * B))
                wait(pe, wcT_ready, n)
                for i in range(3 * PAIRS):
                    k, part = i // 3, i % 3
                    last = e.transpose(wcT_ps[:, i // 6, (i % 6) * NT:(i % 6 + 1) * NT],
                                       wcell[:, part, 2 * k:2 * k + 2, :].rearrange("p h c -> p (h c)"), id16[0:NT, 0:NT])
                last.then_inc(cells_turned, 1)

            def merge_cells(c, t):
                n = c.tile(t)
                pe.wait_ge(wcT_ready, n + 1)
                wait(pe, out_ready, n)
                wait(pe, prod_ready, n)
                for k in range(PAIRS):
                    q = 2 * SLOTS * (k % 2)
                    last = e.matmul(merged[q:q + 2 * SLOTS, k // 2, 0:3 * NT], merge_sb[:, :],
                                    wcT[:, k, :, :].rearrange("p k n -> p (k n)"), start=True, stop=True)
                last.then_inc(merge_done, 1)

            def scatter(c, t):
                m = c.tile(t)
                pe.wait_ge(wl_ready, 2 * (m + 1))
                pe.wait_ge(wm_ready, m + 1)
                pe.wait_ge(high_ready, 2 * m + 1)
                pe.wait_ge(onehigh_ready, 2 * (m + 1))
                for g in range(NG):
                    for k in range(2):
                        for part in range(2):
                            last = e.matmul(coef[:, g, :, :], oh[:, k, g, :, :].rearrange("p v t -> p (v t)"),
                                            wl[:, part, k, :, TG * g:TG * (g + 1)], start=k + part == 0, stop=k + part == 2)
                last.then_inc(scattered, 1)

            def experts_out(c, t):
                m = c.tile(t)
                pe.wait_ge(prod_ready, m + 1)
                for l in range(EL):
                    last = e.matmul(ffn, prod[:, l, :], up_x[:, l, :], start=l == 0, stop=l == EL - 1)
                last.then_inc(ffn_done, 1)

            def body(c):
                do(p1_ax, c, 0)
                do(q_turn_std, c + -1, 1)
                do(p1_turn_x, c + 1)
                do(experts_out, c + -2, 1)
                do(p1_wo, c, 0)
                do(turn_cells, c + -2, 2)
                do(p1_turn_attn, c, 1)
                do(merge_cells, c + -2, 2)
                do(q_second, c + -1, 1)
                do(p1_ax, c, 1)
                do(q_score, c + -1, 1)
                do(p1_wo, c, 1)
                do(p1_turn_attn, c, 2)
                do(scatter, c + -2, 2)
                do(p1_ax, c, 2)
                do(q_product, c + -1, 2)
                do(p1_wo, c, 2)
                do(experts_out, c + -2, 2)
                do(turn_cells, c + -1, 0)
                do(p1_conv, c + 1)
                do(q_turn_std, c + -1, 2)
                do(p1_sum_sq, c + 1)
                do(merge_cells, c + -1, 0)
                do(q_second, c + -1, 2)
                do(q_score, c + -1, 2)
                do(p1_turn_hn, c)
                do(p1_turn_conv, c + 1)
                do(q_product, c, 0)
                do(scatter, c + -1, 0)
                do(q_turn_std, c, 0)
                do(q_second, c, 0)
                do(p1_turn_xl, c + 1)
                do(experts_out, c + -1, 0)
                do(q_inner, c, 0)
                do(p1_project, c + 1)
                do(turn_cells, c + -1, 1)
                do(q_inner, c, 1)
                do(p1_scores, c + 1, 0)
                do(q_inner, c, 2)
                do(p1_scores, c + 1, 1)
                do(merge_cells, c + -1, 1)
                do(q_inner, c, 3)
                do(q_score, c, 0)
                do(q_product, c, 1)
                do(p1_turn_attn, c + 1, 0)
                do(p1_scores, c + 1, 2)
                do(scatter, c + -1, 1)

            run(pe, start, body, lambda: None)

        @block.vector
        def _(dve):
            v = nc.vector

            def start():
                link = linker(dve, setup_dve, 13, 0)
                dve.wait_ge(w_in, ALL_LOADED)
                link(v.tensor_tensor(key_sq[:, :, :], key_in[:, :, :], key_in[:, :, :], ALU.mult))
                link(v.tensor_reduce(out=key_n[:, :], in_=key_sq[:, :, :], axis=X, op=ALU.add))
                dve.wait_ge(setup_key, 2)
                for hd in range(2):
                    for s in range(2):
                        k = 2 * hd + s
                        last = v.tensor_scalar(key_z[:, k, HALF * k:HALF * (k + 1)], key_in[:, s, :], key_n[:, s:s + 1], None, ALU.mult)
                link(last)
                dve.wait_ge(setup_act, 3)
                for wt, mean in ((fwqT[:, :], fmean[:, :]), (fbq_row, bmean[:, :])):
                    w3 = wt.rearrange("p (h q) -> p h q", h=H)
                    link(v.tensor_reduce(out=mean, in_=w3, axis=X, op=ALU.add))
                    link(v.tensor_scalar(mean, mean, 1.0 / QD, None, ALU.mult))
                    link(v.tensor_tensor(w3, w3, mean.unsqueeze(2).to_broadcast([w3.shape[0], H, QD]), ALU.subtract))
                dve.wait_ge(setup_act, 4)
                for q in range(TG):
                    last = v.tensor_copy(down_x[:, :, :, q], downT[:, :].rearrange("p (h l) -> p l h", l=EL))
                link(last)
                gain, bias = (vecs[:, 4 * D + i * QD:4 * D + (i + 1) * QD] for i in range(2))
                link(v.tensor_tensor(wgT[:, :].rearrange("p (h q) -> p h q", h=H), fwqT[:, :].rearrange("p (h q) -> p h q", h=H),
                                     gain.unsqueeze(1).to_broadcast([D, H, QD]), ALU.mult))
                link(v.tensor_tensor(bias9[0:H, :].rearrange("p (h q) -> p h q", h=H), id32[0:H, 0:H].unsqueeze(2).to_broadcast([H, H, QD]),
                                     bias[0:H, :].unsqueeze(1).to_broadcast([H, H, QD]), ALU.mult))
                link(v.tensor_tensor(bias_row[:, :].rearrange("p (h q) -> p h q", h=H), fbq_row.rearrange("p (h q) -> p h q", h=H),
                                     gain[0:1, :].unsqueeze(1).to_broadcast([1, H, QD]), ALU.mult))
                part = linker(dve, setup_fbq, 5, 0)
                part(v.tensor_copy(fbq3[0:1, :], fbq_row))
                part(v.tensor_tensor(fbq_rest[:, 0, :], fbq_row, fbq3[0:1, :], ALU.subtract))
                part(v.tensor_copy(fbq_part[:, 0, :], fbq_rest[:, 0, :]))
                part(v.tensor_tensor(fbq_rest[:, 1, :], fbq_rest[:, 0, :], fbq_part[:, 0, :], ALU.subtract))
                part(v.tensor_copy(fbq_part[:, 1, :], fbq_rest[:, 1, :]))
                dve.wait_ge(setup_pool, 6)

            def p1_wsq(c):
                b = c.b
                dve.wait_ge(wsq_done, b + 1)
                wait(dve, wnorm_ready, 2 * b)
                v.tensor_scalar(wsq[:, :], bankA[0:NT, 3 * D:3 * D + 3], 0.0, None, ALU.max).then_inc(wsq_ready, 1)

            def p1_tscale(c):
                b = c.b
                link = linker(dve, tscale_ready, 2, b)
                dve.wait_ge(wnorm_ready, 2 * (b + 1))
                wait(dve, tanh_done, b)
                link(v.reciprocal(wden[:, :], wnorm[:, :]))
                link(v.tensor_scalar(tscale[:, :], wden[:, :], 1.0, 1.0 / (1.0 + 1.0e-7), ALU.min, ALU.mult), wait=False)

            def p1_stats(c, i):
                b = c.b
                src = (h0, res, h[c.par])[i]
                if i == 0:
                    dve.wait_ge(h0_ready, 2 * (b + 1))
                elif i == 1:
                    dve.wait_ge(res_ready, b + 1)
                else:
                    dve.wait_ge(h_ready, 3 * (b + 1))
                for t in range(3):
                    last = v.bn_stats(out=bns[i][:, t, :], in_=src[:, t, :])
                last.then_inc(ln_stats[i], 1)

            def p1_moments(c, i):
                b = c.b
                dve.wait_ge(ln_stats[i], 2 * b + 1)
                wait(dve, ln_rstd[i], 2 * b)
                settled(dve, passed_dve)
                for t in range(3):
                    last = v.bn_aggr(out=bna[i][:, t, :], in_=bns[i][:, t, :])
                last.then_inc(ln_stats[i], 1)

            def p1_shift(c, i):
                b = c.b
                dve.wait_ge(ln_rstd[i], 2 * (b + 1))
                wait(dve, (xl_ready, xh_ready, hn_ready)[i], b)
                v.scalar_tensor_tensor(out=lnm[i][:, :], in0=bna[i][:, :, 0], scalar=-1.0, in1=lnr[i][:, :],
                                       op0=ALU.mult, op1=ALU.mult).then_inc(ln_shift[i], 1)

            def p1_smax(c, t):
                b, n = c.b, c.tile(t)
                dve.wait_ge(attn_scored, n + 1)
                wait(dve, probs_ready, n)
                wait(dve, sbias_ready, n)
                lo2 = band(t, 2)[0]
                settled(dve, passed_dve)
                for w in range(3):
                    lo, hi = band(t, w)
                    last = v.tensor_tensor_reduce(out=masked[w][:, 0:hi - lo], in0=bankA[0:NT, lo - lo2:hi - lo2], in1=masks[t, w][:, :],
                                                  scale=1.0, scalar=-3.0e38, op0=ALU.add, op1=ALU.max, accum_out=smax[:, w:w + 1])
                last.then_inc(smax_ready, 1)

            def p1_rden(c, t):
                n = c.tile(t)
                dve.wait_ge(probs_ready, n + 1)
                wait(dve, diag_ready, n)
                v.reciprocal(rden[:, :], den[:, :]).then_inc(rden_ready, 1)

            def p1_res(c):
                b = c.b
                dve.wait_ge(wo_done, 3 * (b + 1))
                dve.wait_ge(xb_ready, b + 1)
                wait(dve, xh_ready, b)
                v.tensor_tensor(res[:, :, :].rearrange("p t d -> p (t d)"), bankC[0:NT, D:4 * D],
                                xb[:, :, :].rearrange("p t d -> p (t d)"), ALU.add).then_inc(res_ready, 1)

            def q_guard(c, t):
                n = c.tile(t)
                dve.wait_ge(nss_ready, n + 1)
                dve.wait_ge(std_ready, 3 * (n + 1))
                wait(dve, qscale_ready, n)
                v.tensor_tensor(nmx[:, :, :], nss[:, :, :], qguard[:, :].unsqueeze(2).to_broadcast([NT, H, 2]), ALU.max).then_inc(nmx_ready, 1)

            def rank(c, t, half, step):
                n = c.tile(t)
                src, v_, i_ = scores[c.slot(t)], val[c.slot(t)], idx[c.slot(t)]
                base = 16 * n + 8 * half + 2 * step
                if half == 0 and step == 0:
                    dve.wait_ge(scores_ready, n + 1)
                    wait(dve, cells_ready, 3 * (n - 1))
                    wait(dve, idxf_ready, n - 1)
                for q in range(2):
                    heads = [(4 * half + 2 * q + i, s) for i in range(2) for s in range(2)]
                    if step > 0:
                        dve.wait_ge(ranked, base - 1 + q)
                    settled(dve, passed_dve)
                    best8 = slice(0, 8) if step < 2 else slice(8, 16)
                    for hd, s in heads:
                        if step % 2 == 0:
                            last = v.max(out=v_[:, hd, s, best8], in_=src[:, hd, s, :])
                        else:
                            last = v.max_index(out=i_[:, hd, s, best8], in_max=v_[:, hd, s, best8], in_values=src[:, hd, s, :])
                    if step == 1:
                        for hd, s in heads:
                            last = v.match_replace(out=src[:, hd, s, :], in_to_replace=v_[:, hd, s, best8], in_values=src[:, hd, s, :], imm_value=NEG)
                    last.then_inc(ranked, 1)

            def one_high(c, t, half):
                m = c.tile(t)
                dve.wait_ge(high_ready, 2 * m + 1)
                wait(dve, scattered, m)
                for hi in range(half * EH // 2, (half + 1) * EH // 2):
                    last = v.tensor_scalar(oh[:, :, :, hi, :], eh[:, :, :].rearrange("p k (g t) -> p k g t", t=TG), float(hi), None, ALU.is_equal)
                last.then_inc(onehigh_ready, 1)

            def one_low(c, t):
                m = c.tile(t)
                dve.wait_ge(digits_ready, m + 1)
                for l in range(EL):
                    last = v.tensor_scalar(ol[:, :, l, :], el[:, :, :], float(l), None, ALU.is_equal)
                last.then_inc(wl_ready, 1)

            def low_weights(c, t):
                m = c.tile(t)
                dve.wait_ge(wl_ready, 2 * m + 1)
                dve.wait_ge(wm_ready, m + 1)
                wait(dve, scattered, m)
                for k in range(2):
                    last = v.tensor_tensor(wl[:, :, k, :, :], wm[:, k, 0:2, :].unsqueeze(2).to_broadcast([128, 2, EL, NT]),
                                           ol[:, k, :, :].unsqueeze(1).to_broadcast([128, 2, EL, NT]), ALU.mult)
                last.then_inc(wl_ready, 1)

            def product(c, t):
                b, m = c.b, c.tile(t)
                dve.wait_ge(scattered, m + 1)
                dve.wait_ge(gelu_done, EL * (b + 1))
                wait(dve, ffn_done, m)
                v.tensor_tensor(prod[:, :, :].rearrange("p l (g t) -> p g l t", t=TG), coef, act_g[c.par][:, t, :, :, :], ALU.mult)\
                 .then_inc(prod_ready, 1)

            def finish(c, t):
                b, m = c.b, c.tile(t)
                dve.wait_ge(ffn_done, m + 1)
                wait(dve, stored[t], 16 * b)
                v.scalar_tensor_tensor(out=o_sb[:, t, :], in0=ffn, scalar=1.0 / WSCALE, in1=h[c.par][:, t, :], op0=ALU.mult, op1=ALU.add)\
                 .then_inc(out_ready, 1)

            def choose(c, t, step):
                n = c.tile(t)
                base = 11 * n + 2 * step
                for q in range(2):
                    if step == 0:
                        dve.wait_ge(cells_ready, 3 * n + 1 + q)
                    else:
                        dve.wait_ge(chosen, base - 1 + q)
                    settled(dve, passed_dve)
                    best8, left = (slice(0, 8), cs) if step < 2 else (slice(8, 16), cr)
                    for hd in range(4 * q, 4 * q + 4):
                        if step % 2 == 0:
                            last = v.max(out=best[:, hd, best8], in_=left[:, hd, :])
                        else:
                            last = v.match_replace(out=cr[:, hd, :], in_to_replace=best[:, hd, best8], in_values=left[:, hd, :], imm_value=NEG)
                    last.then_inc(chosen, 1)

            def mark(c, t):
                n = c.tile(t)
                wait(dve, weights, 4 * n)
                dve.wait_ge(chosen, 11 * n + 8)
                v.tensor_scalar(taken[:, :, :], cr[:, :, :], NEG / 2, WSCALE, ALU.is_lt, ALU.mult).then_inc(chosen, 1)

            def sum_exps(c, t):
                n = c.tile(t)
                dve.wait_ge(best_exp_ready, n + 1)
                v.tensor_reduce(out=wsum[:, :], in_=best_exp[:, :, :], axis=X, op=ALU.add).then_inc(chosen, 1)

            def invert_sums(c, t):
                n = c.tile(t)
                wait(dve, weights, 4 * n)
                dve.wait_ge(chosen, 11 * n + 10)
                v.reciprocal(wrec[:, :], wsum[:, :]).then_inc(chosen, 1)

            def body(c):
                do(choose, c + -1, 0, 3)
                do(low_weights, c + -2, 2)
                do(mark, c + -1, 0)
                do(sum_exps, c + -1, 0)
                do(q_guard, c + -1, 1)
                do(invert_sums, c + -1, 0)
                do(rank, c + -1, 1, 0, 0)
                do(rank, c + -1, 1, 0, 1)
                do(product, c + -2, 2)
                do(rank, c + -1, 1, 0, 2)
                do(p1_res, c)
                do(p1_stats, c, 1)
                do(p1_moments, c, 1)
                do(rank, c + -1, 1, 0, 3)
                do(p1_shift, c, 1)
                do(rank, c + -1, 1, 1, 0)
                do(finish, c + -2, 2)
                do(rank, c + -1, 1, 1, 1)
                do(rank, c + -1, 1, 1, 2)
                do(rank, c + -1, 1, 1, 3)
                do(p1_stats, c, 2)
                do(p1_wsq, c + 1)
                do(p1_moments, c, 2)
                do(one_high, c + -1, 0, 0)
                do(p1_shift, c, 2)
                do(one_high, c + -1, 0, 1)
                do(one_low, c + -1, 0)
                do(q_guard, c + -1, 2)
                do(choose, c + -1, 1, 0)
                do(p1_tscale, c + 1)
                do(low_weights, c + -1, 0)
                do(choose, c + -1, 1, 1)
                do(choose, c + -1, 1, 2)
                do(choose, c + -1, 1, 3)
                do(p1_stats, c + 1, 0)
                do(rank, c + -1, 2, 0, 0)
                do(p1_moments, c + 1, 0)
                do(mark, c + -1, 1)
                do(sum_exps, c + -1, 1)
                do(product, c + -1, 0)
                do(invert_sums, c + -1, 1)
                do(p1_shift, c + 1, 0)
                do(rank, c + -1, 2, 0, 1)
                do(rank, c + -1, 2, 0, 2)
                do(rank, c + -1, 2, 0, 3)
                do(rank, c + -1, 2, 1, 0)
                do(rank, c + -1, 2, 1, 1)
                do(rank, c + -1, 2, 1, 2)
                do(rank, c + -1, 2, 1, 3)
                do(finish, c + -1, 0)
                do(q_guard, c, 0)
                do(choose, c + -1, 2, 0)
                do(choose, c + -1, 2, 1)
                do(p1_smax, c + 1, 0)
                do(choose, c + -1, 2, 2)
                do(choose, c + -1, 2, 3)
                do(one_high, c + -1, 1, 0)
                do(one_high, c + -1, 1, 1)
                do(p1_rden, c + 1, 0)
                do(one_low, c + -1, 1)
                do(mark, c + -1, 2)
                do(p1_smax, c + 1, 1)
                do(low_weights, c + -1, 1)
                do(rank, c, 0, 0, 0)
                do(rank, c, 0, 0, 1)
                do(sum_exps, c + -1, 2)
                do(rank, c, 0, 0, 2)
                do(invert_sums, c + -1, 2)
                do(p1_rden, c + 1, 1)
                do(p1_smax, c + 1, 2)
                do(rank, c, 0, 0, 3)
                do(product, c + -1, 1)
                do(rank, c, 0, 1, 0)
                do(rank, c, 0, 1, 1)
                do(rank, c, 0, 1, 2)
                do(finish, c + -1, 1)
                do(rank, c, 0, 1, 3)
                do(p1_rden, c + 1, 2)
                do(choose, c, 0, 0)
                do(choose, c, 0, 1)
                do(choose, c, 0, 2)
                do(one_high, c + -1, 2, 0)
                do(one_high, c + -1, 2, 1)
                do(one_low, c + -1, 2)

            run(dve, start, body, lambda: None)


_INS = ["x", "L0_tok_kernel", "L0_tok_bias", "L0_attn_Wq", "L0_attn_bq", "L0_attn_Wk", "L0_attn_bk", "L0_attn_Wo", "L0_attn_bo",
        "L0_attn_gamma", "L0_attn_beta", "L0_ffn_Wq", "L0_ffn_bq", "L0_ffn_ln_g", "L0_ffn_ln_b", "L0_ffn_keys0", "L0_ffn_keys1",
        "L0_ffn_expert_down", "L0_ffn_expert_up"]


def kernel(**inputs):
    import concourse.bacc as bacc
    from concourse.bass_utils import run_bass_kernel_spmd
    nc = bacc.Bacc("TRN2", target_bir_lowering=False, num_devices=1)
    arrays, args = {}, []
    given = [(name, np.ascontiguousarray(inputs[name])) for name in _INS]
    given += [("merge", merge_matrix()), ("identity", np.eye(128, dtype=np.float32)),
              ("own", np.tile(np.eye(TG, dtype=np.float32), (EH, 1)))]
    for name, a in given:
        arrays[f"in_{name}"] = a
        args.append(nc.dram_tensor(f"in_{name}", a.shape, mybir.dt.from_np(a.dtype), kind="ExternalInput").ap())
    out = nc.dram_tensor("out_0", (B, T, D), mybir.dt.float32, kind="ExternalOutput").ap()
    build(nc, *args, out)
    r = run_bass_kernel_spmd(nc, [arrays], core_ids=[0])
    return r.results[0]["out_0"]
```
